# Optimizing a Trainium2 kernel written in Bass

```python
import numpy as np
import jax
import jax.numpy as jnp

def _softmax(x, axis=-1):
    return jax.nn.softmax(x, axis=axis)

def _gelu(x):
    return jax.nn.gelu(x, approximate=True)

def _silu(x):
    return jax.nn.silu(x)

def _sigmoid(x):
    return jax.nn.sigmoid(x)

def _layernorm(x, axis=-1, eps=1e-05):
    m = jnp.mean(x, axis=axis, keepdims=True)
    v = jnp.var(x, axis=axis, keepdims=True)
    return (x - m) / jnp.sqrt(v + eps)

def _scatter_add(tgt, idx, src, axis=0):
    return tgt.at[idx].add(src)

def _segment_sum(src, seg, n):
    return jax.ops.segment_sum(src, seg, n)
kernel_name = 'mk_xattn_ffn_d1_seqx_r2_b27d78'

def setup_inputs(seed: int=0):
    np.random.seed(seed)
    _w = jnp.asarray

    def _rec_inputs():
        import jax
        import jax.numpy as jnp
        _rk = jax.random.key(seed)
        x = -0.0003929 + 0.9999 * jax.random.normal(jax.random.fold_in(_rk, 1), (8, 512, 1024), jnp.float32)
        _lenS = 512 - jax.random.randint(jax.random.fold_in(_rk, 7), (8,), 0, max(1, 512 // 4) + 1, jnp.int32)
        _lenS2 = 512 - jax.random.randint(jax.random.fold_in(_rk, 8), (8,), 0, max(1, 512 // 4) + 1, jnp.int32)
        _ctx_2048P = jax.random.normal(jax.random.fold_in(_rk, 11), (8, 16, 1024), jnp.float32)
        _ctx_2048c = jax.random.dirichlet(jax.random.fold_in(_rk, 511), 0.3 * jnp.ones((16,), jnp.float32), (8, 512))
        _ctx_2048t = jnp.einsum('bsk,bkd->bsd', _ctx_2048c, _ctx_2048P)
        _ctx_2048t = _ctx_2048t * jax.lax.rsqrt(jnp.mean(jnp.square(_ctx_2048t)) + 1e-12) * 0.953939
        ctx_2048 = -1.39393e-06 + 0.999914 * (_ctx_2048t + 0.3 * jax.random.normal(jax.random.fold_in(_rk, 611), (8, 512, 1024), jnp.float32))
        itok_BxS_0_1023 = jax.random.randint(jax.random.fold_in(_rk, 12), (8, 512), 0, 512, jnp.int32)
        return (x, ctx_2048, itok_BxS_0_1023)
    x, ctx_2048, itok_BxS_0_1023 = _rec_inputs()

    def _L0_xattn_setup():
        import jax, jax.numpy as jnp
        import numpy as np
        B, Lq, Lk = (2, 2048, 512)
        Q_DIM, KV_DIM = (1024, 1024)
        H, HD = (16, 128)
        KVC, QC, R = (256, 384, 64)
        LOOKBACK = 8
        NEG = -1e+30

        def _rope(x, L):
            half = x.shape[-1] // 2
            inv_freq = 1.0 / 10000.0 ** (jnp.arange(half, dtype=jnp.float32) / half)
            ang = jnp.arange(L, dtype=jnp.float32)[:, None] * inv_freq
            cos, sin = (jnp.cos(ang), jnp.sin(ang))
            x1, x2 = (x[..., :half], x[..., half:])
            return jnp.concatenate([x1 * cos - x2 * sin, x1 * sin + x2 * cos], axis=-1)
        key = jax.random.key(seed)
        ks = jax.random.split(key, 11)

        def w(k, shape, fan_in):
            return jax.random.normal(k, shape, jnp.float32) / np.sqrt(fan_in).astype(np.float32)
        return {'q': jax.random.normal(ks[0], (B, Lq, Q_DIM), jnp.float32), 'kv': jax.random.normal(ks[1], (B, Lk, KV_DIM), jnp.float32), 'seg_id': jnp.sort(jax.random.randint(ks[2], (B, Lq), 0, Lk), axis=-1), 'W_kvc': w(ks[3], (KV_DIM, KVC), KV_DIM), 'W_dq': w(ks[4], (Q_DIM, QC), Q_DIM), 'W_uq': w(ks[5], (QC, H * HD), QC), 'W_qr': w(ks[6], (QC, H * R), QC), 'W_uk': w(ks[7], (KVC, H * HD), KVC), 'W_kr': w(ks[8], (KVC, R), KVC), 'W_uv': w(ks[9], (KVC, H * HD), KVC), 'W_o': w(ks[10], (H * HD, Q_DIM), H * HD)}
    _L0_xattn_all = _L0_xattn_setup()
    _L0_xattn_in = {k: v for k, v in _L0_xattn_all.items() if k in ('W_kvc', 'W_dq', 'W_uq', 'W_qr', 'W_uk', 'W_kr', 'W_uv', 'W_o')}
    del _L0_xattn_all

    def _L0_ffn_setup():
        import jax, jax.numpy as jnp
        import numpy as np
        D_MODEL = 1024
        NUM_TILES = 64
        D_SLICE = D_MODEL // NUM_TILES
        TILES_PER_CLUSTER = 8
        NUM_CLUSTERS = NUM_TILES // TILES_PER_CLUSTER
        GRID = 16
        LN_EPS = 1e-05
        DIMS = (np.arange(NUM_TILES)[:, None] * D_SLICE + np.arange(D_SLICE)[None, :]) % D_MODEL
        DIMS = jnp.asarray(DIMS, dtype=jnp.int32)

        def _forward(x, ln_gamma, ln_beta, spline_bases, spline_slopes, output_scale):
            B, S, D = x.shape
            N = B * S
            mu = jnp.mean(x, axis=-1, keepdims=True)
            var = jnp.mean(jnp.square(x - mu), axis=-1, keepdims=True)
            xn = (x - mu) * jax.lax.rsqrt(var + LN_EPS) * ln_gamma + ln_beta
            xf = xn.reshape(N, D)
            slope_sign = jnp.sign(jnp.mean(spline_slopes, axis=-1))
            tile_sigs = jnp.zeros((NUM_TILES, D), dtype=x.dtype)
            tile_sigs = tile_sigs.at[jnp.arange(NUM_TILES)[:, None], DIMS].set(slope_sign)
            cluster_sigs = jnp.sign(tile_sigs.reshape(NUM_CLUSTERS, TILES_PER_CLUSTER, D).mean(axis=1))
            cluster_assign = jnp.arange(NUM_TILES, dtype=jnp.int32) // TILES_PER_CLUSTER
            input_sigs = jnp.sign(xf)
            cluster_scores = input_sigs @ cluster_sigs.T
            best_cluster = jnp.argmax(cluster_scores, axis=-1)
            tile_scores = input_sigs @ tile_sigs.T
            in_cluster = cluster_assign[None, :] == best_cluster[:, None]
            tile_idx = jnp.argmax(jnp.where(in_cluster, tile_scores, -jnp.inf), axis=-1)
            tok_dims = DIMS[tile_idx]
            x_slice = jnp.take_along_axis(xf, tok_dims, axis=1)
            tok_min = x_slice.min(axis=1)
            tok_max = x_slice.max(axis=1)
            onehot = tile_idx[None, :] == jnp.arange(NUM_TILES)[:, None]
            tile_min = jnp.where(onehot, tok_min[None, :], jnp.inf).min(axis=1)
            tile_max = jnp.where(onehot, tok_max[None, :], -jnp.inf).max(axis=1)
            mn = tile_min[tile_idx][:, None]
            mx = tile_max[tile_idx][:, None]
            u = jnp.clip((x_slice - mn) / (mx - mn + 1e-08), 0.0, 1.0 - 1e-06)
            gi = jnp.clip((u * GRID).astype(jnp.int32), 0, GRID - 1)
            j = jnp.arange(D_SLICE)[None, :]
            b = spline_bases[tile_idx[:, None], j, gi]
            s = spline_slopes[tile_idx[:, None], j, gi]
            x_local = (u - gi.astype(u.dtype) / GRID) * GRID
            delta = (b + s * x_local) * output_scale[tile_idx][:, None]
            out = jnp.zeros_like(xf).at[jnp.arange(N)[:, None], tok_dims].set(delta)
            return x + out.reshape(B, S, D)
        key = jax.random.key(seed)
        k1, k2, k3, k4, k5, k6 = jax.random.split(key, 6)
        x = jax.random.normal(k1, (4, 2048, D_MODEL), dtype=jnp.float32)
        ln_gamma = 1.0 + 0.1 * jax.random.normal(k2, (D_MODEL,), dtype=jnp.float32)
        ln_beta = 0.1 * jax.random.normal(k3, (D_MODEL,), dtype=jnp.float32)
        spline_bases = 0.1 * jax.random.normal(k4, (NUM_TILES, D_SLICE, GRID), dtype=jnp.float32)
        spline_slopes = 0.1 + 0.1 * jax.random.normal(k5, (NUM_TILES, D_SLICE, GRID), dtype=jnp.float32)
        output_scale = 1.0 + 0.1 * jax.random.normal(k6, (NUM_TILES,), dtype=jnp.float32)
        return {'x': x, 'ln_gamma': ln_gamma, 'ln_beta': ln_beta, 'spline_bases': spline_bases, 'spline_slopes': spline_slopes, 'output_scale': output_scale}
    _L0_ffn_all = _L0_ffn_setup()
    _L0_ffn_in = {k: v for k, v in _L0_ffn_all.items() if k in ('ln_gamma', 'ln_beta', 'spline_bases', 'spline_slopes', 'output_scale')}
    del _L0_ffn_all
    return {'x': x, 'ctx_2048': ctx_2048, 'itok_BxS_0_1023': itok_BxS_0_1023, 'L0_xattn_W_kvc': _L0_xattn_in['W_kvc'], 'L0_xattn_W_dq': _L0_xattn_in['W_dq'], 'L0_xattn_W_uq': _L0_xattn_in['W_uq'], 'L0_xattn_W_qr': _L0_xattn_in['W_qr'], 'L0_xattn_W_uk': _L0_xattn_in['W_uk'], 'L0_xattn_W_kr': _L0_xattn_in['W_kr'], 'L0_xattn_W_uv': _L0_xattn_in['W_uv'], 'L0_xattn_W_o': _L0_xattn_in['W_o'], 'L0_ffn_ln_gamma': _L0_ffn_in['ln_gamma'], 'L0_ffn_ln_beta': _L0_ffn_in['ln_beta'], 'L0_ffn_spline_bases': _L0_ffn_in['spline_bases'], 'L0_ffn_spline_slopes': _L0_ffn_in['spline_slopes'], 'L0_ffn_output_scale': _L0_ffn_in['output_scale']}

def reference(x, ctx_2048, itok_BxS_0_1023, L0_xattn_W_kvc, L0_xattn_W_dq, L0_xattn_W_uq, L0_xattn_W_qr, L0_xattn_W_uk, L0_xattn_W_kr, L0_xattn_W_uv, L0_xattn_W_o, L0_ffn_ln_gamma, L0_ffn_ln_beta, L0_ffn_spline_bases, L0_ffn_spline_slopes, L0_ffn_output_scale):
    import jax
    import jax.numpy as jnp

    def _L0_xattn_ref(q, kv, seg_id, W_kvc, W_dq, W_uq, W_qr, W_uk, W_kr, W_uv, W_o):
        import jax, jax.numpy as jnp
        import numpy as np
        B, Lq, Lk = (2, 2048, 512)
        Q_DIM, KV_DIM = (1024, 1024)
        H, HD = (16, 128)
        KVC, QC, R = (256, 384, 64)
        LOOKBACK = 8
        NEG = -1e+30

        def _rope(x, L):
            half = x.shape[-1] // 2
            inv_freq = 1.0 / 10000.0 ** (jnp.arange(half, dtype=jnp.float32) / half)
            ang = jnp.arange(L, dtype=jnp.float32)[:, None] * inv_freq
            cos, sin = (jnp.cos(ang), jnp.sin(ang))
            x1, x2 = (x[..., :half], x[..., half:])
            return jnp.concatenate([x1 * cos - x2 * sin, x1 * sin + x2 * cos], axis=-1)
        b, lq, _ = q.shape
        lk = kv.shape[1]
        kv_c = kv @ W_kvc
        q_c = q @ W_dq
        q_nope = (q_c @ W_uq).reshape(b, lq, H, HD).transpose(0, 2, 1, 3)
        q_rope = (q_c @ W_qr).reshape(b, lq, H, R).transpose(0, 2, 1, 3)
        k_nope = (kv_c @ W_uk).reshape(b, lk, H, HD)
        v = (kv_c @ W_uv).reshape(b, lk, H, HD)
        k_rope = kv_c @ W_kr
        q_rope = _rope(q_rope, lq)
        k_rope = _rope(k_rope, lk)
        scale = 1.0 / np.sqrt(HD + R).astype(np.float32)
        scores = (jnp.einsum('bhqd,bkhd->bhqk', q_nope, k_nope) + jnp.einsum('bhqr,bkr->bhqk', q_rope, k_rope)) * scale
        k_ids = jnp.arange(lk)[None, None, :]
        qs = seg_id[:, :, None]
        good = (k_ids <= qs) & (k_ids >= qs - LOOKBACK)
        scores = jnp.where(good[:, None, :, :], scores, NEG)
        attn = jax.nn.softmax(scores, axis=-1)
        out = jnp.einsum('bhqk,bkhd->bqhd', attn, v).reshape(b, lq, H * HD)
        return out @ W_o

    def _L0_ffn_ref(x, ln_gamma, ln_beta, spline_bases, spline_slopes, output_scale):
        import jax, jax.numpy as jnp
        import numpy as np
        D_MODEL = 1024
        NUM_TILES = 64
        D_SLICE = D_MODEL // NUM_TILES
        TILES_PER_CLUSTER = 8
        NUM_CLUSTERS = NUM_TILES // TILES_PER_CLUSTER
        GRID = 16
        LN_EPS = 1e-05
        DIMS = (np.arange(NUM_TILES)[:, None] * D_SLICE + np.arange(D_SLICE)[None, :]) % D_MODEL
        DIMS = jnp.asarray(DIMS, dtype=jnp.int32)

        def _forward(x, ln_gamma, ln_beta, spline_bases, spline_slopes, output_scale):
            B, S, D = x.shape
            N = B * S
            mu = jnp.mean(x, axis=-1, keepdims=True)
            var = jnp.mean(jnp.square(x - mu), axis=-1, keepdims=True)
            xn = (x - mu) * jax.lax.rsqrt(var + LN_EPS) * ln_gamma + ln_beta
            xf = xn.reshape(N, D)
            slope_sign = jnp.sign(jnp.mean(spline_slopes, axis=-1))
            tile_sigs = jnp.zeros((NUM_TILES, D), dtype=x.dtype)
            tile_sigs = tile_sigs.at[jnp.arange(NUM_TILES)[:, None], DIMS].set(slope_sign)
            cluster_sigs = jnp.sign(tile_sigs.reshape(NUM_CLUSTERS, TILES_PER_CLUSTER, D).mean(axis=1))
            cluster_assign = jnp.arange(NUM_TILES, dtype=jnp.int32) // TILES_PER_CLUSTER
            input_sigs = jnp.sign(xf)
            cluster_scores = input_sigs @ cluster_sigs.T
            best_cluster = jnp.argmax(cluster_scores, axis=-1)
            tile_scores = input_sigs @ tile_sigs.T
            in_cluster = cluster_assign[None, :] == best_cluster[:, None]
            tile_idx = jnp.argmax(jnp.where(in_cluster, tile_scores, -jnp.inf), axis=-1)
            tok_dims = DIMS[tile_idx]
            x_slice = jnp.take_along_axis(xf, tok_dims, axis=1)
            tok_min = x_slice.min(axis=1)
            tok_max = x_slice.max(axis=1)
            onehot = tile_idx[None, :] == jnp.arange(NUM_TILES)[:, None]
            tile_min = jnp.where(onehot, tok_min[None, :], jnp.inf).min(axis=1)
            tile_max = jnp.where(onehot, tok_max[None, :], -jnp.inf).max(axis=1)
            mn = tile_min[tile_idx][:, None]
            mx = tile_max[tile_idx][:, None]
            u = jnp.clip((x_slice - mn) / (mx - mn + 1e-08), 0.0, 1.0 - 1e-06)
            gi = jnp.clip((u * GRID).astype(jnp.int32), 0, GRID - 1)
            j = jnp.arange(D_SLICE)[None, :]
            b = spline_bases[tile_idx[:, None], j, gi]
            s = spline_slopes[tile_idx[:, None], j, gi]
            x_local = (u - gi.astype(u.dtype) / GRID) * GRID
            delta = (b + s * x_local) * output_scale[tile_idx][:, None]
            out = jnp.zeros_like(xf).at[jnp.arange(N)[:, None], tok_dims].set(delta)
            return x + out.reshape(B, S, D)
        return _forward(x, ln_gamma, ln_beta, spline_bases, spline_slopes, output_scale)
    x = x + _L0_xattn_ref(_layernorm(x, axis=-1), ctx_2048, itok_BxS_0_1023, L0_xattn_W_kvc, L0_xattn_W_dq, L0_xattn_W_uq, L0_xattn_W_qr, L0_xattn_W_uk, L0_xattn_W_kr, L0_xattn_W_uv, L0_xattn_W_o)
    x = x + _L0_ffn_ref(_layernorm(x, axis=-1), L0_ffn_ln_gamma, L0_ffn_ln_beta, L0_ffn_spline_bases, L0_ffn_spline_slopes, L0_ffn_output_scale)
    return x

_drawn_inputs = setup_inputs


def setup_inputs(seed=0):
    import zlib

    import numpy as np

    out = dict(_drawn_inputs(seed))
    spreads = {}
    factors = {'L0_ffn_ln_gamma': 8.0,
     'L0_ffn_ln_beta': 8.0,
     'L0_ffn_spline_bases': 8.0,
     'L0_ffn_spline_slopes': 8.0,
     'L0_ffn_output_scale': 8.0}
    for name, (base, spread) in spreads.items():
        noise = np.random.default_rng([zlib.crc32(name.encode()), seed]).standard_normal(out[name].shape)
        drawn = base * np.exp(spread * noise) if base else spread * noise
        out[name] = jnp.asarray(drawn.astype(out[name].dtype))
    for name, factor in factors.items():
        out[name] = (out[name] * factor).astype(out[name].dtype)
    return out
```

```python
from contextlib import ExitStack

import concourse.bass as bass
from concourse import mybir

F32 = mybir.dt.float32
F32R = mybir.dt.float32r
BF16 = mybir.dt.bfloat16
I32 = mybir.dt.int32
U32 = mybir.dt.uint32
ALU = mybir.AluOpType
ACT = mybir.ActivationFunctionType
AX = mybir.AxisListType

P = 128
HALF = 512
LOOKBACK = 8
NEG = -1.0e30
BIG = 3.0e38
LN_EPS = 1e-5
ROUND = 8388608.0
GRID = 16
SLICE = 16
NT = 64
CLUSTERS = 8


def xattn_ffn_kernel(nc, x, ctx_in, seg, w_kvc, w_dq, w_uq, w_qr, w_uk, w_kr, w_uv, w_o,
                     gamma, beta, bases, slopes, oscale, cos_t, sin_t, out):
    B, T, D = x.shape
    KVC, QC = w_kvc.shape[1], w_dq.shape[1]
    R = w_kr.shape[1]
    HR = R // 2
    H = w_uq.shape[1] // P
    TT = T // P
    DB = D // P
    CB, QB = KVC // P, QC // P
    HQ = 4
    NQ = H // HQ
    SCALE = 1.0 / float(P + R) ** 0.5
    NTOK = B * T // P
    assert T == HALF and HQ * HR == P and 2 * R == P and D == 2 * HALF and NT * SLICE == D

    A0, AQ = 4, 1 + HQ
    B0, BQ = 3, 1 + HQ
    CQ, DQ = 6, 10
    AN, BN, CN, DN = A0 + NQ * AQ, B0 + NQ * BQ, NQ * CQ, NQ * DQ
    T0, TN = 4 * TT, 4 * TT + H * TT

    def pos_a(b, q, k):
        return b * AN + A0 + q * AQ + k

    def pos_b(b, q, k):
        return b * BN + B0 + q * BQ + k

    def pos_c(b, q, k):
        return b * CN + q * CQ + k

    def pos_d(b, q, k):
        return b * DN + q * DQ + k

    def pos_t(b, q, i, qt):
        return b * TN + T0 + (q * HQ + i) * TT + qt

    def tile_no(b, q, i, qt):
        return b * H * TT + (q * HQ + i) * TT + qt

    NF = 25
    NL = 5

    with ExitStack() as ctx:
        def sb(name, shape, dt=F32):
            return ctx.enter_context(nc.sbuf_tensor(name, shape, dt))

        def bank(name, dt=F32):
            return ctx.enter_context(nc.psum_tensor(name, [P, HALF], dt))

        def sem(name):
            return ctx.enter_context(nc.semaphore(name))

        psS = [bank("psS0"), bank("psS1")]
        psT = [bank("psT0"), bank("psT1")]
        psA, psB, psC, psD = bank("psA"), bank("psB"), bank("psC"), bank("psD")

        wD = sb("w_down", [P, DB, QC])
        wuq = sb("w_uq_ring", [P, 2, QB, P])
        wuk = sb("w_uk_ring", [P, 2, CB, P])
        wqr = sb("w_qr_quad", [P, QB, HQ * R])
        wqp = sb("w_qr_sorted", [P, QB, 2, HQ * HR])
        wuv = sb("w_uv_quad", [P, CB, HQ * P])
        wo = sb("w_o_quad", [P, 2, HQ, HALF])
        wkr = sb("w_kr_in", [P, CB, R])
        wkra = sb("w_kr_a", [P, CB, 2, R])
        wkrb = sb("w_kr_b", [P, CB, 2, R])
        xs = sb("x_stage", [P, 2, D])
        xT = sb("xT", [P, DB, T])
        qc = sb("q_c", [P, QB, T])
        kvc = sb("kv_c", [P, CB, T])
        rt = sb("rope_terms", [P, 2, T])
        rr = sb("rope_out", [P, 2, T])
        rh = sb("rope_hi", [P, 2, T], F32R)
        rl = sb("rope_lo", [P, 2, T], F32R)
        stack = sb("q_rope_stack", [P, HQ, T], F32R)
        krh = sb("k_rope_hi", [P, T], F32R)
        krl = sb("k_rope_lo", [R, T], F32R)
        V = sb("values", [P, TT, HQ * P])
        qh, ql = sb("q_hi", [P, 2, T], F32R), sb("q_lo", [P, 2, T], F32R)
        kh, kl = sb("k_hi", [P, 2, T], F32R), sb("k_lo", [P, 2, T], F32R)
        E = sb("probs", [P, TT, T])
        PT = sb("probsT", [P, TT, T])
        mask = sb("mask", [P, TT, T], BF16)
        attn = sb("attn", [P, HQ, T])
        acc = sb("acc", [P, TT, D])
        cosT, sinT = sb("cosT", [P, T]), sb("sinT", [P, T])
        ident = sb("ident", [P, P])
        identb = sb("ident_b", [P, P], BF16)
        kidx = sb("key_index", [P, T])
        mtmp = sb("mask_terms", [P, 2, T])
        segi = sb("seg_int", [P, TT], I32)
        segf = sb("seg_f", [P, 2, TT])
        nhalf = sb("minus_half", [P, 1])
        mx = sb("neg_max", [P, 2, TT])
        rs = sb("row_sum", [P, 2, TT])
        ri = sb("row_sum_inverse", [P, 2, TT])
        st = sb("ln_stats", [P, 2, 6])
        mv = sb("ln_mean_var", [P, 4])
        st2 = sb("ffn_stats", [P, 2, 6])
        mv2 = sb("ffn_mean_var", [P, 8])
        gb = sb("gamma_b", [P, D])
        bb = sb("beta_b", [P, D])
        ssb = sb("slope_sign_b", [P, D])
        sl = xT[:, 0, 0:256]
        tie = sb("tie_order", [P, NT])
        ts = sb("tile_scores", [P, NT])
        cs = sb("cluster_scores", [P, CLUSTERS])
        key = sb("tile_key", [P, NT])
        kmax = sb("key_max", [P, 1])
        oh = sb("onehot", [P, NTOK, NT], BF16)
        xsl = sb("x_slice", [P, NTOK, SLICE])
        mm = sb("slice_min_max", [P, 2])
        cand = sb("candidates", [P, 3, NT])
        run = sb("run_min_max", [P, 2, NT])
        fy = xT[:, 0:2, :].rearrange("p a n -> p (a n)")
        fx = xT[:, 2:4, :].rearrange("p a n -> p (a n)")
        fs = xT[:, 4:6, :].rearrange("p a n -> p (a n)")
        fsel = xT[:, 6:8, :].rearrange("p a n -> p (a n)")
        tmi = xT[:, 7, 0:T].bitcast(I32)
        sgn64 = xT[:, 1, 0:SLICE]
        ssum = xT[:, 1, SLICE:2 * SLICE]

        AFTER[:] = [sem("waits_apart")]
        s_const = sem("constants_in")
        s_wkr = sem("w_kr_in_sem")
        s_sl = sem("slopes_in")
        s_iota = sem("ramps")
        s_setup = sem("setup_pool")
        s_setv = sem("setup_vector")
        s_seta = sem("setup_scalar")
        s_ssb = sem("slope_sign_in")
        s_ssd = sem("slope_sign_dram")
        s_wd = sem("w_down_in")
        s_wuq, s_wuk = [sem("w_uq_in0"), sem("w_uq_in1")], [sem("w_uk_in0"), sem("w_uk_in1")]
        s_sorted = sem("w_qr_sorted_done")
        s_wqr, s_wuv = sem("w_qr_in"), sem("w_uv_in")
        s_wo = [sem("w_o_in0"), sem("w_o_in1")]
        s_xs = [sem("x_in0"), sem("x_in1")]
        s_seg = sem("seg_in")
        s_rstd, s_rstd2 = sem("ln_rstd"), sem("ffn_rstd")
        s_rinv = sem("row_sum_inverse_done")
        s_ln = sem("ln_steps")
        s_mask = sem("mask_steps")
        s_acc = sem("acc_in")
        fullA, fullB, fullC, fullD = sem("fullA"), sem("fullB"), sem("fullC"), sem("fullD")
        freeA, freeB, freeC, freeD = sem("freeA"), sem("freeB"), sem("freeC"), sem("freeD")
        fullT, freeT = sem("fullT"), sem("freeT")
        s_S, s_sm, s_exp, s_prob = sem("scores"), sem("scores_masked"), sem("exps"), sem("probs_done")
        s_qhi, s_khi = sem("q_hi_done"), sem("k_hi_done")
        s_rope, s_rhi, s_rlo = sem("rope_steps"), sem("rope_hi_done"), sem("rope_lo_done")
        s_stack = [sem(f"stack_in{i}") for i in range(HQ)]
        s_f = sem("ffn_steps")
        s_sign, s_fpool = sem("ffn_sign"), sem("ffn_pool")
        s_z = sem("z_out")
        s_tab = sem("tables_in")
        s_g = sem("gather_pe")
        s_ge = sem("gather_scalar")
        s_gv = sem("gather_vector")
        s_gf = sem("spline_row_used")
        s_gb = sem("spline_row")
        s_sc = sem("scattered")

        x_t = x.rearrange("b (t p) d -> b t p d", p=P)
        c_t = ctx_in.rearrange("b (t p) d -> b t p d", p=P)
        o_t = out.rearrange("b (t p) d -> b t p d", p=P)
        seg_v = seg.rearrange("b (t p) -> b p t", p=P)
        wdq_v = w_dq.rearrange("(c p) n -> p c n", p=P)
        wkvc_v = w_kvc.rearrange("(c p) n -> p c n", p=P)
        wuq_v = w_uq.rearrange("(c p) n -> p c n", p=P)
        wqr_v = w_qr.rearrange("(c p) n -> p c n", p=P)
        wuk_v = w_uk.rearrange("(c p) n -> p c n", p=P)
        wkr_v = w_kr.rearrange("(c p) n -> p c n", p=P)
        wuv_v = w_uv.rearrange("(c p) n -> p c n", p=P)
        wo_v = w_o.rearrange("(h p) n -> p h n", p=P)
        ss_dram = nc.dram_tensor("slope_sign_scratch", [NT, SLICE], F32).ap()

        spl = E[0:NT, 0, :].rearrange("p (a n) -> p a n", a=2)
        tab = E[0:NT, 1, 0:4]
        prod = E[:, 2:4, :]
        ohT = acc[0:NT, :, :].rearrange("p t n -> p (t n)")
        eqb = xT[:, :, :].rearrange("p a n -> p (a n)")
        bsel = PT[:, 0:2, :].rearrange("p a n -> p (a n)")
        fin = PT[:, 2, 0:NTOK * 4].rearrange("p (k c) -> p k c", c=4)
        fu = attn[:, 0, :].rearrange("p (k j) -> p k j", j=SLICE)
        fl = attn[:, 1, :].rearrange("p (k j) -> p k j", j=SLICE)
        fg = attn[:, 2, :].rearrange("p (k j) -> p k j", j=SLICE)
        fd = attn[:, 3, :].rearrange("p (k j) -> p k j", j=SLICE)
        gramp = PT[:, 3, 0:GRID]
        tokb = PT[:, 3, 32:32 + NTOK]
        idxf = PT[:, 3, 96:96 + NTOK]
        dena = PT[:, 3, 160:160 + NTOK]
        idxi = V[:, 0, 0:NTOK].bitcast(I32)
        rampi = V[:, 1, 0:64].bitcast(I32)
        tmpb = V[:, 2:4, :].rearrange("p a n -> p (a n)")

        psTb = [p[:, :].bitcast(BF16) for p in psT]

        def onehot_wide(k):
            return oh[:, k, :].rearrange("p (t a) -> p t a", a=1).broadcast_to([P, NT, SLICE])

        def batches(eng, body):
            body(0, True, False)
            with eng.Fori(1, B - 1) as b:
                body(b, False, False)
            body(B - 1, False, True)

        block = ctx.enter_context(nc.Block())

        @block.sync
        def _(sp):
            def load_dq(b):
                if not (isinstance(b, int) and b == 0):
                    wait_apart(sp, fullA, (b - 1) * AN + 3)
                    wait_apart(sp, fullB, (b - 1) * BN + 2)
                sp.dma_start(wD[:, :, :], wdq_v).then_inc(s_wd, 16)

            def load_kvc(b):
                wait_apart(sp, fullA, b * AN + 2)
                wait_apart(sp, fullB, b * BN + 1)
                sp.dma_start(wD[:, :, 0:KVC], wkvc_v).then_inc(s_wd, 16)

            def load_xs(b, j):
                if j >= 2:
                    wait_apart(sp, fullT, b * TN + 2 * (j - 2) + 2)
                elif not (isinstance(b, int) and b == 0):
                    wait_apart(sp, fullT, (b - 1) * TN + 2 * (j + 6) + 2)
                src = x_t[b, j] if j < TT else c_t[b, j - TT]
                sp.dma_start(xs[:, j % 2, :], src).then_inc(s_xs[j % 2], 16)

            def load_uq(h, slot):
                sp.dma_start(wuq[:, slot], wuq_v[:, :, bass.ds(h * P, P)]).then_inc(s_wuq[slot], 16)

            def load_uk(h, slot):
                sp.dma_start(wuk[:, slot], wuk_v[:, :, bass.ds(h * P, P)]).then_inc(s_wuk[slot], 16)

            def load_qr(q):
                sp.dma_start(wqr[:, :, :], wqr_v[:, :, bass.ds(q * HQ * R, HQ * R)]).then_inc(s_wqr, 16)

            def load_uv(q):
                sp.dma_start(wuv[:, :, :], wuv_v[:, :, bass.ds(q * HQ * P, HQ * P)]).then_inc(s_wuv, 16)

            def load_o(q, half):
                sp.dma_start(wo[:, half], wo_v[:, bass.ds(q * HQ, HQ), half * HALF:(half + 1) * HALF])\
                    .then_inc(s_wo[half], 16)

            def stack_head(b, q, i):
                n = b * (NQ + 1) + 1 + q
                if not (isinstance(b, int) and b == 0 and isinstance(q, int) and q == 0):
                    wait_apart(sp, s_S, tile_no(b, q, i, 0) - (HQ - 1) * TT)
                wait_apart(sp, s_rhi, n + 1)
                wait_apart(sp, s_rlo, n + 1)
                src = slice(i * HR, (i + 1) * HR)
                for lo, part in ((0, rh), (R, rl)):
                    for j in range(2):
                        sp.dma_start(stack[lo + j * HR:lo + (j + 1) * HR, i, :].bitcast(F32),
                                     part[src, j, :].bitcast(F32)).then_inc(s_stack[i], 16)

            def into(b, q, nxt):
                wait_apart(sp, s_sorted, b * NQ + q + 1)
                load_qr(nxt)
                for i in range(HQ - 1):
                    stack_head(b, q, i)
                wait_apart(sp, fullA, pos_a(b, q, 2))
                load_uq(q * HQ + 2, 0)
                wait_apart(sp, fullB, pos_b(b, q, 2))
                load_uk(q * HQ + 2, 0)
                stack_head(b, q, HQ - 1)

            def heads(b, q, nxt, q0):
                for i in range(HQ - 1):
                    slot = (i + 1) % 2
                    h = q * HQ + HQ - 1 if i == 0 else nxt * HQ + i - 1
                    wait_apart(sp, fullA, pos_a(b, q, 2 + i) + 1)
                    load_uq(h, slot)
                    wait_apart(sp, fullB, pos_b(b, q, 2 + i) + 1)
                    load_uk(h, slot)
                    if i == 0:
                        if not q0:
                            for half in range(2):
                                wait_apart(sp, fullC, pos_c(b, q - 1, 4 + 2 * half))
                                wait_apart(sp, fullD, pos_d(b, q - 1, 8 + 2 * half))
                                load_o(q, half)
                        wait_apart(sp, fullC, pos_c(b, q, 2))
                        wait_apart(sp, fullD, pos_d(b, q, 2))
                        load_uv(nxt)

            sp.dma_start(wkr[:, :, :], wkr_v).then_inc(s_wkr, 16)
            sp.dma_start(cosT[:, :], cos_t).then_inc(s_const, 16)
            sp.dma_start(sinT[:, :], sin_t).then_inc(s_const, 16)
            load_xs(0, 0)
            load_xs(0, 1)
            load_dq(0)
            load_xs(0, 2)
            load_xs(0, 3)
            load_qr(0)
            for h in range(2):
                load_uq(h, h)
                load_uk(h, h)
            load_uv(0)
            load_xs(0, 4)
            load_xs(0, 5)
            load_kvc(0)
            load_xs(0, 6)
            load_xs(0, 7)
            sp.dma_start(gb[:, :], gamma.rearrange("(a n) -> a n", a=1).broadcast_to([P, D])).then_inc(s_const, 16)
            sp.dma_start(bb[:, :], beta.rearrange("(a n) -> a n", a=1).broadcast_to([P, D])).then_inc(s_const, 16)
            for half in range(2):
                load_o(0, half)
            into(0, 0, 1)

            def body(b, first, last):
                if not last:
                    load_xs(b + 1, 0)
                    load_xs(b + 1, 1)
                    load_dq(b + 1)
                heads(b, 0, 1, True)
                with sp.Fori(1, NQ) as q:
                    into(b, q, (q + 1) % NQ)
                    heads(b, q, (q + 1) % NQ, False)
                if not last:
                    load_xs(b + 1, 2)
                    load_xs(b + 1, 3)
                    for half in range(2):
                        if half == 1:
                            load_xs(b + 1, 4)
                            load_xs(b + 1, 5)
                            load_kvc(b + 1)
                        wait_apart(sp, fullC, pos_c(b, NQ - 1, 4 + 2 * half))
                        wait_apart(sp, fullD, pos_d(b, NQ - 1, 8 + 2 * half))
                        load_o(0, half)
                    load_xs(b + 1, 6)
                    load_xs(b + 1, 7)
                    into(b + 1, 0, 1)

            batches(sp, body)
            wait_apart(sp, s_prob, tile_no(B, 0, 0, 0))
            wait_apart(sp, fullT, B * TN)
            sp.dma_start(spl[:, 0, :], bases.rearrange("t j g -> t (j g)")).then_inc(s_tab, 16)
            sp.dma_start(spl[:, 1, :], slopes.rearrange("t j g -> t (j g)")).then_inc(s_tab, 16)
            sp.dma_start(tab[:, 2:3], oscale.rearrange("(t a) -> t a", a=1), allow_slow_non_contiguous=True).then_inc(s_tab, 16)
            wait_apart(sp, s_z, 16 * NTOK)

        @block.gpsimd
        def _(pool):
            n_set = [0]

            def setup(ins):
                n_set[0] += 1
                ins.then_inc(s_setup, 1)
                wait_apart(pool, s_setup, n_set[0])

            setup(pool.memset(ident[:, :], 0.0))
            setup(pool.affine_select(out=ident[:, :], in_=ident[:, :], compare_op=ALU.not_equal, fill=1.0,
                                     base=0, pattern=[[-1, P]], channel_multiplier=1))
            setup(pool.tensor_copy(identb[:, :], ident[:, :]))
            setup(pool.iota(tmi[:, 0:T], [[1, T]], base=0, channel_multiplier=0))
            setup(pool.tensor_copy(kidx[:, :], tmi[:, 0:T]))
            setup(pool.iota(tmi[:, 0:NT], [[-512, CLUSTERS], [-1, NT // CLUSTERS]],
                            base=512 * (CLUSTERS - 1) + 8 * SLICE + NT // CLUSTERS - 1, channel_multiplier=0))
            setup(pool.tensor_copy(tie[:, :], tmi[:, 0:NT]))
            setup(pool.memset(run[:, 0, :], BIG))
            setup(pool.memset(run[:, 1, :], -BIG))
            setup(pool.memset(nhalf[:, :], -0.5))
            pool.dma_start(sl[0:NT, :], slopes.rearrange("t j g -> t (j g)")).then_inc(s_sl, 16)
            wait_apart(pool, s_seta, 1)
            pool.dma_start(ss_dram, sgn64[0:NT, :]).then_inc(s_ssd, 16)
            wait_apart(pool, s_ssd, 16)
            pool.dma_start(ssb[:, :], ss_dram.rearrange("(a t) j -> a (t j)", a=1).broadcast_to([P, D]))\
                .then_inc(s_ssb, 16)
            for t in range(TT):
                pool.dma_start(acc[:, t, :], x_t[0, t]).then_inc(s_acc, 16)

            def masks(b, first):
                if not first:
                    wait_apart(pool, s_sm, b * H * TT)
                pool.dma_start(segi[:, :], seg_v[b], allow_slow_non_contiguous=True).then_inc(s_seg, 16)
                wait_apart(pool, s_seg, 16 * (b + 1))
                c = Chain(pool, s_mask, b * NM)
                c.do(pool.tensor_copy(segf[:, 0, :], segi[:, :]))
                c.do(pool.tensor_scalar(segf[:, 1, :], segf[:, 0, :], -float(LOOKBACK), None, ALU.add))
                for t in range(TT):
                    lo, hi = mtmp[:, 0, :], mtmp[:, 1, :]
                    c.do(pool.tensor_scalar(lo, kidx[:, :], segf[:, 1, t:t + 1], None, ALU.is_ge))
                    c.do(pool.tensor_scalar(hi, kidx[:, :], segf[:, 0, t:t + 1], None, ALU.is_le))
                    c.do(pool.tensor_tensor(lo, lo, hi, ALU.mult))
                    c.do(pool.tensor_scalar(mask[:, t, :], lo, 1.0, -NEG, ALU.subtract, ALU.mult))
                assert c.n == NM

            def rstds(b):
                for t in range(TT):
                    wait_apart(pool, s_ln, (b * TT + t) * NL + 4)
                    pool.tensor_tensor(mv[:, 3:4], mv[:, 2:3], nhalf[:, :], ALU.pow).then_inc(s_rstd, 1)

            def rope_lo(b, k):
                n = b * (NQ + 1) + 1 + k
                wait_apart(pool, s_rhi, n + 1)
                pool.tensor_tensor(rl[:, :, :], rr[:, :, :], rh[:, :, :].bitcast(F32), ALU.subtract)\
                    .then_inc(s_rlo, 1)

            def k_rope_lo(b):
                n = b * (NQ + 1)
                wait_apart(pool, s_rhi, n + 1)
                pool.tensor_tensor(krl[:, :], rr[0:R, 0, :], krh[0:R, :].bitcast(F32), ALU.subtract)\
                    .then_inc(s_rlo, 1)

            def ffn(b, t, last=False):
                base = (b * TT + t) * NF
                wait_apart(pool, s_f, base + 4)
                pool.tensor_tensor(mv2[:, 3:4], mv2[:, 2:3], nhalf[:, :], ALU.pow).then_inc(s_rstd2, 1)
                wait_apart(pool, s_f, base + 9)
                pool.tensor_tensor(mv2[:, 7:8], mv2[:, 6:7], nhalf[:, :], ALU.pow).then_inc(s_rstd2, 1)
                wait_apart(pool, s_sign, b * TT + t + 1)
                pool.tensor_tensor(fs, fs, ssb[:, :], ALU.mult).then_inc(s_fpool, 1)
                pool.tensor_tensor(acc[:, t, :], acc[:, t, :], fy, ALU.add).then_inc(s_fpool, 1)
                wait_apart(pool, s_fpool, (b * TT + t) * 3 + 2)
                pool.dma_start(o_t[b, t], acc[:, t, :]).then_inc(s_z, 16)
                wait_apart(pool, s_f, base + 17)
                pool.tensor_tensor(fsel.rearrange("p (t j) -> p t j", j=SLICE),
                                   fx.rearrange("p (t j) -> p t j", j=SLICE),
                                   onehot_wide(b * TT + t), ALU.mult).then_inc(s_fpool, 1)
                if not last:
                    wait_apart(pool, s_z, 16 * (b * TT + t + 1))
                    pool.dma_start(acc[:, t, :], x_t[b + 1, t]).then_inc(s_acc, 16)

            def sort_qr(n):
                wait_apart(pool, s_wqr, 16 * (n + 1))
                for c in range(QB):
                    for j in range(2):
                        ins = pool.tensor_copy(
                            wqp[:, c, j, :].rearrange("p (h r) -> p h r", r=HR),
                            wqr[:, c, :].rearrange("p (h j r) -> p j h r", j=2, r=HR)[:, j])
                ins.then_inc(s_sorted, 1)

            rstds(0)
            sort_qr(0)
            masks(0, True)
            k_rope_lo(0)
            rope_lo(0, 0)
            sort_qr(1)

            def body(b, first, last):
                def quad(q, q0):
                    if q0 and not first:
                        for t in range(TT):
                            ffn(b - 1, t)

                quad(0, True)
                with pool.Fori(1, NQ) as q:
                    rope_lo(b, q)
                    sort_qr(b * NQ + q + 1)
                if not last:
                    rstds(b + 1)
                    masks(b + 1, False)
                    k_rope_lo(b + 1)
                    rope_lo(b + 1, 0)
                    sort_qr((b + 1) * NQ + 1)

            batches(pool, body)
            for t in range(TT):
                ffn(B - 1, t, True)

            wait_apart(pool, fullD, B * DN)
            wait_apart(pool, fullC, B * CN)
            wait_apart(pool, s_prob, B * H * TT)
            c = Chain(pool, s_iota, 0)
            c.do(pool.iota(rampi[:, 0:GRID], [[1, GRID]], base=0, channel_multiplier=0))
            c.do(pool.tensor_copy(gramp, rampi[:, 0:GRID]))
            c.do(pool.iota(rampi[:, 0:NTOK], [[P * NT, NTOK]], base=0, channel_multiplier=NT))
            c.do(pool.tensor_copy(tokb, rampi[:, 0:NTOK]))
            wait_apart(pool, fullT, B * TN)
            c.do(pool.iota(rampi[0:NT, 0:1], [[1, 1]], base=0, channel_multiplier=1))
            c.do(pool.tensor_copy(tab[:, 3:4], rampi[0:NT, 0:1]))
            rows = out.rearrange("b s (t j) -> (b s t) j", j=SLICE)
            wait_apart(pool, s_z, 16 * NTOK)
            wait_apart(pool, s_gv, NG)
            for k in range(NTOK):
                pool.indirect_dma_start(rows, bass.IndirectOffsetOnAxis(ap=idxi[:, k:k + 1], axis=0),
                                        fd[:, k, :], None, compute_op=ALU.add).then_inc(s_sc, 16)
            wait_apart(pool, s_sc, 16 * NTOK)

        @block.scalar
        def _(act):
            act.wait_ge(s_setv, 1)
            act.activation(sgn64[0:NT, :], ssum[0:NT, :], ACT.Sign).then_inc(s_seta, 1)

            def stage_turned(b, j, ctx_side):
                for half in range(2):
                    k = (TT * 2 if ctx_side else 0) + 2 * j + half
                    act.wait_ge(fullT, b * TN + k + 1)
                    if k == 0 and not (isinstance(b, int) and b <= 1):
                        act.wait_ge(s_f, (b - 1) * TT * NF)
                        act.wait_ge(s_fpool, (b - 1) * TT * 3)
                    if k == 0 and isinstance(b, int) and b == 0:
                        act.wait_ge(s_setup, 10)
                        act.wait_ge(s_ssd, 16)
                    act.activation(xT[:, 4 * half:4 * half + 4, j * P:(j + 1) * P],
                                   psT[k % 2][:, :].rearrange("p (c n) -> p c n", c=4), ACT.Copy)\
                       .then_inc(freeT, 1)

            def down(ps, full, free, n, dst):
                act.wait_ge(full, n + 1)
                act.activation(dst, ps[:, :], ACT.Copy).then_inc(free, 1)

            def q_hi(b, q, i):
                act.wait_ge(fullA, pos_a(b, q, 1 + i) + 1)
                act.activation(qh[:, i % 2, :], psA[:, :], ACT.Copy).then_inc(s_qhi, 1)

            def k_hi(b, q, i):
                act.wait_ge(fullB, pos_b(b, q, 1 + i) + 1)
                act.activation(kh[:, i % 2, :], psB[:, :], ACT.Copy).then_inc(s_khi, 1)

            def values(b, q):
                for kt in range(TT):
                    ps, full, free, n = ((psC, fullC, freeC, pos_c(b, q, kt // 2)) if kt % 2 == 0 else
                                         (psD, fullD, freeD, pos_d(b, q, kt // 2)))
                    act.wait_ge(full, n + 1)
                    act.activation(V[:, kt, :], ps[:, :], ACT.Copy).then_inc(free, 1)

            def k_rope_hi(b):
                n = b * (NQ + 1)
                act.wait_ge(s_rope, b * NR + 1)
                act.activation(krh[:, :], rr[:, 0, :], ACT.Copy).then_inc(s_rhi, 1)

            def rope_hi(b, q, prev):
                act.wait_ge(s_rope, b * NR + 1 + 4 * (q + 1))
                if prev:
                    for i in range(HQ):
                        act.wait_ge(s_stack[i], 64 * (b * NQ + q))
                act.activation(rh[:, :, :], rr[:, :, :], ACT.Copy).then_inc(s_rhi, 1)

            def expo(b, q, i, qt):
                act.wait_ge(s_sm, tile_no(b, q, i, qt) + 1)
                act.activation(E[:, qt, :], E[:, qt, :], ACT.Exp, scale=-1.0,
                               bias=mx[:, i % 2, qt:qt + 1],
                               accum_out=rs[:, i % 2, qt:qt + 1]).then_inc(s_exp, 1)

            def probs_turned(b, q, i, qt):
                act.wait_ge(fullT, pos_t(b, q, i, qt) + 1)
                act.activation(PT[:, :, qt * P:(qt + 1) * P],
                               psT[qt % 2][:, :].rearrange("p (c n) -> p c n", c=TT), ACT.Copy)\
                   .then_inc(freeT, 1)

            def attended(b, q, i):
                act.wait_ge(fullD, pos_d(b, q, 2 + i) + 1)
                act.activation(attn[:, i, :], psD[:, :], ACT.Copy).then_inc(freeD, 1)

            def sign(b, t):
                act.wait_ge(s_f, (b * TT + t) * NF + 11)
                act.activation(fs, fx, ACT.Sign).then_inc(s_sign, 1)

            def prologue(b, first):
                for j in range(TT):
                    stage_turned(b, j, False)
                down(psA, fullA, freeA, b * AN, qc[:, 0, :])
                down(psB, fullB, freeB, b * BN, qc[:, 1, :])
                down(psA, fullA, freeA, b * AN + 1, qc[:, 2, :])
                for j in range(TT):
                    stage_turned(b, j, True)
                down(psB, fullB, freeB, b * BN + 1, kvc[:, 0, :])
                down(psA, fullA, freeA, b * AN + 2, kvc[:, 1, :])
                k_rope_hi(b)
                rope_hi(b, 0, not first)
                q_hi(b, 0, 0)
                k_hi(b, 0, 0)

            prologue(0, True)

            def body(b, first, last):
                def head(q, i, q0, nxt=None):
                    expo(b, q, i, 0)
                    expo(b, q, i, 1)
                    if i > 0:
                        attended(b, q, i - 1)
                    elif not q0:
                        attended(b, q - 1, HQ - 1)
                    probs_turned(b, q, i, 0)
                    expo(b, q, i, 2)
                    if nxt is not None:
                        rope_hi(b, nxt, True)
                        q_hi(b, nxt, 0)
                    elif i < HQ - 1:
                        q_hi(b, q, i + 1)
                    probs_turned(b, q, i, 1)
                    expo(b, q, i, 3)
                    if nxt is not None:
                        k_hi(b, nxt, 0)
                    elif i < HQ - 1:
                        k_hi(b, q, i + 1)
                    if q0 and not first:
                        for t in FFN_AT[i]:
                            sign(b - 1, t)
                    probs_turned(b, q, i, 2)
                    probs_turned(b, q, i, 3)
                    if i == 0 and not q0:
                        values(b, q)

                values(b, 0)
                for i in range(HQ - 1):
                    head(0, i, True)
                with act.Fori(1, NQ) as q:
                    head(q - 1, HQ - 1, False, q)
                    for i in range(HQ - 1):
                        head(q, i, False)
                head(NQ - 1, HQ - 1, False)
                attended(b, NQ - 1, HQ - 1)
                if not last:
                    prologue(b + 1, False)

            batches(act, body)
            for t in range(TT):
                sign(B - 1, t)
            act.wait_ge(s_z, 16 * NTOK)
            for g in range(NTOK // 4):
                act.wait_ge(s_g, 2 + g + 1)
                act.activation(ohT[:, g * 512:(g + 1) * 512], psTb[g % 2][0:NT, 0:512], ACT.Copy)\
                   .then_inc(s_ge, 1)

        @block.vector
        def _(dve):
            dve.wait_ge(s_sl, 16)
            dve.tensor_reduce(ssum[0:NT, :], sl[0:NT, :].rearrange("p (j g) -> p j g", g=GRID), AX.X, ALU.add)\
               .then_inc(s_setv, 1)
            dve.wait_ge(s_wkr, 16)
            for c in range(2):
                dve.tensor_copy(wkra[:, :, c, :], wkr[:, :, :]).then_inc(s_setv, 1)
                dve.tensor_scalar(wkrb[:, :, c, 0:HR], wkr[:, :, HR:R], -1.0, None, ALU.mult).then_inc(s_setv, 1)
                dve.tensor_copy(wkrb[:, :, c, HR:R], wkr[:, :, 0:HR]).then_inc(s_setv, 1)

            def norm_x(b, t):
                xt = xs[:, t % 2, :]
                dve.wait_ge(s_xs[t % 2], 16 * (b * TT + t // 2 + 1))
                c = Chain(dve, s_ln, (b * TT + t) * NL)
                for h in range(2):
                    c.do(dve.bn_stats(st[:, h, :], xt[:, h * HALF:(h + 1) * HALF]), wait=h == 1)
                c.do(dve.bn_aggr(mv[:, 0:2], st[:, :, :].rearrange("p a s -> p (a s)")))
                c.do(dve.tensor_scalar(mv[:, 2:3], mv[:, 1:2], LN_EPS, None, ALU.add), wait=False)
                dve.wait_ge(s_rstd, b * TT + t + 1)
                c.do(dve.tensor_scalar(xt, xt, mv[:, 0:1], mv[:, 3:4], ALU.subtract, ALU.mult))
                assert c.n == NL

            def rope_k(b):
                if not (isinstance(b, int) and b == 0):
                    dve.wait_ge(s_rhi, b * (NQ + 1))
                    dve.wait_ge(s_rlo, b * (NQ + 1))
                dve.wait_ge(fullA, b * AN + 4)
                dve.tensor_tensor(rt[:, 0, :], psA[:, :], cosT[:, :], ALU.mult).then_inc(freeA, 1)
                dve.wait_ge(fullB, b * BN + 3)
                dve.tensor_tensor(rt[:, 1, :], psB[:, :], sinT[:, :], ALU.mult).then_inc(freeB, 1)
                dve.wait_ge(freeA, b * AN + 4)
                dve.wait_ge(freeB, b * BN + 3)
                dve.tensor_tensor(rr[:, 0, :], rt[:, 0, :], rt[:, 1, :], ALU.add).then_inc(s_rope, 1)

            def rope_q(b, q):
                n = b * (NQ + 1) + 1 + q
                c = Chain(dve, s_rope, b * NR + 1 + 4 * q)
                dve.wait_ge(s_rope, b * NR + 1 + 4 * q)
                dve.wait_ge(fullA, pos_a(b, q, 0) + 1)
                c.do(dve.tensor_tensor(rt[:, 0, :], psA[:, :], cosT[:, :], ALU.mult), wait=False)
                dve.wait_ge(fullB, pos_b(b, q, 0) + 1)
                c.do(dve.tensor_tensor(rt[:, 1, :], psB[:, :], sinT[:, :], ALU.mult))
                dve.wait_ge(s_rhi, n)
                dve.wait_ge(s_rlo, n)
                c.do(dve.tensor_tensor(rr[:, 0, :], rt[:, 0, :], rt[:, 1, :], ALU.subtract))
                dve.tensor_tensor(rt[:, 0, :], psA[:, :], sinT[:, :], ALU.mult).then_inc(freeA, 1)
                dve.tensor_tensor(rt[:, 1, :], psB[:, :], cosT[:, :], ALU.mult).then_inc(freeB, 1)
                dve.wait_ge(freeA, pos_a(b, q, 0) + 1)
                dve.wait_ge(freeB, pos_b(b, q, 0) + 1)
                c.do(dve.tensor_tensor(rr[:, 1, :], rt[:, 0, :], rt[:, 1, :], ALU.add), wait=False)

            def q_lo(b, q, i):
                dve.wait_ge(s_qhi, b * H + q * HQ + i + 1)
                dve.tensor_tensor(ql[:, i % 2, :], psA[:, :], qh[:, i % 2, :].bitcast(F32), ALU.subtract)\
                   .then_inc(freeA, 1)

            def k_lo(b, q, i):
                dve.wait_ge(s_khi, b * H + q * HQ + i + 1)
                dve.tensor_tensor(kl[:, i % 2, :], psB[:, :], kh[:, i % 2, :].bitcast(F32), ALU.subtract)\
                   .then_inc(freeB, 1)

            def mask_scores(b, q, i, qt, head0):
                n = tile_no(b, q, i, qt)
                dve.wait_ge(s_S, n + 1)
                if head0:
                    dve.wait_ge(s_mask, (b + 1) * NM)
                    if not (isinstance(b, int) and b == 0):
                        wait_apart(dve, fullT, b * TN - TT + qt + 1)
                else:
                    wait_apart(dve, fullT, pos_t(b, q, i, qt) - TT + 1)
                dve.tensor_tensor_reduce(E[:, qt, :], psS[qt % 2][:, :], mask[:, qt, :], -SCALE, BIG,
                                         ALU.add, ALU.min, mx[:, i % 2, qt:qt + 1]).then_inc(s_sm, 1)

            def divide(b, q, i, qt):
                dve.wait_ge(s_exp, tile_no(b, q, i, qt) + 1)
                dve.reciprocal(ri[:, i % 2, qt:qt + 1], rs[:, i % 2, qt:qt + 1]).then_inc(s_rinv, 1)
                dve.wait_ge(s_rinv, tile_no(b, q, i, qt) + 1)
                dve.tensor_scalar(E[:, qt, :], E[:, qt, :], ri[:, i % 2, qt:qt + 1], None, ALU.mult)\
                   .then_inc(s_prob, 1)

            def add_out(b, q, w, first_add):
                half, t = w // TT, w % TT
                if w % 2 == 0:
                    ps, full, free, n = psC, fullC, freeC, pos_c(b, q, 2 + w // 2)
                else:
                    ps, full, free, n = psD, fullD, freeD, pos_d(b, q, 6 + w // 2)
                if first_add:
                    dve.wait_ge(s_acc, 16 * TT * (b + 1))
                dve.wait_ge(full, n + 1)
                if w < 2:
                    pass
                a = acc[:, t, half * HALF:(half + 1) * HALF]
                dve.tensor_tensor(a, a, ps[:, :], ALU.add).then_inc(free, 1)

            def ffn_norms(b, t):
                c = Chain(dve, s_f, (b * TT + t) * NF)
                if t == 0:
                    dve.wait_ge(freeC, pos_c(b, NQ - 1, 6))
                    dve.wait_ge(freeD, pos_d(b, NQ - 1, 10))
                x1 = acc[:, t, :]
                for h in range(2):
                    c.do(dve.bn_stats(st2[:, h, :], x1[:, h * HALF:(h + 1) * HALF]), wait=h == 1)
                c.do(dve.bn_aggr(mv2[:, 0:2], st2[:, :, :].rearrange("p a s -> p (a s)")))
                c.do(dve.tensor_scalar(mv2[:, 2:3], mv2[:, 1:2], LN_EPS, None, ALU.add), wait=False)
                dve.wait_ge(s_rstd2, 2 * (b * TT + t) + 1)
                c.do(dve.tensor_scalar(fy, x1, mv2[:, 0:1], mv2[:, 3:4], ALU.subtract, ALU.mult))
                for h in range(2):
                    c.do(dve.bn_stats(st2[:, h, :], fy[:, h * HALF:(h + 1) * HALF]), wait=h == 1)
                c.do(dve.bn_aggr(mv2[:, 4:6], st2[:, :, :].rearrange("p a s -> p (a s)")))
                c.do(dve.tensor_scalar(mv2[:, 6:7], mv2[:, 5:6], LN_EPS, None, ALU.add), wait=False)
                c.do(dve.scalar_tensor_tensor(out=fx, in0=fy, scalar=mv2[:, 4:5], in1=gb[:, :],
                                              op0=ALU.subtract, op1=ALU.mult))
                dve.wait_ge(s_rstd2, 2 * (b * TT + t) + 2)
                c.do(dve.scalar_tensor_tensor(out=fx, in0=fx, scalar=mv2[:, 7:8], in1=bb[:, :],
                                              op0=ALU.mult, op1=ALU.add), wait=False)
                assert c.n == 11

            def ffn_route(b, t):
                k = b * TT + t
                c = Chain(dve, s_f, k * NF)
                c.n = 11
                dve.wait_ge(s_fpool, k * 3 + 1)
                c.do(dve.tensor_reduce(ts[:, :], fs.rearrange("p (t j) -> p t j", j=SLICE), AX.X, ALU.add))
                c.do(dve.tensor_reduce(cs[:, :], ts[:, :].rearrange("p (c t) -> p c t", c=CLUSTERS),
                                       AX.X, ALU.add))
                wide = cs[:, :].rearrange("p (c a) -> p c a", a=1)\
                    .broadcast_to([P, CLUSTERS, NT // CLUSTERS])
                c.do(dve.scalar_tensor_tensor(out=key[:, :].rearrange("p (c t) -> p c t", c=CLUSTERS),
                                              in0=wide, scalar=4096.0,
                                              in1=tie[:, :].rearrange("p (c t) -> p c t", c=CLUSTERS),
                                              op0=ALU.mult, op1=ALU.add))
                c.do(dve.scalar_tensor_tensor(out=key[:, :], in0=ts[:, :], scalar=float(NT // CLUSTERS),
                                              in1=key[:, :], op0=ALU.mult, op1=ALU.add))
                c.do(dve.tensor_reduce(kmax[:, :], key[:, :], AX.X, ALU.max))
                c.do(dve.tensor_scalar(oh[:, k, :], key[:, :], kmax[:, 0:1], None, ALU.is_equal), wait=False)
                assert c.n == 17

            def ffn_slice(b, t):
                k = b * TT + t
                c = Chain(dve, s_f, k * NF)
                c.n = 17
                wait_apart(dve, s_fpool, k * 3 + 3)
                c.do(dve.tensor_reduce(xsl[:, k, :], fsel.rearrange("p (t j) -> p j t", j=SLICE), AX.X, ALU.add))
                c.do(dve.tensor_reduce(mm[:, 0:1], xsl[:, k, :], AX.X, ALU.min), wait=False)
                c.do(dve.tensor_reduce(mm[:, 1:2], xsl[:, k, :], AX.X, ALU.max), wait=False)
                c.do(dve.tensor_scalar(cand[:, 2, :], oh[:, k, :], 1.0, -BIG, ALU.subtract, ALU.mult))
                c.do(dve.scalar_tensor_tensor(out=cand[:, 0, :], in0=oh[:, k, :], scalar=mm[:, 0:1],
                                              in1=cand[:, 2, :], op0=ALU.mult, op1=ALU.add), wait=False)
                c.do(dve.scalar_tensor_tensor(out=cand[:, 1, :], in0=oh[:, k, :], scalar=mm[:, 1:2],
                                              in1=cand[:, 2, :], op0=ALU.mult, op1=ALU.subtract))
                c.do(dve.tensor_tensor(run[:, 0, :], run[:, 0, :], cand[:, 0, :], ALU.min), wait=False)
                c.do(dve.tensor_tensor(run[:, 1, :], run[:, 1, :], cand[:, 1, :], ALU.max))
                assert c.n == NF

            def prologue(b):
                rope_k(b)
                rope_q(b, 0)
                q_lo(b, 0, 0)
                k_lo(b, 0, 0)

            for t in range(TT):
                norm_x(0, t)
            dve.wait_ge(s_const, 64)
            dve.wait_ge(s_ssb, 16)
            dve.wait_ge(s_setup, 10)
            prologue(0)

            def body(b, first, last):
                def head(q, i, q0, nxt=None):
                    head0 = q0 and i == 0
                    adds = not q0 and i == 0
                    mask_scores(b, q, i, 0, head0)
                    mask_scores(b, q, i, 1, head0)
                    divide(b, q, i, 0)
                    divide(b, q, i, 1)
                    if nxt is not None:
                        rope_q(b, nxt)
                    mask_scores(b, q, i, 2, head0)
                    if adds:
                        add_out(b, q - 1, 0, True)
                        add_out(b, q - 1, 1, False)
                    if nxt is not None:
                        q_lo(b, nxt, 0)
                    elif i < HQ - 1:
                        q_lo(b, q, i + 1)
                    divide(b, q, i, 2)
                    mask_scores(b, q, i, 3, head0)
                    if q0 and not first:
                        ffn_norms(b - 1, FFN_AT[i][0])
                    if adds:
                        add_out(b, q - 1, 2, False)
                        add_out(b, q - 1, 3, False)
                    if nxt is not None:
                        k_lo(b, nxt, 0)
                    elif i < HQ - 1:
                        k_lo(b, q, i + 1)
                    divide(b, q, i, 3)
                    if adds:
                        for w in range(4, 8):
                            add_out(b, q - 1, w, False)
                    if q0 and not first:
                        for t in FFN_AT[i]:
                            if t != FFN_AT[i][0]:
                                ffn_norms(b - 1, t)
                            ffn_route(b - 1, t)
                            ffn_slice(b - 1, t)

                for i in range(HQ - 1):
                    head(0, i, True)
                with dve.Fori(1, NQ) as q:
                    head(q - 1, HQ - 1, False, q)
                    for i in range(HQ - 1):
                        head(q, i, False)
                head(NQ - 1, HQ - 1, False)
                if not last:
                    norm_x(b + 1, 0)
                    norm_x(b + 1, 1)
                for w in range(0, 4):
                    add_out(b, NQ - 1, w, False)
                if not last:
                    norm_x(b + 1, 2)
                    norm_x(b + 1, 3)
                for w in range(4, 8):
                    add_out(b, NQ - 1, w, False)
                if not last:
                    prologue(b + 1)

            batches(dve, body)
            for t in range(TT):
                ffn_norms(B - 1, t)
                ffn_route(B - 1, t)
                ffn_slice(B - 1, t)

            dve.wait_ge(s_g, 2)
            dve.wait_ge(s_tab, 48)
            c = Chain(dve, s_gv, 0)
            c.do(dve.tensor_reduce(tab[:, 0:1], psA[0:NT, 0:P], AX.X, ALU.min), wait=False)
            c.do(dve.tensor_reduce(tab[:, 1:2], psB[0:NT, 0:P], AX.X, ALU.max), wait=False)
            dve.wait_ge(s_g, 3 + NTOK // 4)
            wide = [NTOK, SLICE]

            def per_tile(v):
                return v.rearrange("p (k a) -> p k a", a=1).broadcast_to([P, NTOK, SLICE])

            c.do(dve.tensor_copy(fin, psC[:, 0:NTOK * 4].rearrange("p (k c) -> p k c", c=4)))
            c.do(dve.tensor_tensor(dena, fin[:, :, 1], fin[:, :, 0], ALU.subtract))
            c.do(dve.tensor_scalar(dena, dena, 1e-8, None, ALU.add))
            c.do(dve.tensor_tensor(fu, xsl[:, :, :], per_tile(fin[:, :, 0]), ALU.subtract))
            c.do(dve.reciprocal(dena, dena))
            c.do(dve.tensor_tensor(fu, fu, per_tile(dena), ALU.mult))
            c.do(dve.tensor_scalar(fu, fu, 0.0, 1.0 - 1e-6, ALU.max, ALU.min))
            c.do(dve.tensor_scalar(fu, fu, float(GRID), None, ALU.mult))
            c.do(dve.tensor_scalar(fg, fu, ROUND, None, ALU.add))
            c.do(dve.tensor_scalar(fg, fg, ROUND, None, ALU.subtract))
            c.do(dve.tensor_tensor(fl, fg, fu, ALU.is_gt))
            c.do(dve.tensor_tensor(fg, fg, fl, ALU.subtract))
            c.do(dve.tensor_tensor(fl, fu, fg, ALU.subtract))
            dve.wait_ge(s_iota, 6)
            c.do(dve.tensor_tensor(idxf, fin[:, :, 3], tokb, ALU.add))
            c.do(dve.tensor_copy(idxi, idxf))
            n0 = c.n
            for g in range(2):
                eq = eqb.rearrange("p (k g) -> p k g", g=GRID)
                cells = fg[:, g * 16:(g + 1) * 16, :].rearrange("p k (j a) -> p (k j) a", a=1)
                ramp = gramp.rearrange("p (a g) -> p a g", a=1).broadcast_to([P, 16 * SLICE, GRID])
                c.do(dve.tensor_tensor(eq, cells.broadcast_to([P, 16 * SLICE, GRID]), ramp, ALU.is_equal))
                for kk in range(16):
                    k = g * 16 + kk
                    ps = [psA, psB, psD, psS[0]][k % 4]
                    dve.wait_ge(s_gb, k + 1)
                    e = eqb.rearrange("p (k j g) -> p k j g", j=SLICE, g=GRID)[:, kk, :, :]
                    pr = prod[:, k % 2, :].rearrange("p (a j g) -> p a j g", a=2, g=GRID)
                    for a in range(2):
                        ins = dve.tensor_tensor(pr[:, a], ps[:, a * 256:(a + 1) * 256]
                                                .rearrange("p (j g) -> p j g", g=GRID), e, ALU.mult)
                        if a == 0:
                            ins.then_inc(s_gv, 1)
                            c.n += 1
                        else:
                            ins.then_inc(s_gf, 1)
                    dve.wait_ge(s_gf, k + 1)
                    dve.wait_ge(s_gv, c.n)
                    c.do(dve.tensor_reduce(bsel[:, k * 32:(k + 1) * 32],
                                           prod[:, k % 2, :].rearrange("p (m g) -> p m g", g=GRID),
                                           AX.X, ALU.add), wait=False)
                dve.wait_ge(s_gv, c.n)
            bs = bsel.rearrange("p (k a j) -> p k a j", a=2, j=SLICE)
            c.do(dve.tensor_tensor(fd, bs[:, :, 1, :], fl, ALU.mult))
            c.do(dve.tensor_tensor(fd, fd, bs[:, :, 0, :], ALU.add))
            c.do(dve.tensor_tensor(fd, fd, per_tile(fin[:, :, 2]), ALU.mult), wait=False)
            assert c.n == NG, c.n

        @block.tensor
        def _(pe):
            def turn_stage(b, j, ctx_side):
                jj = j + (TT if ctx_side else 0)
                if ctx_side:
                    pe.wait_ge(s_xs[j % 2], 16 * (b * TT + 2 + j // 2 + 1))
                else:
                    pe.wait_ge(s_ln, (b * TT + j + 1) * NL)
                for half in range(2):
                    k = 2 * jj + half
                    if not (isinstance(b, int) and b == 0 and k < 2):
                        pe.wait_ge(freeT, b * TN + k - 1)
                    for c in range(4):
                        blk = 4 * half + c
                        mm_ = pe.transpose(psT[k % 2][:, c * P:(c + 1) * P],
                                           xs[:, j % 2, blk * P:(blk + 1) * P], ident[:, :])
                    mm_.then_inc(fullT, 1)

            def wait_free(free, n):
                if not (isinstance(n, int) and n == 0):
                    pe.wait_ge(free, n)

            def down(ps, full, free, n, col):
                wait_free(free, n)
                for c in range(DB):
                    mm_ = pe.matmul(ps[:, :], wD[:, c, col * P:(col + 1) * P], xT[:, c, :],
                                    start=c == 0, stop=c == DB - 1)
                mm_.then_inc(full, 1)

            def rope_keys(b):
                for ps, full, free, n, w in ((psA, fullA, freeA, b * AN + 3, wkra),
                                             (psB, fullB, freeB, b * BN + 2, wkrb)):
                    wait_free(free, n)
                    for c in range(CB):
                        mm_ = pe.matmul(ps[:, :], w[:, c].rearrange("p a r -> p (a r)"), kvc[:, c, :],
                                        start=c == 0, stop=c == CB - 1)
                    mm_.then_inc(full, 1)

            def rope_queries(b, q):
                pe.wait_ge(s_sorted, b * NQ + q + 1)
                for ps, full, free, n, j in ((psA, fullA, freeA, pos_a(b, q, 0), 0),
                                             (psB, fullB, freeB, pos_b(b, q, 0), 1)):
                    wait_free(free, n)
                    for c in range(QB):
                        mm_ = pe.matmul(ps[:, :], wqp[:, c, j, :], qc[:, c, :],
                                        start=c == 0, stop=c == QB - 1)
                    mm_.then_inc(full, 1)

            def queries(b, q, i):
                pe.wait_ge(s_wuq[i % 2], 16 * (b * (H // 2) + q * (HQ // 2) + i // 2 + 1))
                wait_free(freeA, pos_a(b, q, 1 + i))
                for c in range(QB):
                    mm_ = pe.matmul(psA[:, :], wuq[:, i % 2, c, :], qc[:, c, :], start=c == 0, stop=c == QB - 1)
                mm_.then_inc(fullA, 1)

            def keys(b, q, i):
                pe.wait_ge(s_wuk[i % 2], 16 * (b * (H // 2) + q * (HQ // 2) + i // 2 + 1))
                wait_free(freeB, pos_b(b, q, 1 + i))
                for c in range(CB):
                    mm_ = pe.matmul(psB[:, :], wuk[:, i % 2, c, :], kvc[:, c, :], start=c == 0, stop=c == CB - 1)
                mm_.then_inc(fullB, 1)

            def values(b, q):
                pe.wait_ge(s_wuv, 16 * (b * NQ + q + 1))
                for kt in range(TT):
                    ps, full, free, n = ((psC, fullC, freeC, pos_c(b, q, kt // 2)) if kt % 2 == 0 else
                                         (psD, fullD, freeD, pos_d(b, q, kt // 2)))
                    wait_free(free, n)
                    for c in range(CB):
                        mm_ = pe.matmul(ps[:, :], kvc[:, c, kt * P:(kt + 1) * P], wuv[:, c, :],
                                        start=c == 0, stop=c == CB - 1)
                    mm_.then_inc(full, 1)

            def scores(b, q, i, qt, very_first):
                n = tile_no(b, q, i, qt)
                if qt == 0:
                    pe.wait_ge(freeA, pos_a(b, q, 1 + i) + 1)
                    pe.wait_ge(freeB, pos_b(b, q, 1 + i) + 1)
                    pe.wait_ge(s_stack[i], 64 * (b * NQ + q + 1))
                    if i == 0 and isinstance(q, int):
                        pe.wait_ge(s_rhi, b * (NQ + 1) + 1)
                        pe.wait_ge(s_rlo, b * (NQ + 1) + 1)
                if not (very_first and qt < 2):
                    pe.wait_ge(s_sm, n - 1)
                cols = slice(qt * P, (qt + 1) * P)
                ps, s = psS[qt % 2][:, :], i % 2
                pe.matmul(ps, qh[:, s, cols], kh[:, s, :], start=True, stop=False)
                pe.matmul(ps, qh[:, s, cols], kl[:, s, :], start=False, stop=False)
                pe.matmul(ps, ql[:, s, cols], kh[:, s, :], start=False, stop=False)
                pe.matmul(ps, stack[:, i, cols], krh[:, :], start=False, stop=False)
                pe.matmul(ps, stack[0:R, i, cols], krl[:, :], start=False, stop=True).then_inc(s_S, 1)

            def turn_probs(b, q, i, qt):
                pe.wait_ge(s_prob, tile_no(b, q, i, qt) + 1)
                pe.wait_ge(freeT, pos_t(b, q, i, qt) - 1)
                for c in range(TT):
                    mm_ = pe.transpose(psT[qt % 2][:, c * P:(c + 1) * P], E[:, qt, c * P:(c + 1) * P], ident[:, :])
                mm_.then_inc(fullT, 1)

            def attend(b, q, i):
                pe.wait_ge(freeT, pos_t(b, q, i, TT - 1) + 1)
                if i == 0:
                    pe.wait_ge(freeC, pos_c(b, q, 2))
                pe.wait_ge(freeD, pos_d(b, q, 2 + i))
                for kt in range(TT):
                    mm_ = pe.matmul(psD[:, :], V[:, kt, i * P:(i + 1) * P], PT[:, kt, :],
                                    start=kt == 0, stop=kt == TT - 1)
                mm_.then_inc(fullD, 1)

            def out_proj(b, q, w):
                half, t = w // TT, w % TT
                if w % 2 == 0:
                    ps, full, free, n = psC, fullC, freeC, pos_c(b, q, 2 + w // 2)
                else:
                    ps, full, free, n = psD, fullD, freeD, pos_d(b, q, 6 + w // 2)
                if t == 0:
                    pe.wait_ge(s_wo[half], 16 * (b * NQ + q + 1))
                if w == 0:
                    pe.wait_ge(freeD, pos_d(b, q, 6))
                pe.wait_ge(free, n)
                for i in range(HQ):
                    mm_ = pe.matmul(ps[:, :], attn[:, i, t * P:(t + 1) * P], wo[:, half, i, :],
                                    start=i == 0, stop=i == HQ - 1)
                mm_.then_inc(full, 1)

            def down_q(b):
                pe.wait_ge(s_wd, 32 * b + 16)
                pe.wait_ge(freeT, b * TN + 2 * TT)
                down(psA, fullA, freeA, b * AN, 0)
                down(psB, fullB, freeB, b * BN, 1)
                down(psA, fullA, freeA, b * AN + 1, 2)

            def down_kv(b):
                pe.wait_ge(s_wd, 32 * b + 32)
                pe.wait_ge(freeT, b * TN + 4 * TT)
                down(psB, fullB, freeB, b * BN + 1, 0)
                down(psA, fullA, freeA, b * AN + 2, 1)

            def into_heads(b):
                pe.wait_ge(freeA, b * AN + 3)
                pe.wait_ge(freeB, b * BN + 2)
                rope_keys(b)
                rope_queries(b, 0)
                queries(b, 0, 0)
                keys(b, 0, 0)

            pe.wait_ge(s_setup, 3)
            for j in range(TT):
                turn_stage(0, j, False)
            down_q(0)
            for j in range(TT):
                turn_stage(0, j, True)
            down_kv(0)
            pe.wait_ge(s_setv, 7)
            into_heads(0)

            def body(b, first, last):
                def head(q, i, q0, nxt=None):
                    vf = first and q0 and i == 0
                    outs = not q0 and i == 0
                    scores(b, q, i, 0, vf)
                    scores(b, q, i, 1, vf)
                    if i > 0:
                        attend(b, q, i - 1)
                    elif not q0:
                        attend(b, q - 1, HQ - 1)
                    if nxt is not None:
                        rope_queries(b, nxt)
                    turn_probs(b, q, i, 0)
                    scores(b, q, i, 2, vf)
                    if outs:
                        out_proj(b, q - 1, 0)
                        out_proj(b, q - 1, 1)
                    if nxt is not None:
                        queries(b, nxt, 0)
                    elif i < HQ - 1:
                        queries(b, q, i + 1)
                    turn_probs(b, q, i, 1)
                    scores(b, q, i, 3, vf)
                    if outs:
                        out_proj(b, q - 1, 2)
                        out_proj(b, q - 1, 3)
                    if nxt is not None:
                        keys(b, nxt, 0)
                    elif i < HQ - 1:
                        keys(b, q, i + 1)
                    turn_probs(b, q, i, 2)
                    if outs:
                        for w in range(4, 8):
                            out_proj(b, q - 1, w)
                    turn_probs(b, q, i, 3)
                    if outs:
                        values(b, q)

                values(b, 0)
                for i in range(HQ - 1):
                    head(0, i, True)
                with pe.Fori(1, NQ) as q:
                    head(q - 1, HQ - 1, False, q)
                    for i in range(HQ - 1):
                        head(q, i, False)
                head(NQ - 1, HQ - 1, False)
                attend(b, NQ - 1, HQ - 1)
                for w in range(4):
                    out_proj(b, NQ - 1, w)
                if not last:
                    for j in range(TT):
                        turn_stage(b + 1, j, False)
                    down_q(b + 1)
                for w in range(4, 8):
                    out_proj(b, NQ - 1, w)
                if not last:
                    for j in range(TT):
                        turn_stage(b + 1, j, True)
                    down_kv(b + 1)
                    into_heads(b + 1)

            batches(pe, body)

            pe.wait_ge(s_f, NTOK * NF)
            pe.wait_ge(freeA, B * AN)
            pe.wait_ge(freeB, B * BN)
            pe.transpose(psA[0:NT, 0:P], run[:, 0, :], ident[:, :]).then_inc(s_g, 1)
            pe.transpose(psB[0:NT, 0:P], run[:, 1, :], ident[:, :]).then_inc(s_g, 1)
            for g in range(NTOK // 4):
                if g >= 2:
                    pe.wait_ge(s_ge, g - 1)
                for k in range(4):
                    mm_ = pe.transpose(psTb[g % 2][0:NT, k * P:(k + 1) * P], oh[:, 4 * g + k, :], identb[:, :])
                mm_.then_inc(s_g, 1)
            pe.wait_ge(s_gv, 2)
            pe.wait_ge(s_iota, 6)
            pe.wait_ge(s_tab, 48)
            pe.wait_ge(s_ge, NTOK // 4)
            pe.wait_ge(freeC, B * CN)
            for k in range(NTOK):
                mm_ = pe.matmul(psC[:, k * 4:k * 4 + 4], ohT[:, k * P:(k + 1) * P], tab[:, :], start=True, stop=True)
            mm_.then_inc(s_g, 1)
            pe.wait_ge(freeD, B * DN)
            for k in range(NTOK):
                ps = [psA, psB, psD, psS[0]][k % 4]
                if k >= 4:
                    pe.wait_ge(s_gf, k - 3)
                pe.matmul(ps[:, :], ohT[:, k * P:(k + 1) * P], spl.rearrange("p a n -> p (a n)"),
                          start=True, stop=True).then_inc(s_gb, 1)


FFN_AT = [[0], [1], [2, 3]]
NM = 2 + 4 * 4
NR = 1 + 4 * 4
NG = 2 + 15 + 2 + 32 * 2 + 3


def wait_apart(eng, sem, n):
    eng.wait_ge(sem, n)
    if not isinstance(n, int):
        eng.sem_inc(AFTER[0], 1)


AFTER = []


class Chain:

    def __init__(self, eng, sem, base):
        self.eng, self.sem, self.base, self.n = eng, sem, base, 0

    def do(self, ins, wait=True):
        self.n += 1
        ins.then_inc(self.sem, 1)
        if wait:
            wait_apart(self.eng, self.sem, self.base + self.n)


_INS = ['x', 'ctx_2048', 'itok_BxS_0_1023', 'L0_xattn_W_kvc', 'L0_xattn_W_dq', 'L0_xattn_W_uq', 'L0_xattn_W_qr',
        'L0_xattn_W_uk', 'L0_xattn_W_kr', 'L0_xattn_W_uv', 'L0_xattn_W_o', 'L0_ffn_ln_gamma', 'L0_ffn_ln_beta',
        'L0_ffn_spline_bases', 'L0_ffn_spline_slopes', 'L0_ffn_output_scale']
_OUTS = [((8, 512, 1024), 'float32')]


def _rotary_tables(length, half):
    import numpy as _np
    steps = _np.arange(half, dtype=_np.float32) / _np.float32(half)
    inv = (_np.float32(1.0) / _np.power(_np.float32(10000.0), steps)).astype(_np.float32)
    ang = (_np.arange(length, dtype=_np.float32)[:, None] * inv).astype(_np.float64)
    reps = 128 // half
    return [_np.ascontiguousarray(_np.tile(f(ang).astype(_np.float32).T, (reps, 1))) for f in (_np.cos, _np.sin)]


def kernel(**inputs):
    import numpy as _np
    import concourse.bacc as _bacc
    from concourse import mybir as _mybir
    from concourse.bass_utils import run_bass_kernel_spmd as _run

    nc = _bacc.Bacc("TRN2", target_bir_lowering=False, num_devices=1)
    arrays, args = {}, []
    cos_t, sin_t = _rotary_tables(512, 32)
    data = [(name, _np.ascontiguousarray(inputs[name])) for name in _INS] + [('cos_t', cos_t), ('sin_t', sin_t)]
    for name, a in data:
        arrays[f"in_{name}_dram"] = a
        args.append(nc.dram_tensor(f"in_{name}_dram", a.shape, _mybir.dt.from_np(a.dtype), kind="ExternalInput").ap())
    for i, (shape, dtype) in enumerate(_OUTS):
        dt = _mybir.dt.from_np(_np.dtype(dtype))
        args.append(nc.dram_tensor(f"out_{i}_dram", shape, dt, kind="ExternalOutput").ap())
    xattn_ffn_kernel(nc, *args)
    r = _run(nc, [arrays], core_ids=[0])
    got = tuple(r.results[0][f"out_{i}_dram"] for i in range(len(_OUTS)))
    return got[0]
```

```python
from contextlib import ExitStack

import concourse.bass as bass
from concourse import mybir

F32 = mybir.dt.float32
F32R = mybir.dt.float32r
BF16 = mybir.dt.bfloat16
I32 = mybir.dt.int32
U32 = mybir.dt.uint32
ALU = mybir.AluOpType
ACT = mybir.ActivationFunctionType
AX = mybir.AxisListType

P = 128
HALF = 512
LOOKBACK = 8
NEG = -1.0e30
BIG = 3.0e38
LN_EPS = 1e-5
ROUND = 8388608.0
GRID = 16
SLICE = 16
NT = 64
CLUSTERS = 8


def xattn_ffn_kernel(nc, x, ctx_in, seg, w_kvc, w_dq, w_uq, w_qr, w_uk, w_kr, w_uv, w_o,
                     gamma, beta, bases, slopes, oscale, cos_t, sin_t, out):
    B, T, D = x.shape
    KVC, QC = w_kvc.shape[1], w_dq.shape[1]
    R = w_kr.shape[1]
    HR = R // 2
    H = w_uq.shape[1] // P
    TT = T // P
    DB = D // P
    CB, QB = KVC // P, QC // P
    HQ = 4
    NQ = H // HQ
    SCALE = 1.0 / float(P + R) ** 0.5
    NTOK = B * T // P
    assert T == HALF and HQ * HR == P and 2 * R == P and D == 2 * HALF and NT * SLICE == D

    A0, AQ = 4, 1 + HQ
    B0, BQ = 3, 1 + HQ
    CQ, DQ = 6, 10
    AN, BN, CN, DN = A0 + NQ * AQ, B0 + NQ * BQ, NQ * CQ, NQ * DQ
    T0, TN = 4 * TT, 4 * TT + 2 * H * TT

    def pos_a(b, q, k):
        return b * AN + A0 + q * AQ + k

    def pos_b(b, q, k):
        return b * BN + B0 + q * BQ + k

    def pos_c(b, q, k):
        return b * CN + q * CQ + k

    def pos_d(b, q, k):
        return b * DN + q * DQ + k

    def pos_t(b, q, i, qt):
        return b * TN + T0 + 2 * ((q * HQ + i) * TT + qt)

    def tile_no(b, q, i, qt):
        return b * H * TT + (q * HQ + i) * TT + qt

    NF = 25
    NL = 5

    with ExitStack() as ctx:
        def sb(name, shape, dt=F32):
            return ctx.enter_context(nc.sbuf_tensor(name, shape, dt))

        def bank(name, dt=F32):
            return ctx.enter_context(nc.psum_tensor(name, [P, HALF], dt))

        def sem(name):
            return ctx.enter_context(nc.semaphore(name))

        psS = [bank("psS0"), bank("psS1")]
        psT = [bank("psT0"), bank("psT1")]
        psA, psB, psC, psD = bank("psA"), bank("psB"), bank("psC"), bank("psD")

        wD = sb("w_down", [P, DB, QC])
        wuq = sb("w_uq_ring", [P, 2, QB, P])
        wuk = sb("w_uk_ring", [P, 2, CB, P])
        wqr = sb("w_qr_quad", [P, QB, HQ * R])
        wqp = sb("w_qr_sorted", [P, QB, 2, HQ * HR])
        wuv = sb("w_uv_quad", [P, CB, HQ * P])
        wo = sb("w_o_quad", [P, 2, HQ, HALF])
        wkra = sb("w_kr_a", [P, CB, 2, R])
        wkrb = sb("w_kr_b", [P, CB, 2, R])
        xs = sb("x_stage", [P, 2, D])
        xT = sb("xT", [P, DB, T])
        qc = sb("q_c", [P, QB, T])
        kvc = sb("kv_c", [P, CB, T])
        rt = sb("rope_terms", [P, 2, T])
        rr = sb("rope_out", [P, 2, T])
        rh = sb("rope_hi", [P, 2, T], F32R)
        rl = sb("rope_lo", [P, 2, T], F32R)
        stack = sb("q_rope_stack", [P, HQ, T], F32R)
        krh = sb("k_rope_hi", [P, T], F32R)
        krl = sb("k_rope_lo", [R, T], F32R)
        V = [sb("values_hi", [P, TT, HQ * P], F32R), sb("values_lo", [P, TT, HQ * P], F32R)]
        qh, ql = sb("q_hi", [P, T], F32R), sb("q_lo", [P, T], F32R)
        kh, kl = sb("k_hi", [P, T], F32R), sb("k_lo", [P, T], F32R)
        E = sb("exps_ring", [P, 2, T])
        Ph = [sb("probs_hi", [P, 2, T], F32R), sb("probs_lo", [P, 2, T], F32R)]
        PT = [sb("probsT_hi", [P, TT, T], F32R), sb("probsT_lo", [P, TT, T], F32R)]
        mask = sb("mask", [P, TT, T], BF16)
        attn = sb("attn", [P, HQ, T])
        acc = sb("acc", [P, TT, D])
        cosT, sinT = sb("cosT", [P, T]), sb("sinT", [P, T])
        identr = sb("ident", [P, P], F32R)
        ident = identr[:, :].bitcast(F32)
        identb = sb("ident_b", [P, P], BF16)
        kidx = sb("key_index", [P, T], mybir.dt.float16)
        mtmp = rl[:, :, :].bitcast(F32)
        segi = sb("seg_int", [P, TT], I32)
        segf = sb("seg_f", [P, 2, TT])
        nhalf = sb("minus_half", [P, 1])
        mx = sb("neg_max", [P, 2, TT])
        rs = sb("row_sum", [P, 2, TT])
        ri = sb("row_sum_inverse", [P, 2, TT])
        st = sb("ln_stats", [P, 2, 6])
        mv = sb("ln_mean_var", [P, 4])
        st2 = sb("ffn_stats", [P, 2, 6])
        mv2 = sb("ffn_mean_var", [P, 8])
        gb = sb("gamma_b", [P, D])
        bb = sb("beta_b", [P, D])
        ssb = sb("slope_sign_b", [P, D], BF16)
        sl = xT[:, 0, 0:256]
        tie = sb("tie_order", [P, NT])
        ts = sb("tile_scores", [P, NT])
        cs = sb("cluster_scores", [P, CLUSTERS])
        key = sb("tile_key", [P, NT])
        kmax = sb("key_max", [P, 1])
        oh = sb("onehot", [P, NT], BF16)
        xsl = sb("x_slice", [P, NTOK, SLICE])
        mm = sb("slice_min_max", [P, 2])
        cand = sb("candidates", [P, 3, NT])
        run = sb("run_min_max", [P, 2, NT])
        fy = xT[:, 0:2, :].rearrange("p a n -> p (a n)")
        fx = xT[:, 2:4, :].rearrange("p a n -> p (a n)")
        fs = xT[:, 4:6, :].rearrange("p a n -> p (a n)")
        fsel = xT[:, 6:8, :].rearrange("p a n -> p (a n)")
        tmi = xT[:, 7, 0:T].bitcast(I32)
        idt = xT[:, 6, 0:P]
        wkr = xT[:, 5, 0:CB * R].rearrange("p (c r) -> p c r", c=CB)
        ssf = xT[:, 2:4, :].rearrange("p a n -> p (a n)")
        sgn64 = xT[:, 1, 0:SLICE]
        ssum = xT[:, 1, SLICE:2 * SLICE]

        AFTER[:] = [sem("waits_apart")]
        s_const = sem("constants_in")
        s_wkr = sem("w_kr_in_sem")
        s_sl = sem("slopes_in")
        s_iota = sem("ramps")
        s_setup = sem("setup_pool")
        s_setv = sem("setup_vector")
        s_seta = sem("setup_scalar")
        s_ssb = sem("slope_sign_in")
        s_ssd = sem("slope_sign_dram")
        s_wd = sem("w_down_in")
        s_wuq, s_wuk = [sem("w_uq_in0"), sem("w_uq_in1")], [sem("w_uk_in0"), sem("w_uk_in1")]
        s_sorted = sem("w_qr_sorted_done")
        s_wqr, s_wuv = sem("w_qr_in"), sem("w_uv_in")
        s_wo = [sem("w_o_in0"), sem("w_o_in1")]
        s_xs = [sem("x_in0"), sem("x_in1")]
        s_seg = sem("seg_in")
        s_rstd, s_rstd2 = sem("ln_rstd"), sem("ffn_rstd")
        s_rinv = sem("row_sum_inverse_done")
        s_ln = sem("ln_steps")
        s_mask = sem("mask_steps")
        s_acc = sem("acc_in")
        fullA, fullB, fullC, fullD = sem("fullA"), sem("fullB"), sem("fullC"), sem("fullD")
        freeA, freeB, freeC, freeD = sem("freeA"), sem("freeB"), sem("freeC"), sem("freeD")
        fullT, freeT = sem("fullT"), sem("freeT")
        s_S, s_sm, s_exp, s_prob = sem("scores"), sem("scores_masked"), sem("exps"), sem("probs_done")
        s_vhi = sem("v_hi_done")
        s_qhi, s_khi = sem("q_hi_done"), sem("k_hi_done")
        s_rope, s_rhi, s_rlo = sem("rope_steps"), sem("rope_hi_done"), sem("rope_lo_done")
        s_stack = [sem(f"stack_in{i}") for i in range(HQ)]
        s_f = sem("ffn_steps")
        s_sign, s_fpool = sem("ffn_sign"), sem("ffn_pool")
        s_x1, s_x1in = sem("x1_out"), sem("x1_in")
        s_oh, s_ohin = sem("onehot_out"), sem("onehot_in")
        s_plo = sem("probs_lo_done")
        s_z = sem("z_out")
        s_tab = sem("tables_in")
        s_g = sem("gather_pe")
        s_ge = sem("gather_scalar")
        s_gv = sem("gather_vector")
        s_gf = sem("spline_row_used")
        s_gb = sem("spline_row")
        s_sc = sem("scattered")

        x_t = x.rearrange("b (t p) d -> b t p d", p=P)
        c_t = ctx_in.rearrange("b (t p) d -> b t p d", p=P)
        o_t = out.rearrange("b (t p) d -> b t p d", p=P)
        seg_v = seg.rearrange("b (t p) -> b p t", p=P)
        wdq_v = w_dq.rearrange("(c p) n -> p c n", p=P)
        wkvc_v = w_kvc.rearrange("(c p) n -> p c n", p=P)
        wuq_v = w_uq.rearrange("(c p) n -> p c n", p=P)
        wqr_v = w_qr.rearrange("(c p) n -> p c n", p=P)
        wuk_v = w_uk.rearrange("(c p) n -> p c n", p=P)
        wkr_v = w_kr.rearrange("(c p) n -> p c n", p=P)
        wuv_v = w_uv.rearrange("(c p) n -> p c n", p=P)
        wo_v = w_o.rearrange("(h p) n -> p h n", p=P)
        oh_dram = nc.dram_tensor("onehot_scratch", [NTOK, P, NT], BF16).ap()
        ss_dram = nc.dram_tensor("slope_sign_scratch", [NT, SLICE], F32).ap()

        spl = qc[0:NT, 0:1, :]
        tab = kvc[0:NT, 0, 0:4]
        prod = rt[:, :, :]
        ohT = acc[0:NT, :, :].rearrange("p t n -> p (t n)")
        eqb = xT[:, :, :].rearrange("p a n -> p (a n)")
        bsel = wD[:, 0:4, 0:256]
        wideb = wuv[:, :, :].rearrange("p c n -> p (c n)")
        ohall = xs[:, 0, :].bitcast(BF16).rearrange("p (k t) -> p k t", t=NT)
        fin = qc[:, 2, 0:NTOK * 4].rearrange("p (k c) -> p k c", c=4)
        fu = attn[:, 0, :].rearrange("p (k j) -> p k j", j=SLICE)
        fl = attn[:, 1, :].rearrange("p (k j) -> p k j", j=SLICE)
        fg = attn[:, 2, :].rearrange("p (k j) -> p k j", j=SLICE)
        fd = attn[:, 3, :].rearrange("p (k j) -> p k j", j=SLICE)
        gramp = kvc[:, 1, 0:GRID]
        tokb = kvc[:, 1, 32:32 + NTOK]
        idxf = kvc[:, 1, 96:96 + NTOK]
        dena = kvc[:, 1, 160:160 + NTOK]
        idxi = kvc[:, 1, 256:256 + NTOK].bitcast(I32)
        rampi = kvc[:, 1, 320:384].bitcast(I32)

        psTb = [p[:, :].bitcast(BF16) for p in psT]

        def onehot_wide():
            return oh[:, :].rearrange("p (t a) -> p t a", a=1).broadcast_to([P, NT, SLICE])

        def batches(eng, body):
            body(0, True, False)
            with eng.Fori(1, B - 1) as b:
                body(b, False, False)
            body(B - 1, False, True)

        block = ctx.enter_context(nc.Block())

        @block.sync
        def _(sp):
            def load_dq(b):
                if not (isinstance(b, int) and b == 0):
                    wait_apart(sp, fullA, (b - 1) * AN + 3)
                    wait_apart(sp, fullB, (b - 1) * BN + 2)
                sp.dma_start(wD[:, :, :], wdq_v).then_inc(s_wd, 16)

            def load_kvc(b):
                wait_apart(sp, fullA, b * AN + 2)
                wait_apart(sp, fullB, b * BN + 1)
                sp.dma_start(wD[:, :, 0:KVC], wkvc_v).then_inc(s_wd, 16)

            def load_xs(b, j):
                if j >= 2:
                    wait_apart(sp, fullT, b * TN + 2 * (j - 2) + 2)
                elif not (isinstance(b, int) and b == 0):
                    wait_apart(sp, fullT, (b - 1) * TN + 2 * (j + 6) + 2)
                src = x_t[b, j] if j < TT else c_t[b, j - TT]
                sp.dma_start(xs[:, j % 2, :], src).then_inc(s_xs[j % 2], 16)

            def load_uq(h, slot):
                sp.dma_start(wuq[:, slot], wuq_v[:, :, bass.ds(h * P, P)]).then_inc(s_wuq[slot], 16)

            def load_uk(h, slot):
                sp.dma_start(wuk[:, slot], wuk_v[:, :, bass.ds(h * P, P)]).then_inc(s_wuk[slot], 16)

            def load_qr(q):
                sp.dma_start(wqr[:, :, :], wqr_v[:, :, bass.ds(q * HQ * R, HQ * R)]).then_inc(s_wqr, 16)

            def load_uv(q):
                sp.dma_start(wuv[:, :, :], wuv_v[:, :, bass.ds(q * HQ * P, HQ * P)]).then_inc(s_wuv, 16)

            def load_o(q, half):
                sp.dma_start(wo[:, half], wo_v[:, bass.ds(q * HQ, HQ), half * HALF:(half + 1) * HALF])\
                    .then_inc(s_wo[half], 16)

            def stack_head(b, q, i):
                n = b * (NQ + 1) + 1 + q
                if not (isinstance(b, int) and b == 0 and isinstance(q, int) and q == 0):
                    wait_apart(sp, s_S, tile_no(b, q, i, 0) - (HQ - 1) * TT)
                wait_apart(sp, s_rhi, n + 1)
                wait_apart(sp, s_rlo, n + 1)
                src = slice(i * HR, (i + 1) * HR)
                for lo, part in ((0, rh), (R, rl)):
                    for j in range(2):
                        sp.dma_start(stack[lo + j * HR:lo + (j + 1) * HR, i, :].bitcast(F32),
                                     part[src, j, :].bitcast(F32)).then_inc(s_stack[i], 16)

            def into(b, q, nxt):
                wait_apart(sp, s_sorted, b * NQ + q + 1)
                load_qr(nxt)
                for i in range(HQ - 1):
                    stack_head(b, q, i)
                wait_apart(sp, fullA, pos_a(b, q, 2))
                load_uq(q * HQ + 2, 0)
                wait_apart(sp, fullB, pos_b(b, q, 2))
                load_uk(q * HQ + 2, 0)
                if not (isinstance(b, int) and b == 0):
                    if not isinstance(q, int):
                        wait_apart(sp, s_f, ((b - 1) * TT + q) * NF)
                    wait_apart(sp, s_x1, 16 * TT * b)
                    sp.dma_start(fsel, o_t[b - 1, q] if isinstance(q, int) else
                                 o_t[b - 1, bass.ds(q, 1)].rearrange("a p d -> (a p) d")).then_inc(s_x1in, 16)
                stack_head(b, q, HQ - 1)

            def heads(b, q, nxt, q0):
                for i in range(HQ - 1):
                    slot = (i + 1) % 2
                    h = q * HQ + HQ - 1 if i == 0 else nxt * HQ + i - 1
                    wait_apart(sp, fullA, pos_a(b, q, 2 + i) + 1)
                    load_uq(h, slot)
                    wait_apart(sp, fullB, pos_b(b, q, 2 + i) + 1)
                    load_uk(h, slot)
                    if i == 0:
                        if not q0:
                            for half in range(2):
                                wait_apart(sp, fullC, pos_c(b, q - 1, 4 + 2 * half))
                                wait_apart(sp, fullD, pos_d(b, q - 1, 8 + 2 * half))
                                load_o(q, half)
                        wait_apart(sp, fullC, pos_c(b, q, 2))
                        wait_apart(sp, fullD, pos_d(b, q, 2))
                        load_uv(nxt)

            sp.dma_start(wkr, wkr_v).then_inc(s_wkr, 16)
            sp.dma_start(cosT[:, :], cos_t).then_inc(s_const, 16)
            sp.dma_start(sinT[:, :], sin_t).then_inc(s_const, 16)
            load_xs(0, 0)
            load_xs(0, 1)
            load_dq(0)
            load_xs(0, 2)
            load_xs(0, 3)
            load_qr(0)
            for h in range(2):
                load_uq(h, h)
                load_uk(h, h)
            load_uv(0)
            load_xs(0, 4)
            load_xs(0, 5)
            load_kvc(0)
            load_xs(0, 6)
            load_xs(0, 7)
            sp.dma_start(gb[:, :], gamma.rearrange("(a n) -> a n", a=1).broadcast_to([P, D])).then_inc(s_const, 16)
            sp.dma_start(bb[:, :], beta.rearrange("(a n) -> a n", a=1).broadcast_to([P, D])).then_inc(s_const, 16)
            for half in range(2):
                load_o(0, half)
            for t in range(TT):
                sp.dma_start(acc[:, t, :], x_t[0, t]).then_inc(s_acc, 16)
            into(0, 0, 1)

            def ffn_stores(b, q):
                k = b * TT + q
                tile = bass.ds(q, 1)
                wait_apart(sp, s_fpool, k * 3 + 1)
                sp.dma_start(o_t[b, tile].rearrange("a p d -> (a p) d"), fy).then_inc(s_z, 16)
                wait_apart(sp, s_f, k * NF + 17)
                sp.dma_start(oh_dram[bass.ds(k, 1)].rearrange("a p t -> (a p) t"), oh[:, :]).then_inc(s_oh, 16)

            def body(b, first, last):
                if not last:
                    load_xs(b + 1, 0)
                    load_xs(b + 1, 1)
                    load_dq(b + 1)
                heads(b, 0, 1, True)
                if not first:
                    ffn_stores(b - 1, 0)
                with sp.Fori(1, NQ) as q:
                    into(b, q, (q + 1) % NQ)
                    heads(b, q, (q + 1) % NQ, False)
                    if not first:
                        ffn_stores(b - 1, q)
                if not last:
                    load_xs(b + 1, 2)
                    load_xs(b + 1, 3)
                    for half in range(2):
                        if half == 1:
                            load_xs(b + 1, 4)
                            load_xs(b + 1, 5)
                            load_kvc(b + 1)
                        wait_apart(sp, fullC, pos_c(b, NQ - 1, 4 + 2 * half))
                        wait_apart(sp, fullD, pos_d(b, NQ - 1, 8 + 2 * half))
                        load_o(0, half)
                    load_xs(b + 1, 6)
                    load_xs(b + 1, 7)
                    for t in range(TT):
                        ps_free, n = (freeC, pos_c(b, NQ - 1, 4 + t // 2)) if t % 2 == 0 else \
                                     (freeD, pos_d(b, NQ - 1, 8 + t // 2))
                        wait_apart(sp, ps_free, n + 1)
                        sp.dma_start(o_t[b, t], acc[:, t, :]).then_inc(s_x1, 16)
                    into(b + 1, 0, 1)
                    wait_apart(sp, s_x1, 16 * TT * (b + 1))
                    for t in range(TT):
                        sp.dma_start(acc[:, t, :], x_t[b + 1, t]).then_inc(s_acc, 16)

            batches(sp, body)
            wait_apart(sp, fullA, B * AN)
            wait_apart(sp, fullB, B * BN)
            wait_apart(sp, fullC, B * CN)
            wait_apart(sp, fullD, B * DN)
            sp.dma_start(spl[:, 0, 0:256], bases.rearrange("t j g -> t (j g)")).then_inc(s_tab, 16)
            sp.dma_start(spl[:, 0, 256:512], slopes.rearrange("t j g -> t (j g)")).then_inc(s_tab, 16)
            sp.dma_start(tab[:, 2:3], oscale.rearrange("(t a) -> t a", a=1), allow_slow_non_contiguous=True)\
                .then_inc(s_tab, 16)
            for t in range(TT):
                ffn_stores(B - 1, t)
            wait_apart(sp, s_z, 16 * NTOK)
            wait_apart(sp, s_oh, 16 * NTOK)
            sp.dma_start(ohall, oh_dram.rearrange("k p t -> p k t")).then_inc(s_ohin, 16)

        @block.gpsimd
        def _(pool):
            n_set = [0]

            def setup(ins):
                n_set[0] += 1
                ins.then_inc(s_setup, 1)
                wait_apart(pool, s_setup, n_set[0])

            setup(pool.memset(idt, 0.0))
            setup(pool.affine_select(out=idt, in_=idt, compare_op=ALU.not_equal, fill=1.0,
                                     base=0, pattern=[[-1, P]], channel_multiplier=1))
            setup(pool.tensor_copy(identb[:, :], idt))
            setup(pool.tensor_copy(identr[:, :], idt))
            setup(pool.iota(tmi[:, 0:T], [[1, T]], base=0, channel_multiplier=0))
            setup(pool.tensor_copy(kidx[:, :], tmi[:, 0:T]))
            setup(pool.iota(tmi[:, 0:NT], [[-512, CLUSTERS], [-1, NT // CLUSTERS]],
                            base=512 * (CLUSTERS - 1) + 8 * SLICE + NT // CLUSTERS - 1, channel_multiplier=0))
            setup(pool.tensor_copy(tie[:, :], tmi[:, 0:NT]))
            setup(pool.memset(run[:, 0, :], BIG))
            setup(pool.memset(run[:, 1, :], -BIG))
            setup(pool.memset(nhalf[:, :], -0.5))
            pool.dma_start(sl[0:NT, :], slopes.rearrange("t j g -> t (j g)")).then_inc(s_sl, 16)
            wait_apart(pool, s_seta, 1)
            pool.dma_start(ss_dram, sgn64[0:NT, :]).then_inc(s_ssd, 16)
            wait_apart(pool, s_ssd, 16)
            pool.dma_start(ssf, ss_dram.rearrange("(a t) j -> a (t j)", a=1).broadcast_to([P, D]))\
                .then_inc(s_ssb, 16)
            wait_apart(pool, s_ssb, 16)
            setup(pool.tensor_copy(ssb[:, :], ssf))

            def masks(b, first):
                if not first:
                    wait_apart(pool, s_sm, b * H * TT)
                    for i in range(HQ):
                        wait_apart(pool, s_stack[i], 64 * b * NQ)
                pool.dma_start(segi[:, :], seg_v[b], allow_slow_non_contiguous=True).then_inc(s_seg, 16)
                wait_apart(pool, s_seg, 16 * (b + 1))
                c = Chain(pool, s_mask, b * NM)
                c.do(pool.tensor_copy(segf[:, 0, :], segi[:, :]))
                c.do(pool.tensor_scalar(segf[:, 1, :], segf[:, 0, :], -float(LOOKBACK), None, ALU.add))
                for t in range(TT):
                    lo, hi = mtmp[:, 0, :], mtmp[:, 1, :]
                    c.do(pool.tensor_scalar(lo, kidx[:, :], segf[:, 1, t:t + 1], None, ALU.is_ge))
                    c.do(pool.tensor_scalar(hi, kidx[:, :], segf[:, 0, t:t + 1], None, ALU.is_le))
                    c.do(pool.tensor_tensor(lo, lo, hi, ALU.mult))
                    c.do(pool.tensor_scalar(mask[:, t, :], lo, 1.0, -NEG, ALU.subtract, ALU.mult))
                assert c.n == NM

            def rstds(b):
                for t in range(TT):
                    wait_apart(pool, s_ln, (b * TT + t) * NL + 4)
                    pool.tensor_tensor(mv[:, 3:4], mv[:, 2:3], nhalf[:, :], ALU.pow).then_inc(s_rstd, 1)

            def rope_lo(b, k):
                n = b * (NQ + 1) + 1 + k
                wait_apart(pool, s_rhi, n + 1)
                pool.tensor_tensor(rl[:, :, :], rr[:, :, :], rh[:, :, :].bitcast(F32), ALU.subtract)\
                    .then_inc(s_rlo, 1)

            def k_rope_lo(b):
                n = b * (NQ + 1)
                wait_apart(pool, s_rhi, n + 1)
                pool.tensor_tensor(krl[:, :], rr[0:R, 0, :], krh[0:R, :].bitcast(F32), ALU.subtract)\
                    .then_inc(s_rlo, 1)

            def ffn(b, t, x1):
                k = b * TT + t
                base = k * NF
                wait_apart(pool, s_f, base + 4)
                pool.tensor_tensor(mv2[:, 3:4], mv2[:, 2:3], nhalf[:, :], ALU.pow).then_inc(s_rstd2, 1)
                wait_apart(pool, s_f, base + 9)
                pool.tensor_tensor(mv2[:, 7:8], mv2[:, 6:7], nhalf[:, :], ALU.pow).then_inc(s_rstd2, 1)
                wait_apart(pool, s_f, base + 10)
                pool.tensor_tensor(fy, fy, x1, ALU.add).then_inc(s_fpool, 1)
                wait_apart(pool, s_sign, k + 1)
                pool.tensor_tensor(fs, fs, ssb[:, :], ALU.mult).then_inc(s_fpool, 1)
                wait_apart(pool, s_f, base + 17)
                pool.tensor_tensor(fsel.rearrange("p (t j) -> p t j", j=SLICE),
                                   fx.rearrange("p (t j) -> p t j", j=SLICE),
                                   onehot_wide(), ALU.mult).then_inc(s_fpool, 1)

            def sort_qr(n):
                wait_apart(pool, s_wqr, 16 * (n + 1))
                for c in range(QB):
                    for j in range(2):
                        ins = pool.tensor_copy(
                            wqp[:, c, j, :].rearrange("p (h r) -> p h r", r=HR),
                            wqr[:, c, :].rearrange("p (h j r) -> p j h r", j=2, r=HR)[:, j])
                ins.then_inc(s_sorted, 1)

            rstds(0)
            sort_qr(0)
            masks(0, True)
            k_rope_lo(0)
            rope_lo(0, 0)
            sort_qr(1)

            def body(b, first, last):
                if not first:
                    ffn(b - 1, 0, fsel)
                with pool.Fori(1, NQ) as q:
                    rope_lo(b, q)
                    sort_qr(b * NQ + q + 1)
                    if not first:
                        ffn(b - 1, q, fsel)
                if not last:
                    rstds(b + 1)
                    masks(b + 1, False)
                    k_rope_lo(b + 1)
                    rope_lo(b + 1, 0)
                    sort_qr((b + 1) * NQ + 1)

            batches(pool, body)
            for t in range(TT):
                ffn(B - 1, t, acc[:, t, :])

            wait_apart(pool, fullD, B * DN)
            wait_apart(pool, fullC, B * CN)
            wait_apart(pool, fullA, B * AN)
            wait_apart(pool, fullB, B * BN)
            c = Chain(pool, s_iota, 0)
            c.do(pool.iota(rampi[:, 0:GRID], [[1, GRID]], base=0, channel_multiplier=0))
            c.do(pool.tensor_copy(gramp, rampi[:, 0:GRID]))
            c.do(pool.iota(rampi[:, 0:NTOK], [[P * NT, NTOK]], base=0, channel_multiplier=NT))
            c.do(pool.tensor_copy(tokb, rampi[:, 0:NTOK]))
            c.do(pool.iota(rampi[0:NT, 0:1], [[1, 1]], base=0, channel_multiplier=1))
            c.do(pool.tensor_copy(tab[:, 3:4], rampi[0:NT, 0:1]))
            rows = out.rearrange("b s (t j) -> (b s t) j", j=SLICE)
            wait_apart(pool, s_z, 16 * NTOK)
            wait_apart(pool, s_gv, NG)
            for k in range(NTOK):
                pool.indirect_dma_start(rows, bass.IndirectOffsetOnAxis(ap=idxi[:, k:k + 1], axis=0),
                                        fd[:, k, :], None, compute_op=ALU.add).then_inc(s_sc, 16)
            wait_apart(pool, s_sc, 16 * NTOK)

        @block.scalar
        def _(act):
            act.wait_ge(s_setv, 1)
            act.activation(sgn64[0:NT, :], ssum[0:NT, :], ACT.Sign).then_inc(s_seta, 1)

            def stage_turned(b, j, ctx_side):
                for half in range(2):
                    k = (TT * 2 if ctx_side else 0) + 2 * j + half
                    act.wait_ge(fullT, b * TN + k + 1)
                    if k == 0 and not (isinstance(b, int) and b <= 1):
                        act.wait_ge(s_f, (b - 1) * TT * NF)
                        act.wait_ge(s_fpool, (b - 1) * TT * 3)
                        act.wait_ge(s_z, 16 * (b - 1) * TT)
                    if k == 0 and isinstance(b, int) and b == 0:
                        act.wait_ge(s_setup, 11)
                        act.wait_ge(s_setup, 12)
                        act.wait_ge(s_ssd, 16)
                        act.wait_ge(s_setv, 7)
                    act.activation(xT[:, 4 * half:4 * half + 4, j * P:(j + 1) * P],
                                   psT[k % 2][:, :].rearrange("p (c n) -> p c n", c=4), ACT.Copy)\
                       .then_inc(freeT, 1)

            def down(ps, full, free, n, dst):
                act.wait_ge(full, n + 1)
                act.activation(dst, ps[:, :], ACT.Copy).then_inc(free, 1)

            def q_hi(b, q, i):
                act.wait_ge(fullA, pos_a(b, q, 1 + i) + 1)
                act.activation(qh[:, :], psA[:, :], ACT.Copy).then_inc(s_qhi, 1)

            def k_hi(b, q, i):
                act.wait_ge(fullB, pos_b(b, q, 1 + i) + 1)
                act.activation(kh[:, :], psB[:, :], ACT.Copy).then_inc(s_khi, 1)

            def values(b, q):
                for kt in range(TT):
                    ps, full, free, n = ((psC, fullC, freeC, pos_c(b, q, kt // 2)) if kt % 2 == 0 else
                                         (psD, fullD, freeD, pos_d(b, q, kt // 2)))
                    act.wait_ge(full, n + 1)
                    act.activation(V[0][:, kt, :], ps[:, :], ACT.Copy).then_inc(s_vhi, 1)

            def k_rope_hi(b):
                n = b * (NQ + 1)
                act.wait_ge(s_rope, b * NR + 1)
                act.activation(krh[:, :], rr[:, 0, :], ACT.Copy).then_inc(s_rhi, 1)

            def rope_hi(b, q, prev):
                act.wait_ge(s_rope, b * NR + 1 + 4 * (q + 1))
                if prev:
                    for i in range(HQ):
                        act.wait_ge(s_stack[i], 64 * (b * NQ + q))
                act.activation(rh[:, :, :], rr[:, :, :], ACT.Copy).then_inc(s_rhi, 1)

            def expo(b, q, i, qt):
                act.wait_ge(s_sm, tile_no(b, q, i, qt) + 1)
                act.activation(E[:, qt % 2, :], E[:, qt % 2, :], ACT.Exp, scale=-1.0,
                               bias=mx[:, i % 2, qt:qt + 1],
                               accum_out=rs[:, i % 2, qt:qt + 1]).then_inc(s_exp, 1)

            def probs_turned(b, q, i, qt):
                for part in range(2):
                    act.wait_ge(fullT, pos_t(b, q, i, qt) + part + 1)
                    act.activation(PT[part][:, :, qt * P:(qt + 1) * P],
                                   psT[part][:, :].rearrange("p (c n) -> p c n", c=TT), ACT.Copy)\
                       .then_inc(freeT, 1)

            def attended(b, q, i):
                act.wait_ge(fullD, pos_d(b, q, 2 + i) + 1)
                act.activation(attn[:, i, :], psD[:, :], ACT.Copy).then_inc(freeD, 1)

            def sign(b, t):
                act.wait_ge(s_f, (b * TT + t) * NF + 11)
                act.activation(fs, fx, ACT.Sign).then_inc(s_sign, 1)

            def prologue(b, first):
                for j in range(TT):
                    stage_turned(b, j, False)
                down(psA, fullA, freeA, b * AN, qc[:, 0, :])
                down(psB, fullB, freeB, b * BN, qc[:, 1, :])
                down(psA, fullA, freeA, b * AN + 1, qc[:, 2, :])
                for j in range(TT):
                    stage_turned(b, j, True)
                down(psB, fullB, freeB, b * BN + 1, kvc[:, 0, :])
                down(psA, fullA, freeA, b * AN + 2, kvc[:, 1, :])
                k_rope_hi(b)
                rope_hi(b, 0, not first)
                q_hi(b, 0, 0)
                k_hi(b, 0, 0)

            prologue(0, True)

            def body(b, first, last):
                def head(q, i, q0, nxt=None):
                    expo(b, q, i, 0)
                    expo(b, q, i, 1)
                    if i > 0:
                        attended(b, q, i - 1)
                    elif not q0:
                        attended(b, q - 1, HQ - 1)
                    if nxt is not None:
                        rope_hi(b, nxt, True)
                    probs_turned(b, q, i, 0)
                    expo(b, q, i, 2)
                    probs_turned(b, q, i, 1)
                    expo(b, q, i, 3)
                    if nxt is not None:
                        q_hi(b, nxt, 0)
                        k_hi(b, nxt, 0)
                    elif i < HQ - 1:
                        q_hi(b, q, i + 1)
                        k_hi(b, q, i + 1)
                    probs_turned(b, q, i, 2)
                    probs_turned(b, q, i, 3)
                    if i == 0 and not q0:
                        values(b, q)
                    if i == 1 and not first:
                        sign(b - 1, q)

                values(b, 0)
                for i in range(HQ - 1):
                    head(0, i, True)
                with act.Fori(1, NQ) as q:
                    head(q - 1, HQ - 1, False, q)
                    for i in range(HQ - 1):
                        head(q, i, False)
                head(NQ - 1, HQ - 1, False)
                attended(b, NQ - 1, HQ - 1)
                if not last:
                    prologue(b + 1, False)

            batches(act, body)
            for t in range(TT):
                sign(B - 1, t)
            act.wait_ge(s_z, 16 * NTOK)
            for g in range(NTOK // 4):
                act.wait_ge(s_g, 2 + g + 1)
                act.activation(ohT[:, g * 512:(g + 1) * 512], psTb[g % 2][0:NT, 0:512], ACT.Copy)\
                   .then_inc(s_ge, 1)

        @block.vector
        def _(dve):
            dve.wait_ge(s_sl, 16)
            dve.tensor_reduce(ssum[0:NT, :], sl[0:NT, :].rearrange("p (j g) -> p j g", g=GRID), AX.X, ALU.add)\
               .then_inc(s_setv, 1)
            dve.wait_ge(s_wkr, 16)
            for c in range(2):
                dve.tensor_copy(wkra[:, :, c, :], wkr).then_inc(s_setv, 1)
                dve.tensor_scalar(wkrb[:, :, c, 0:HR], wkr[:, :, HR:R], -1.0, None, ALU.mult).then_inc(s_setv, 1)
                dve.tensor_copy(wkrb[:, :, c, HR:R], wkr[:, :, 0:HR]).then_inc(s_setv, 1)

            def norm_x(b, t):
                xt = xs[:, t % 2, :]
                dve.wait_ge(s_xs[t % 2], 16 * (b * TT + t // 2 + 1))
                c = Chain(dve, s_ln, (b * TT + t) * NL)
                for h in range(2):
                    c.do(dve.bn_stats(st[:, h, :], xt[:, h * HALF:(h + 1) * HALF]), wait=h == 1)
                c.do(dve.bn_aggr(mv[:, 0:2], st[:, :, :].rearrange("p a s -> p (a s)")))
                c.do(dve.tensor_scalar(mv[:, 2:3], mv[:, 1:2], LN_EPS, None, ALU.add), wait=False)
                dve.wait_ge(s_rstd, b * TT + t + 1)
                c.do(dve.tensor_scalar(xt, xt, mv[:, 0:1], mv[:, 3:4], ALU.subtract, ALU.mult))
                assert c.n == NL

            def rope_k(b):
                if not (isinstance(b, int) and b == 0):
                    dve.wait_ge(s_rhi, b * (NQ + 1))
                    dve.wait_ge(s_rlo, b * (NQ + 1))
                dve.wait_ge(fullA, b * AN + 4)
                dve.tensor_tensor(rt[:, 0, :], psA[:, :], cosT[:, :], ALU.mult).then_inc(freeA, 1)
                dve.wait_ge(fullB, b * BN + 3)
                dve.tensor_tensor(rt[:, 1, :], psB[:, :], sinT[:, :], ALU.mult).then_inc(freeB, 1)
                dve.wait_ge(freeA, b * AN + 4)
                dve.wait_ge(freeB, b * BN + 3)
                dve.tensor_tensor(rr[:, 0, :], rt[:, 0, :], rt[:, 1, :], ALU.add).then_inc(s_rope, 1)

            def rope_q(b, q):
                n = b * (NQ + 1) + 1 + q
                c = Chain(dve, s_rope, b * NR + 1 + 4 * q)
                dve.wait_ge(s_rope, b * NR + 1 + 4 * q)
                dve.wait_ge(fullA, pos_a(b, q, 0) + 1)
                c.do(dve.tensor_tensor(rt[:, 0, :], psA[:, :], cosT[:, :], ALU.mult), wait=False)
                dve.wait_ge(fullB, pos_b(b, q, 0) + 1)
                c.do(dve.tensor_tensor(rt[:, 1, :], psB[:, :], sinT[:, :], ALU.mult))
                dve.wait_ge(s_rhi, n)
                dve.wait_ge(s_rlo, n)
                c.do(dve.tensor_tensor(rr[:, 0, :], rt[:, 0, :], rt[:, 1, :], ALU.subtract))
                dve.tensor_tensor(rt[:, 0, :], psA[:, :], sinT[:, :], ALU.mult).then_inc(freeA, 1)
                dve.tensor_tensor(rt[:, 1, :], psB[:, :], cosT[:, :], ALU.mult).then_inc(freeB, 1)
                dve.wait_ge(freeA, pos_a(b, q, 0) + 1)
                dve.wait_ge(freeB, pos_b(b, q, 0) + 1)
                c.do(dve.tensor_tensor(rr[:, 1, :], rt[:, 0, :], rt[:, 1, :], ALU.add), wait=False)

            def q_lo(b, q, i):
                dve.wait_ge(s_qhi, b * H + q * HQ + i + 1)
                dve.tensor_tensor(ql[:, :], psA[:, :], qh[:, :].bitcast(F32), ALU.subtract)\
                   .then_inc(freeA, 1)

            def k_lo(b, q, i):
                dve.wait_ge(s_khi, b * H + q * HQ + i + 1)
                dve.tensor_tensor(kl[:, :], psB[:, :], kh[:, :].bitcast(F32), ALU.subtract)\
                   .then_inc(freeB, 1)

            def values_lo(b, q):
                for kt in range(TT):
                    ps, free = (psC, freeC) if kt % 2 == 0 else (psD, freeD)
                    dve.wait_ge(s_vhi, (b * NQ + q) * TT + kt + 1)
                    dve.tensor_tensor(V[1][:, kt, :], ps[:, :], V[0][:, kt, :].bitcast(F32), ALU.subtract)\
                       .then_inc(free, 1)

            def mask_scores(b, q, i, qt, head0):
                n = tile_no(b, q, i, qt)
                if head0 and qt == 0:
                    dve.wait_ge(s_mask, (b + 1) * NM)
                wait_apart(dve, s_S, n + 1)
                dve.tensor_tensor_reduce(E[:, qt % 2, :], psS[qt % 2][:, :], mask[:, qt, :], -SCALE, BIG,
                                         ALU.add, ALU.min, mx[:, i % 2, qt:qt + 1]).then_inc(s_sm, 1)

            def divide(b, q, i, qt, very_first):
                n = tile_no(b, q, i, qt)
                e, r = E[:, qt % 2, :], ri[:, i % 2, qt:qt + 1]
                dve.wait_ge(s_exp, n + 1)
                dve.reciprocal(r, rs[:, i % 2, qt:qt + 1]).then_inc(s_rinv, 1)
                if not very_first:
                    if qt < 2 and isinstance(q, int) and q == 0 and i == 0:
                        dve.wait_ge(fullT, b * TN - 4 + 2 * qt + 2)
                    else:
                        dve.wait_ge(fullT, pos_t(b, q, i, qt) - 2)
                dve.wait_ge(s_rinv, n + 1)
                dve.tensor_scalar(Ph[0][:, qt % 2, :], e, r, None, ALU.mult).then_inc(s_prob, 1)
                dve.wait_ge(s_prob, n + 1)
                dve.scalar_tensor_tensor(out=Ph[1][:, qt % 2, :], in0=e, scalar=r,
                                         in1=Ph[0][:, qt % 2, :].bitcast(F32), op0=ALU.mult, op1=ALU.subtract)\
                   .then_inc(s_plo, 1)

            def add_out(b, q, w, first_add):
                half, t = w // TT, w % TT
                if w % 2 == 0:
                    ps, full, free, n = psC, fullC, freeC, pos_c(b, q, 2 + w // 2)
                else:
                    ps, full, free, n = psD, fullD, freeD, pos_d(b, q, 6 + w // 2)
                if first_add:
                    dve.wait_ge(s_acc, 16 * TT * (b + 1))
                dve.wait_ge(full, n + 1)
                if w < 2:
                    pass
                a = acc[:, t, half * HALF:(half + 1) * HALF]
                dve.tensor_tensor(a, a, ps[:, :], ALU.add).then_inc(free, 1)

            def ffn_chunks(b, t, x1, tail):
                k = b * TT + t
                c = Chain(dve, s_f, k * NF)

                def stats_x():
                    if not tail:
                        wait_apart(dve, s_x1in, 16 * (k + 1))
                    elif t == 0:
                        dve.wait_ge(freeC, pos_c(b, NQ - 1, 6))
                        dve.wait_ge(freeD, pos_d(b, NQ - 1, 10))
                    for h in range(2):
                        c.do(dve.bn_stats(st2[:, h, :], x1[:, h * HALF:(h + 1) * HALF]), wait=h == 1)

                def aggregate_x():
                    c.do(dve.bn_aggr(mv2[:, 0:2], st2[:, :, :].rearrange("p a s -> p (a s)")))
                    c.do(dve.tensor_scalar(mv2[:, 2:3], mv2[:, 1:2], LN_EPS, None, ALU.add), wait=False)

                def norm():
                    dve.wait_ge(s_rstd2, 2 * k + 1)
                    if not (isinstance(k, int) and k == 0):
                        dve.wait_ge(s_z, z_before(k))
                    c.do(dve.tensor_scalar(fy, x1, mv2[:, 0:1], mv2[:, 3:4], ALU.subtract, ALU.mult))

                def stats_norm():
                    for h in range(2):
                        c.do(dve.bn_stats(st2[:, h, :], fy[:, h * HALF:(h + 1) * HALF]), wait=h == 1)

                def aggregate_norm():
                    c.do(dve.bn_aggr(mv2[:, 4:6], st2[:, :, :].rearrange("p a s -> p (a s)")))
                    c.do(dve.tensor_scalar(mv2[:, 6:7], mv2[:, 5:6], LN_EPS, None, ALU.add), wait=False)

                def scale_in():
                    c.do(dve.scalar_tensor_tensor(out=fx, in0=fy, scalar=mv2[:, 4:5], in1=gb[:, :],
                                                  op0=ALU.subtract, op1=ALU.mult))

                def shift_in():
                    dve.wait_ge(s_rstd2, 2 * k + 2)
                    c.do(dve.scalar_tensor_tensor(out=fx, in0=fx, scalar=mv2[:, 7:8], in1=bb[:, :],
                                                  op0=ALU.mult, op1=ALU.add), wait=False)
                    assert c.n == 11

                def score_tiles():
                    dve.wait_ge(s_fpool, k * 3 + 2)
                    c.do(dve.tensor_reduce(ts[:, :], fs.rearrange("p (t j) -> p t j", j=SLICE), AX.X, ALU.add))

                def choose():
                    by_cluster = {"c": CLUSTERS}
                    c.do(dve.tensor_reduce(cs[:, :], ts[:, :].rearrange("p (c t) -> p c t", **by_cluster),
                                           AX.X, ALU.add))
                    wide = cs[:, :].rearrange("p (c a) -> p c a", a=1).broadcast_to([P, CLUSTERS, NT // CLUSTERS])
                    c.do(dve.scalar_tensor_tensor(out=key[:, :].rearrange("p (c t) -> p c t", **by_cluster),
                                                  in0=wide, scalar=4096.0,
                                                  in1=tie[:, :].rearrange("p (c t) -> p c t", **by_cluster),
                                                  op0=ALU.mult, op1=ALU.add))
                    c.do(dve.scalar_tensor_tensor(out=key[:, :], in0=ts[:, :], scalar=float(NT // CLUSTERS),
                                                  in1=key[:, :], op0=ALU.mult, op1=ALU.add))
                    c.do(dve.tensor_reduce(kmax[:, :], key[:, :], AX.X, ALU.max))
                    if not (isinstance(k, int) and k == 0):
                        dve.wait_ge(s_oh, z_before(k))
                    c.do(dve.tensor_scalar(oh[:, :], key[:, :], kmax[:, 0:1], None, ALU.is_equal), wait=False)
                    assert c.n == 17

                def take_slice():
                    xk = xsl[:, k, :]
                    wait_apart(dve, s_fpool, k * 3 + 3)
                    c.do(dve.tensor_reduce(xk, fsel.rearrange("p (t j) -> p j t", j=SLICE), AX.X, ALU.add))
                    c.do(dve.tensor_reduce(mm[:, 0:1], xk, AX.X, ALU.min), wait=False)
                    c.do(dve.tensor_reduce(mm[:, 1:2], xk, AX.X, ALU.max), wait=False)
                    c.do(dve.tensor_scalar(cand[:, 2, :], oh[:, :], 1.0, -BIG, ALU.subtract, ALU.mult))
                    c.do(dve.scalar_tensor_tensor(out=cand[:, 0, :], in0=oh[:, :], scalar=mm[:, 0:1],
                                                  in1=cand[:, 2, :], op0=ALU.mult, op1=ALU.add), wait=False)
                    c.do(dve.scalar_tensor_tensor(out=cand[:, 1, :], in0=oh[:, :], scalar=mm[:, 1:2],
                                                  in1=cand[:, 2, :], op0=ALU.mult, op1=ALU.subtract))
                    c.do(dve.tensor_tensor(run[:, 0, :], run[:, 0, :], cand[:, 0, :], ALU.min), wait=False)
                    c.do(dve.tensor_tensor(run[:, 1, :], run[:, 1, :], cand[:, 1, :], ALU.max))
                    assert c.n == NF

                return [[[stats_x], [aggregate_x], [norm], [stats_norm]],
                        [[aggregate_norm], [scale_in], [shift_in], []],
                        [[score_tiles], [choose], [], [take_slice]]]

            def z_before(k):
                return 16 * k

            def prologue(b):
                rope_k(b)
                rope_q(b, 0)
                q_lo(b, 0, 0)
                k_lo(b, 0, 0)

            for t in range(TT):
                norm_x(0, t)
            dve.wait_ge(s_const, 64)
            dve.wait_ge(s_setup, 11)
            prologue(0)

            def body(b, first, last):
                def head(q, i, q0, nxt=None, ffn=None):
                    head0 = q0 and i == 0
                    vf = first and head0
                    adds = not q0 and i == 0

                    def piece(slot):
                        for part in (ffn[i][slot] if ffn else ()):
                            part()

                    mask_scores(b, q, i, 0, head0)
                    mask_scores(b, q, i, 1, head0)
                    divide(b, q, i, 0, vf)
                    divide(b, q, i, 1, vf)
                    if nxt is not None:
                        rope_q(b, nxt)
                    piece(0)
                    mask_scores(b, q, i, 2, head0)
                    if adds:
                        add_out(b, q - 1, 0, True)
                        add_out(b, q - 1, 1, False)
                    piece(1)
                    divide(b, q, i, 2, False)
                    mask_scores(b, q, i, 3, head0)
                    if adds:
                        add_out(b, q - 1, 2, False)
                        add_out(b, q - 1, 3, False)
                    if nxt is not None:
                        q_lo(b, nxt, 0)
                    elif i < HQ - 1:
                        q_lo(b, q, i + 1)
                    divide(b, q, i, 3, False)
                    if nxt is not None:
                        k_lo(b, nxt, 0)
                    elif i < HQ - 1:
                        k_lo(b, q, i + 1)
                    piece(2)
                    if adds:
                        for w in range(4, 8):
                            add_out(b, q - 1, w, False)
                        values_lo(b, q)
                    piece(3)

                def steps(q):
                    return None if first else ffn_chunks(b - 1, q, fsel, False)

                values_lo(b, 0)
                ffn = steps(0)
                for i in range(HQ - 1):
                    head(0, i, True, None, ffn)
                with dve.Fori(1, NQ) as q:
                    head(q - 1, HQ - 1, False, q)
                    ffn = steps(q)
                    for i in range(HQ - 1):
                        head(q, i, False, None, ffn)
                head(NQ - 1, HQ - 1, False)
                if not last:
                    norm_x(b + 1, 0)
                    norm_x(b + 1, 1)
                for w in range(0, 4):
                    add_out(b, NQ - 1, w, False)
                if not last:
                    norm_x(b + 1, 2)
                    norm_x(b + 1, 3)
                for w in range(4, 8):
                    add_out(b, NQ - 1, w, False)
                if not last:
                    prologue(b + 1)

            batches(dve, body)
            for t in range(TT):
                for step in ffn_chunks(B - 1, t, acc[:, t, :], True):
                    for slot in step:
                        for part in slot:
                            part()

            dve.wait_ge(s_g, 2)
            dve.wait_ge(s_tab, 48)
            c = Chain(dve, s_gv, 0)
            c.do(dve.tensor_reduce(tab[:, 0:1], psA[0:NT, 0:P], AX.X, ALU.min), wait=False)
            c.do(dve.tensor_reduce(tab[:, 1:2], psB[0:NT, 0:P], AX.X, ALU.max), wait=False)
            dve.wait_ge(s_g, 3 + NTOK // 4)
            wide = [NTOK, SLICE]

            def per_tile(v):
                return v.rearrange("p (k a) -> p k a", a=1).broadcast_to([P, NTOK, SLICE])

            c.do(dve.tensor_copy(fin, psC[:, 0:NTOK * 4].rearrange("p (k c) -> p k c", c=4)))
            c.do(dve.tensor_tensor(dena, fin[:, :, 1], fin[:, :, 0], ALU.subtract))
            c.do(dve.tensor_scalar(dena, dena, 1e-8, None, ALU.add))
            c.do(dve.tensor_tensor(fu, xsl[:, :, :], per_tile(fin[:, :, 0]), ALU.subtract))
            c.do(dve.reciprocal(dena, dena))
            c.do(dve.tensor_tensor(fu, fu, per_tile(dena), ALU.mult))
            c.do(dve.tensor_scalar(fu, fu, 0.0, 1.0 - 1e-6, ALU.max, ALU.min))
            c.do(dve.tensor_scalar(fu, fu, float(GRID), None, ALU.mult))
            c.do(dve.tensor_scalar(fg, fu, ROUND, None, ALU.add))
            c.do(dve.tensor_scalar(fg, fg, ROUND, None, ALU.subtract))
            c.do(dve.tensor_tensor(fl, fg, fu, ALU.is_gt))
            c.do(dve.tensor_tensor(fg, fg, fl, ALU.subtract))
            c.do(dve.tensor_tensor(fl, fu, fg, ALU.subtract))
            dve.wait_ge(s_iota, 6)
            c.do(dve.tensor_tensor(idxf, fin[:, :, 3], tokb, ALU.add))
            c.do(dve.tensor_copy(idxi, idxf))
            n0 = c.n
            for g in range(2):
                eq = eqb.rearrange("p (k g) -> p k g", g=GRID)
                cells = fg[:, g * 16:(g + 1) * 16, :].rearrange("p k (j a) -> p (k j) a", a=1)
                ramp = gramp.rearrange("p (a g) -> p a g", a=1).broadcast_to([P, 16 * SLICE, GRID])
                c.do(dve.tensor_tensor(eq, cells.broadcast_to([P, 16 * SLICE, GRID]), ramp, ALU.is_equal))
                for kk in range(16):
                    k = g * 16 + kk
                    ps = [psA, psB, psD, psS[0]][k % 4]
                    dve.wait_ge(s_gb, k + 1)
                    e = eqb.rearrange("p (k j g) -> p k j g", j=SLICE, g=GRID)[:, kk, :, :]
                    pr = prod[:, k % 2, :].rearrange("p (a j g) -> p a j g", a=2, g=GRID)
                    for a in range(2):
                        ins = dve.tensor_tensor(pr[:, a], ps[:, a * 256:(a + 1) * 256]
                                                .rearrange("p (j g) -> p j g", g=GRID), e, ALU.mult)
                        if a == 0:
                            ins.then_inc(s_gv, 1)
                            c.n += 1
                        else:
                            ins.then_inc(s_gf, 1)
                    dve.wait_ge(s_gf, k + 1)
                    dve.wait_ge(s_gv, c.n)
                    c.do(dve.tensor_reduce(bsel[:, k // 8, (k % 8) * 32:(k % 8 + 1) * 32],
                                           prod[:, k % 2, :].rearrange("p (m g) -> p m g", g=GRID),
                                           AX.X, ALU.add), wait=False)
                dve.wait_ge(s_gv, c.n)
            bs = bsel.rearrange("p m (k a j) -> p m k a j", a=2, j=SLICE)
            fd4 = fd.rearrange("p (m k) j -> p m k j", m=4)
            fl4 = fl.rearrange("p (m k) j -> p m k j", m=4)
            c.do(dve.tensor_tensor(fd4, bs[:, :, :, 1, :], fl4, ALU.mult))
            c.do(dve.tensor_tensor(fd4, fd4, bs[:, :, :, 0, :], ALU.add))
            c.do(dve.tensor_tensor(fd, fd, per_tile(fin[:, :, 2]), ALU.mult), wait=False)
            assert c.n == NG, c.n

        @block.tensor
        def _(pe):
            def turn_stage(b, j, ctx_side):
                jj = j + (TT if ctx_side else 0)
                if ctx_side:
                    pe.wait_ge(s_xs[j % 2], 16 * (b * TT + 2 + j // 2 + 1))
                else:
                    pe.wait_ge(s_ln, (b * TT + j + 1) * NL)
                for half in range(2):
                    k = 2 * jj + half
                    if not (isinstance(b, int) and b == 0 and k < 2):
                        pe.wait_ge(freeT, b * TN + k - 1)
                    for c in range(4):
                        blk = 4 * half + c
                        mm_ = pe.transpose(psT[k % 2][:, c * P:(c + 1) * P],
                                           xs[:, j % 2, blk * P:(blk + 1) * P], ident)
                    mm_.then_inc(fullT, 1)

            def wait_free(free, n):
                if not (isinstance(n, int) and n == 0):
                    pe.wait_ge(free, n)

            def down(ps, full, free, n, col):
                wait_free(free, n)
                for c in range(DB):
                    mm_ = pe.matmul(ps[:, :], wD[:, c, col * P:(col + 1) * P], xT[:, c, :],
                                    start=c == 0, stop=c == DB - 1)
                mm_.then_inc(full, 1)

            def rope_keys(b):
                for ps, full, free, n, w in ((psA, fullA, freeA, b * AN + 3, wkra),
                                             (psB, fullB, freeB, b * BN + 2, wkrb)):
                    wait_free(free, n)
                    for c in range(CB):
                        mm_ = pe.matmul(ps[:, :], w[:, c].rearrange("p a r -> p (a r)"), kvc[:, c, :],
                                        start=c == 0, stop=c == CB - 1)
                    mm_.then_inc(full, 1)

            def rope_queries(b, q):
                pe.wait_ge(s_sorted, b * NQ + q + 1)
                for ps, full, free, n, j in ((psA, fullA, freeA, pos_a(b, q, 0), 0),
                                             (psB, fullB, freeB, pos_b(b, q, 0), 1)):
                    wait_free(free, n)
                    for c in range(QB):
                        mm_ = pe.matmul(ps[:, :], wqp[:, c, j, :], qc[:, c, :],
                                        start=c == 0, stop=c == QB - 1)
                    mm_.then_inc(full, 1)

            def queries(b, q, i):
                pe.wait_ge(s_wuq[i % 2], 16 * (b * (H // 2) + q * (HQ // 2) + i // 2 + 1))
                wait_free(freeA, pos_a(b, q, 1 + i))
                for c in range(QB):
                    mm_ = pe.matmul(psA[:, :], wuq[:, i % 2, c, :], qc[:, c, :], start=c == 0, stop=c == QB - 1)
                mm_.then_inc(fullA, 1)

            def keys(b, q, i):
                pe.wait_ge(s_wuk[i % 2], 16 * (b * (H // 2) + q * (HQ // 2) + i // 2 + 1))
                wait_free(freeB, pos_b(b, q, 1 + i))
                for c in range(CB):
                    mm_ = pe.matmul(psB[:, :], wuk[:, i % 2, c, :], kvc[:, c, :], start=c == 0, stop=c == CB - 1)
                mm_.then_inc(fullB, 1)

            def values(b, q):
                pe.wait_ge(s_wuv, 16 * (b * NQ + q + 1))
                for kt in range(TT):
                    ps, full, free, n = ((psC, fullC, freeC, pos_c(b, q, kt // 2)) if kt % 2 == 0 else
                                         (psD, fullD, freeD, pos_d(b, q, kt // 2)))
                    wait_free(free, n)
                    for c in range(CB):
                        mm_ = pe.matmul(ps[:, :], kvc[:, c, kt * P:(kt + 1) * P], wuv[:, c, :],
                                        start=c == 0, stop=c == CB - 1)
                    mm_.then_inc(full, 1)

            def scores(b, q, i, qt, very_first):
                n = tile_no(b, q, i, qt)
                if qt == 0:
                    pe.wait_ge(freeA, pos_a(b, q, 1 + i) + 1)
                    pe.wait_ge(freeB, pos_b(b, q, 1 + i) + 1)
                    pe.wait_ge(s_stack[i], 64 * (b * NQ + q + 1))
                    if i == 0 and isinstance(q, int):
                        pe.wait_ge(s_rhi, b * (NQ + 1) + 1)
                        pe.wait_ge(s_rlo, b * (NQ + 1) + 1)
                if not (very_first and qt < 2):
                    pe.wait_ge(s_sm, n - 1)
                cols = slice(qt * P, (qt + 1) * P)
                ps = psS[qt % 2][:, :]
                pe.matmul(ps, qh[:, cols], kh[:, :], start=True, stop=False)
                pe.matmul(ps, qh[:, cols], kl[:, :], start=False, stop=False)
                pe.matmul(ps, ql[:, cols], kh[:, :], start=False, stop=False)
                pe.matmul(ps, stack[:, i, cols], krh[:, :], start=False, stop=False)
                pe.matmul(ps, stack[0:R, i, cols], krl[:, :], start=False, stop=True).then_inc(s_S, 1)

            def turn_probs(b, q, i, qt):
                for part, done in ((0, s_prob), (1, s_plo)):
                    pe.wait_ge(done, tile_no(b, q, i, qt) + 1)
                    pe.wait_ge(freeT, pos_t(b, q, i, qt) + part - 1)
                    for c in range(TT):
                        mm_ = pe.transpose(psT[part][:, c * P:(c + 1) * P].bitcast(F32R),
                                           Ph[part][:, qt % 2, c * P:(c + 1) * P], identr[:, :])
                    mm_.then_inc(fullT, 1)

            def attend(b, q, i):
                pe.wait_ge(freeT, pos_t(b, q, i, TT - 1) + 2)
                if i == 0:
                    pe.wait_ge(freeC, pos_c(b, q, 2))
                pe.wait_ge(freeD, pos_d(b, q, 2 + i))
                for kt in range(TT):
                    for v, p in ((0, 0), (0, 1), (1, 0)):
                        mm_ = pe.matmul(psD[:, :], V[v][:, kt, i * P:(i + 1) * P], PT[p][:, kt, :],
                                        start=kt == 0 and v + p == 0, stop=kt == TT - 1 and v == 1)
                mm_.then_inc(fullD, 1)

            def out_proj(b, q, w):
                half, t = w // TT, w % TT
                if w % 2 == 0:
                    ps, full, free, n = psC, fullC, freeC, pos_c(b, q, 2 + w // 2)
                else:
                    ps, full, free, n = psD, fullD, freeD, pos_d(b, q, 6 + w // 2)
                if t == 0:
                    pe.wait_ge(s_wo[half], 16 * (b * NQ + q + 1))
                if w == 0:
                    pe.wait_ge(freeD, pos_d(b, q, 6))
                pe.wait_ge(free, n)
                for i in range(HQ):
                    mm_ = pe.matmul(ps[:, :], attn[:, i, t * P:(t + 1) * P], wo[:, half, i, :],
                                    start=i == 0, stop=i == HQ - 1)
                mm_.then_inc(full, 1)

            def down_q(b):
                pe.wait_ge(s_wd, 32 * b + 16)
                pe.wait_ge(freeT, b * TN + 2 * TT)
                down(psA, fullA, freeA, b * AN, 0)
                down(psB, fullB, freeB, b * BN, 1)
                down(psA, fullA, freeA, b * AN + 1, 2)

            def down_kv(b):
                pe.wait_ge(s_wd, 32 * b + 32)
                pe.wait_ge(freeT, b * TN + 4 * TT)
                down(psB, fullB, freeB, b * BN + 1, 0)
                down(psA, fullA, freeA, b * AN + 2, 1)

            def into_heads(b):
                pe.wait_ge(freeA, b * AN + 3)
                pe.wait_ge(freeB, b * BN + 2)
                rope_keys(b)
                rope_queries(b, 0)
                queries(b, 0, 0)
                keys(b, 0, 0)

            pe.wait_ge(s_setup, 4)
            for j in range(TT):
                turn_stage(0, j, False)
            down_q(0)
            for j in range(TT):
                turn_stage(0, j, True)
            down_kv(0)
            pe.wait_ge(s_setv, 7)
            into_heads(0)

            def body(b, first, last):
                def head(q, i, q0, nxt=None):
                    vf = first and q0 and i == 0
                    outs = not q0 and i == 0
                    scores(b, q, i, 0, vf)
                    scores(b, q, i, 1, vf)
                    if i > 0:
                        attend(b, q, i - 1)
                    elif not q0:
                        attend(b, q - 1, HQ - 1)
                    if nxt is not None:
                        rope_queries(b, nxt)
                    turn_probs(b, q, i, 0)
                    scores(b, q, i, 2, vf)
                    if outs:
                        out_proj(b, q - 1, 0)
                        out_proj(b, q - 1, 1)
                    turn_probs(b, q, i, 1)
                    scores(b, q, i, 3, vf)
                    if outs:
                        out_proj(b, q - 1, 2)
                        out_proj(b, q - 1, 3)
                    if nxt is not None:
                        queries(b, nxt, 0)
                        keys(b, nxt, 0)
                    elif i < HQ - 1:
                        queries(b, q, i + 1)
                        keys(b, q, i + 1)
                    turn_probs(b, q, i, 2)
                    if outs:
                        for w in range(4, 8):
                            out_proj(b, q - 1, w)
                    turn_probs(b, q, i, 3)
                    if outs:
                        values(b, q)

                values(b, 0)
                for i in range(HQ - 1):
                    head(0, i, True)
                with pe.Fori(1, NQ) as q:
                    head(q - 1, HQ - 1, False, q)
                    for i in range(HQ - 1):
                        head(q, i, False)
                head(NQ - 1, HQ - 1, False)
                attend(b, NQ - 1, HQ - 1)
                for w in range(4):
                    out_proj(b, NQ - 1, w)
                if not last:
                    for j in range(TT):
                        turn_stage(b + 1, j, False)
                    down_q(b + 1)
                for w in range(4, 8):
                    out_proj(b, NQ - 1, w)
                if not last:
                    for j in range(TT):
                        turn_stage(b + 1, j, True)
                    down_kv(b + 1)
                    into_heads(b + 1)

            batches(pe, body)

            pe.wait_ge(s_f, NTOK * NF)
            pe.wait_ge(freeA, B * AN)
            pe.wait_ge(freeB, B * BN)
            pe.transpose(psA[0:NT, 0:P], run[:, 0, :], ident).then_inc(s_g, 1)
            pe.transpose(psB[0:NT, 0:P], run[:, 1, :], ident).then_inc(s_g, 1)
            pe.wait_ge(s_ohin, 16)
            for g in range(NTOK // 4):
                if g >= 2:
                    pe.wait_ge(s_ge, g - 1)
                for k in range(4):
                    mm_ = pe.transpose(psTb[g % 2][0:NT, k * P:(k + 1) * P], ohall[:, 4 * g + k, :], identb[:, :])
                mm_.then_inc(s_g, 1)
            pe.wait_ge(s_gv, 2)
            pe.wait_ge(s_iota, 6)
            pe.wait_ge(s_tab, 48)
            pe.wait_ge(s_ge, NTOK // 4)
            pe.wait_ge(freeC, B * CN)
            for k in range(NTOK):
                mm_ = pe.matmul(psC[:, k * 4:k * 4 + 4], ohT[:, k * P:(k + 1) * P], tab[:, :], start=True, stop=True)
            mm_.then_inc(s_g, 1)
            pe.wait_ge(freeD, B * DN)
            for k in range(NTOK):
                ps = [psA, psB, psD, psS[0]][k % 4]
                if k >= 4:
                    pe.wait_ge(s_gf, k - 3)
                pe.matmul(ps[:, :], ohT[:, k * P:(k + 1) * P], spl[:, 0, :],
                          start=True, stop=True).then_inc(s_gb, 1)


NM = 2 + 4 * 4
NR = 1 + 4 * 4
NG = 2 + 15 + 2 + 32 * 2 + 3


def wait_apart(eng, sem, n):
    eng.wait_ge(sem, n)
    if not isinstance(n, int):
        eng.sem_inc(AFTER[0], 1)


AFTER = []


class Chain:

    def __init__(self, eng, sem, base):
        self.eng, self.sem, self.base, self.n = eng, sem, base, 0

    def do(self, ins, wait=True):
        self.n += 1
        ins.then_inc(self.sem, 1)
        if wait:
            wait_apart(self.eng, self.sem, self.base + self.n)


_INS = ['x', 'ctx_2048', 'itok_BxS_0_1023', 'L0_xattn_W_kvc', 'L0_xattn_W_dq', 'L0_xattn_W_uq', 'L0_xattn_W_qr',
        'L0_xattn_W_uk', 'L0_xattn_W_kr', 'L0_xattn_W_uv', 'L0_xattn_W_o', 'L0_ffn_ln_gamma', 'L0_ffn_ln_beta',
        'L0_ffn_spline_bases', 'L0_ffn_spline_slopes', 'L0_ffn_output_scale']
_OUTS = [((8, 512, 1024), 'float32')]


def _rotary_tables(length, half):
    import numpy as _np
    steps = _np.arange(half, dtype=_np.float32) / _np.float32(half)
    inv = (_np.float32(1.0) / _np.power(_np.float32(10000.0), steps)).astype(_np.float32)
    ang = (_np.arange(length, dtype=_np.float32)[:, None] * inv).astype(_np.float64)
    reps = 128 // half
    return [_np.ascontiguousarray(_np.tile(f(ang).astype(_np.float32).T, (reps, 1))) for f in (_np.cos, _np.sin)]


def kernel(**inputs):
    import numpy as _np
    import concourse.bacc as _bacc
    from concourse import mybir as _mybir
    from concourse.bass_utils import run_bass_kernel_spmd as _run

    nc = _bacc.Bacc("TRN2", target_bir_lowering=False, num_devices=1)
    arrays, args = {}, []
    cos_t, sin_t = _rotary_tables(512, 32)
    data = [(name, _np.ascontiguousarray(inputs[name])) for name in _INS] + [('cos_t', cos_t), ('sin_t', sin_t)]
    for name, a in data:
        arrays[f"in_{name}_dram"] = a
        args.append(nc.dram_tensor(f"in_{name}_dram", a.shape, _mybir.dt.from_np(a.dtype), kind="ExternalInput").ap())
    for i, (shape, dtype) in enumerate(_OUTS):
        dt = _mybir.dt.from_np(_np.dtype(dtype))
        args.append(nc.dram_tensor(f"out_{i}_dram", shape, dt, kind="ExternalOutput").ap())
    xattn_ffn_kernel(nc, *args)
    r = _run(nc, [arrays], core_ids=[0])
    got = tuple(r.results[0][f"out_{i}_dram"] for i in range(len(_OUTS)))
    return got[0]
```

```python
from contextlib import ExitStack

import concourse.bass as bass
from concourse import mybir

F32 = mybir.dt.float32
F32R = mybir.dt.float32r
BF16 = mybir.dt.bfloat16
I32 = mybir.dt.int32
U32 = mybir.dt.uint32
ALU = mybir.AluOpType
ACT = mybir.ActivationFunctionType
AX = mybir.AxisListType

P = 128
HALF = 512
LOOKBACK = 8
NEG = -1.0e30
BIG = 3.0e38
LN_EPS = 1e-5
ROUND = 8388608.0
GRID = 16
SLICE = 16
NT = 64
CLUSTERS = 8


def xattn_ffn_kernel(nc, x, ctx_in, seg, w_kvc, w_dq, w_uq, w_qr, w_uk, w_kr, w_uv, w_o,
                     gamma, beta, bases, slopes, oscale, cos_t, sin_t, out):
    B, T, D = x.shape
    KVC, QC = w_kvc.shape[1], w_dq.shape[1]
    R = w_kr.shape[1]
    HR = R // 2
    H = w_uq.shape[1] // P
    TT = T // P
    DB = D // P
    CB, QB = KVC // P, QC // P
    HQ = 4
    NQ = H // HQ
    SCALE = 1.0 / float(P + R) ** 0.5
    NTOK = B * T // P
    assert T == HALF and HQ * HR == P and 2 * R == P and D == 2 * HALF and NT * SLICE == D

    A0, AQ = 4, 1 + HQ
    B0, BQ = 3, 1 + HQ
    CQ, DQ = 10, 14
    PAIRS = H // 2
    AN, BN, CN, DN = A0 + NQ * AQ, B0 + NQ * BQ, NQ * CQ, NQ * DQ
    T0, TN = 4 * TT, 4 * TT + 2 * H * TT

    def pos_a(b, q, k):
        if isinstance(q, int) and q == 0 and k == 0:
            return b * AN + 2
        return b * AN + A0 + q * AQ + k

    def pos_b(b, q, k):
        if isinstance(q, int) and q == 0 and k == 0:
            return b * BN + 1
        return b * BN + B0 + q * BQ + k

    def pos_c(b, q, k):
        return b * CN + q * CQ + k

    def pos_d(b, q, k):
        return b * DN + q * DQ + k

    def pos_av(b, q, i):
        return pos_d(b, q, 2 + 6 * (i // 2) + i % 2)

    def pos_oc(b, q, pair, w):
        return pos_c(b, q, 2 + 4 * pair + w // 2)

    def pos_od(b, q, pair, w):
        return pos_d(b, q, 4 + 6 * pair + w // 2)

    def pos_t(b, q, i, qt):
        return b * TN + T0 + 2 * ((q * HQ + i) * TT + qt)

    def rope_no(b, q):
        return b * (NQ + 1) + (0 if isinstance(q, int) and q == 0 else 1 + q)

    def rope_base(b, q):
        return b * NR + (0 if isinstance(q, int) and q == 0 else 1 + 4 * q)

    def tile_no(b, q, i, qt):
        return b * H * TT + (q * HQ + i) * TT + qt

    NF = 25
    NL = 5

    with ExitStack() as ctx:
        def sb(name, shape, dt=F32):
            return ctx.enter_context(nc.sbuf_tensor(name, shape, dt))

        def bank(name, dt=F32):
            return ctx.enter_context(nc.psum_tensor(name, [P, HALF], dt))

        def sem(name):
            return ctx.enter_context(nc.semaphore(name))

        psS = [bank("psS0"), bank("psS1")]
        psT = [bank("psT0"), bank("psT1")]
        psA, psB, psC, psD = bank("psA"), bank("psB"), bank("psC"), bank("psD")

        wD = sb("w_down", [P, DB, QC])
        wuq = sb("w_uq_ring", [P, 2, QB, P])
        wuk = sb("w_uk_ring", [P, 2, CB, P])
        wqr = sb("w_qr_quad", [P, QB, HQ * R])
        wqp = sb("w_qr_sorted", [P, QB, 2, HQ * HR])
        wuv = sb("w_uv_quad", [P, CB, HQ * P])
        WO = [sb("w_o_pair_hi", [P, 2, D], F32R), sb("w_o_pair_lo", [P, 2, D], F32R)]
        wkra = sb("w_kr_a", [P, CB, 2, R])
        wkrb = sb("w_kr_b", [P, CB, 2, R])
        xs = sb("x_stage", [P, 2, D])
        xT = sb("xT", [P, DB, T])
        qc = sb("q_c", [P, QB, T])
        kvc = sb("kv_c", [P, CB, T])
        rt = sb("rope_terms", [P, 2, T])
        rr = sb("rope_out", [P, 2, T])
        rh = sb("rope_hi", [P, 2, T], F32R)
        rl = sb("rope_lo", [P, 2, T], F32R)
        stack = sb("q_rope_stack", [P, HQ, T], F32R)
        krh = sb("k_rope_hi", [P, T], F32R)
        krl = sb("k_rope_lo", [R, T], F32R)
        V = [sb("values_hi", [P, TT, HQ * P], F32R), sb("values_lo", [P, TT, HQ * P], F32R)]
        qh, ql = sb("q_hi", [P, T], F32R), sb("q_lo", [P, T], F32R)
        kh, kl = sb("k_hi", [P, T], F32R), sb("k_lo", [P, T], F32R)
        E = sb("exps_ring", [P, 2, T])
        Ph = [sb("probs_hi", [P, 2, T], F32R), sb("probs_lo", [P, 2, T], F32R)]
        PT = [sb("probsT_hi", [P, TT, T], F32R), sb("probsT_lo", [P, TT, T], F32R)]
        mask = sb("mask", [P, TT, T], BF16)
        attn = [sb("attn_hi", [P, 2, T], F32R), sb("attn_lo", [P, 2, T], F32R)]
        acc = sb("acc", [P, TT, D])
        cosT, sinT = sb("cosT", [P, T]), sb("sinT", [P, T])
        identr = sb("ident", [P, P], F32R)
        ident = identr[:, :].bitcast(F32)
        identb = sb("ident_b", [P, P], BF16)
        kidx = sb("key_index", [P, T], mybir.dt.float16)
        mtmp = rl[:, :, :].bitcast(F32)
        segi = sb("seg_int", [P, TT], I32)
        segf = sb("seg_f", [P, 2, TT])
        nhalf = sb("minus_half", [P, 1])
        mx = sb("neg_max", [P, 2, TT])
        rs = sb("row_sum", [P, 2, TT])
        ri = sb("row_sum_inverse", [P, 2, TT])
        st = sb("ln_stats", [P, 2, 6])
        mv = sb("ln_mean_var", [P, 4])
        st2 = sb("ffn_stats", [P, 2, 6])
        mv2 = sb("ffn_mean_var", [P, 8])
        gb = sb("gamma_b", [P, D])
        bb = sb("beta_b", [P, D])
        ssb = sb("slope_sign_b", [P, D], BF16)
        sl = xT[:, 0, 0:256]
        tie = sb("tie_order", [P, NT])
        ts = sb("tile_scores", [P, NT])
        cs = sb("cluster_scores", [P, CLUSTERS])
        key = sb("tile_key", [P, NT])
        kmax = sb("key_max", [P, 1])
        oh = sb("onehot", [P, NT], BF16)
        xsl = sb("x_slice", [P, NTOK, SLICE])
        mm = sb("slice_min_max", [P, 2])
        cand = sb("candidates", [P, 3, NT])
        run = sb("run_min_max", [P, 2, NT])
        fy = xT[:, 0:2, :].rearrange("p a n -> p (a n)")
        fx = xT[:, 2:4, :].rearrange("p a n -> p (a n)")
        fs = xT[:, 4:6, :].rearrange("p a n -> p (a n)")
        fsel = xT[:, 6:8, :].rearrange("p a n -> p (a n)")
        tmi = xT[:, 7, 0:T].bitcast(I32)
        idt = xT[:, 6, 0:P]
        wkr = xT[:, 5, 0:CB * R].rearrange("p (c r) -> p c r", c=CB)
        ssf = xT[:, 2:4, :].rearrange("p a n -> p (a n)")
        sgn64 = xT[:, 1, 0:SLICE]
        ssum = xT[:, 1, SLICE:2 * SLICE]

        AFTER[:] = [sem("waits_apart")]
        s_const = sem("constants_in")
        s_wkr = sem("w_kr_in_sem")
        s_sl = sem("slopes_in")
        s_iota = sem("ramps")
        s_setup = sem("setup_pool")
        s_setv = sem("setup_vector")
        s_seta = sem("setup_scalar")
        s_ssb = sem("slope_sign_in")
        s_ssd = sem("slope_sign_dram")
        s_wd = sem("w_down_in")
        s_wuq, s_wuk = [sem("w_uq_in0"), sem("w_uq_in1")], [sem("w_uk_in0"), sem("w_uk_in1")]
        s_sorted = sem("w_qr_sorted_done")
        s_wqr, s_wuv = sem("w_qr_in"), sem("w_uv_in")
        s_wo = [sem("w_o_in0"), sem("w_o_in1")]
        s_wohi, s_wolo = sem("w_o_hi_done"), sem("w_o_lo_done")
        s_ahi = sem("attn_hi_done")
        s_xs = [sem("x_in0"), sem("x_in1")]
        s_seg = sem("seg_in")
        s_rstd, s_rstd2 = sem("ln_rstd"), sem("ffn_rstd")
        s_rinv = sem("row_sum_inverse_done")
        s_ln = sem("ln_steps")
        s_mask = sem("mask_steps")
        s_acc = sem("acc_in")
        fullA, fullB, fullC, fullD = sem("fullA"), sem("fullB"), sem("fullC"), sem("fullD")
        freeA, freeB, freeC, freeD = sem("freeA"), sem("freeB"), sem("freeC"), sem("freeD")
        fullT, freeT = sem("fullT"), sem("freeT")
        s_S, s_sm, s_exp, s_prob = sem("scores"), sem("scores_masked"), sem("exps"), sem("probs_done")
        s_vhi = sem("v_hi_done")
        s_qhi, s_khi = sem("q_hi_done"), sem("k_hi_done")
        s_rope, s_rhi, s_rlo = sem("rope_steps"), sem("rope_hi_done"), sem("rope_lo_done")
        s_stack = [sem(f"stack_in{i}") for i in range(HQ)]
        s_f = sem("ffn_steps")
        s_sign, s_fpool = sem("ffn_sign"), sem("ffn_pool")
        s_x1, s_x1in = sem("x1_out"), sem("x1_in")
        s_oh, s_ohin = sem("onehot_out"), sem("onehot_in")
        s_plo = sem("probs_lo_done")
        s_z = sem("z_out")
        s_tab = sem("tables_in")
        s_g = sem("gather_pe")
        s_ge = sem("gather_scalar")
        s_gv = sem("gather_vector")
        s_gf = sem("spline_row_used")
        s_gb = sem("spline_row")
        s_sc = sem("scattered")

        x_t = x.rearrange("b (t p) d -> b t p d", p=P)
        c_t = ctx_in.rearrange("b (t p) d -> b t p d", p=P)
        o_t = out.rearrange("b (t p) d -> b t p d", p=P)
        seg_v = seg.rearrange("b (t p) -> b p t", p=P)
        wdq_v = w_dq.rearrange("(c p) n -> p c n", p=P)
        wkvc_v = w_kvc.rearrange("(c p) n -> p c n", p=P)
        wuq_v = w_uq.rearrange("(c p) n -> p c n", p=P)
        wqr_v = w_qr.rearrange("(c p) n -> p c n", p=P)
        wuk_v = w_uk.rearrange("(c p) n -> p c n", p=P)
        wkr_v = w_kr.rearrange("(c p) n -> p c n", p=P)
        wuv_v = w_uv.rearrange("(c p) n -> p c n", p=P)
        wo_v = w_o.rearrange("(h p) n -> p h n", p=P)
        oh_dram = nc.dram_tensor("onehot_scratch", [NTOK, P, NT], BF16).ap()
        ss_dram = nc.dram_tensor("slope_sign_scratch", [NT, SLICE], F32).ap()

        spl = qc[0:NT, 0:1, :]
        tab = kvc[0:NT, 0, 0:4]
        prod = rt[:, :, :]
        ohT = acc[0:NT, :, :].rearrange("p t n -> p (t n)")
        eqb = xT[:, :, :].rearrange("p a n -> p (a n)")
        bsel = wD[:, 0:4, 0:256]
        ohall = xs[:, 0, :].bitcast(BF16).rearrange("p (k t) -> p k t", t=NT)
        fin = qc[:, 2, 0:NTOK * 4].rearrange("p (k c) -> p k c", c=4)
        fu = E[:, 0, :].rearrange("p (k j) -> p k j", j=SLICE)
        fl = E[:, 1, :].rearrange("p (k j) -> p k j", j=SLICE)
        fg = rr[:, 0, :].rearrange("p (k j) -> p k j", j=SLICE)
        fd = rr[:, 1, :].rearrange("p (k j) -> p k j", j=SLICE)
        gramp = kvc[:, 1, 0:GRID]
        tokb = kvc[:, 1, 32:32 + NTOK]
        idxf = kvc[:, 1, 96:96 + NTOK]
        dena = kvc[:, 1, 160:160 + NTOK]
        idxi = kvc[:, 1, 256:256 + NTOK].bitcast(I32)
        rampi = kvc[:, 1, 320:384].bitcast(I32)

        psTb = [p[:, :].bitcast(BF16) for p in psT]

        def onehot_wide():
            return oh[:, :].rearrange("p (t a) -> p t a", a=1).broadcast_to([P, NT, SLICE])

        def batches(eng, body):
            body(0, True, False)
            with eng.Fori(1, B - 1) as b:
                body(b, False, False)
            body(B - 1, False, True)

        block = ctx.enter_context(nc.Block())

        @block.sync
        def _(sp):
            def load_dq(b):
                if not (isinstance(b, int) and b == 0):
                    wait_apart(sp, fullA, (b - 1) * AN + 4)
                    wait_apart(sp, fullB, (b - 1) * BN + 3)
                sp.dma_start(wD[:, :, :], wdq_v).then_inc(s_wd, 16)

            def load_kvc(b):
                wait_apart(sp, fullA, b * AN + 2)
                wait_apart(sp, fullB, b * BN + 1)
                sp.dma_start(wD[:, :, 0:KVC], wkvc_v).then_inc(s_wd, 16)

            def load_xs(b, j):
                if j >= 2:
                    wait_apart(sp, fullT, b * TN + 2 * (j - 2) + 2)
                elif not (isinstance(b, int) and b == 0):
                    wait_apart(sp, s_wolo, 2 * PAIRS * b - 1 + j)
                src = x_t[b, j] if j < TT else c_t[b, j - TT]
                sp.dma_start(xs[:, j % 2, :], src).then_inc(s_xs[j % 2], 16)

            def load_uq(h, slot):
                sp.dma_start(wuq[:, slot], wuq_v[:, :, bass.ds(h * P, P)]).then_inc(s_wuq[slot], 16)

            def load_uk(h, slot):
                sp.dma_start(wuk[:, slot], wuk_v[:, :, bass.ds(h * P, P)]).then_inc(s_wuk[slot], 16)

            def load_qr(q):
                sp.dma_start(wqr[:, :, :], wqr_v[:, :, bass.ds(q * HQ * R, HQ * R)]).then_inc(s_wqr, 16)

            def load_uv(q):
                sp.dma_start(wuv[:, :, :], wuv_v[:, :, bass.ds(q * HQ * P, HQ * P)]).then_inc(s_wuv, 16)

            def load_o(b, q, pair):
                n = (b * NQ + q) * 2 + pair
                for j in range(2):
                    if pair == 0 and isinstance(q, int):
                        wait_apart(sp, fullT, b * TN + 2 * (j + 6) + 2)
                    else:
                        wait_apart(sp, s_wolo, 2 * (n - 1) + j + 1)
                    h = q * HQ + 2 * pair + j
                    sp.dma_start(xs[:, j, :], wo_v[:, bass.ds(h, 1), :].rearrange("p a n -> p (a n)"))\
                        .then_inc(s_wo[j], 16)

            def stack_head(b, q, i):
                n = rope_no(b, q)
                if not (isinstance(b, int) and b == 0 and isinstance(q, int) and q == 0):
                    wait_apart(sp, s_S, tile_no(b, q, i, 0) - (HQ - 1) * TT)
                wait_apart(sp, s_rhi, n + 1)
                wait_apart(sp, s_rlo, n + 1)
                src = slice(i * HR, (i + 1) * HR)
                for lo, part in ((0, rh), (R, rl)):
                    for j in range(2):
                        sp.dma_start(stack[lo + j * HR:lo + (j + 1) * HR, i, :].bitcast(F32),
                                     part[src, j, :].bitcast(F32)).then_inc(s_stack[i], 16)

            def into(b, q, nxt):
                wait_apart(sp, s_sorted, b * NQ + q + 1)
                load_qr(nxt)
                for i in range(HQ - 1):
                    stack_head(b, q, i)
                wait_apart(sp, fullA, pos_a(b, q, 2))
                load_uq(q * HQ + 2, 0)
                wait_apart(sp, fullB, pos_b(b, q, 2))
                load_uk(q * HQ + 2, 0)
                if not (isinstance(b, int) and b == 0):
                    if not isinstance(q, int):
                        wait_apart(sp, s_f, ((b - 1) * TT + q) * NF)
                    wait_apart(sp, s_x1, 16 * TT * b)
                    sp.dma_start(fsel, o_t[b - 1, q] if isinstance(q, int) else
                                 o_t[b - 1, bass.ds(q, 1)].rearrange("a p d -> (a p) d")).then_inc(s_x1in, 16)
                stack_head(b, q, HQ - 1)

            def heads(b, q, nxt, q0):
                for i in range(HQ - 1):
                    slot = (i + 1) % 2
                    h = q * HQ + HQ - 1 if i == 0 else nxt * HQ + i - 1
                    wait_apart(sp, fullA, pos_a(b, q, 2 + i) + 1)
                    load_uq(h, slot)
                    wait_apart(sp, fullB, pos_b(b, q, 2 + i) + 1)
                    load_uk(h, slot)
                    if i == 0:
                        load_o(b, q, 0)
                        wait_apart(sp, fullC, pos_c(b, q, 2))
                        wait_apart(sp, fullD, pos_d(b, q, 2))
                        load_uv(nxt)
                load_o(b, q, 1)

            sp.dma_start(wkr, wkr_v).then_inc(s_wkr, 16)
            sp.dma_start(cosT[:, :], cos_t).then_inc(s_const, 16)
            sp.dma_start(sinT[:, :], sin_t).then_inc(s_const, 16)
            load_xs(0, 0)
            load_xs(0, 1)
            load_dq(0)
            load_xs(0, 2)
            load_xs(0, 3)
            load_qr(0)
            for h in range(2):
                load_uq(h, h)
                load_uk(h, h)
            load_uv(0)
            load_xs(0, 4)
            load_xs(0, 5)
            load_kvc(0)
            load_xs(0, 6)
            load_xs(0, 7)
            sp.dma_start(gb[:, :], gamma.rearrange("(a n) -> a n", a=1).broadcast_to([P, D])).then_inc(s_const, 16)
            sp.dma_start(bb[:, :], beta.rearrange("(a n) -> a n", a=1).broadcast_to([P, D])).then_inc(s_const, 16)
            for t in range(TT):
                sp.dma_start(acc[:, t, :], x_t[0, t]).then_inc(s_acc, 16)
            into(0, 0, 1)

            def ffn_stores(b, q):
                k = b * TT + q
                tile = bass.ds(q, 1)
                wait_apart(sp, s_fpool, k * 3 + 1)
                sp.dma_start(o_t[b, tile].rearrange("a p d -> (a p) d"), fy).then_inc(s_z, 16)
                wait_apart(sp, s_f, k * NF + 17)
                sp.dma_start(oh_dram[bass.ds(k, 1)].rearrange("a p t -> (a p) t"), oh[:, :]).then_inc(s_oh, 16)

            def body(b, first, last):
                if not last:
                    load_dq(b + 1)
                heads(b, 0, 1, True)
                if not first:
                    ffn_stores(b - 1, 0)
                with sp.Fori(1, NQ) as q:
                    into(b, q, (q + 1) % NQ)
                    heads(b, q, (q + 1) % NQ, False)
                    if not first:
                        ffn_stores(b - 1, q)
                if not last:
                    for j in range(6):
                        load_xs(b + 1, j)
                    load_kvc(b + 1)
                    load_xs(b + 1, 6)
                    load_xs(b + 1, 7)
                    for t in range(TT):
                        ps_free, n = (freeC, pos_oc(b, NQ - 1, 1, TT + t)) if t % 2 == 0 else \
                                     (freeD, pos_od(b, NQ - 1, 1, TT + t))
                        wait_apart(sp, ps_free, n + 1)
                        sp.dma_start(o_t[b, t], acc[:, t, :]).then_inc(s_x1, 16)
                    into(b + 1, 0, 1)
                    wait_apart(sp, s_x1, 16 * TT * (b + 1))
                    for t in range(TT):
                        sp.dma_start(acc[:, t, :], x_t[b + 1, t]).then_inc(s_acc, 16)

            batches(sp, body)
            wait_apart(sp, fullA, B * AN)
            wait_apart(sp, fullB, B * BN)
            wait_apart(sp, fullC, B * CN)
            wait_apart(sp, fullD, B * DN)
            sp.dma_start(spl[:, 0, 0:256], bases.rearrange("t j g -> t (j g)")).then_inc(s_tab, 16)
            sp.dma_start(spl[:, 0, 256:512], slopes.rearrange("t j g -> t (j g)")).then_inc(s_tab, 16)
            sp.dma_start(tab[:, 2:3], oscale.rearrange("(t a) -> t a", a=1), allow_slow_non_contiguous=True)\
                .then_inc(s_tab, 16)
            for t in range(TT):
                ffn_stores(B - 1, t)
            wait_apart(sp, s_z, 16 * NTOK)
            wait_apart(sp, s_oh, 16 * NTOK)
            sp.dma_start(ohall, oh_dram.rearrange("k p t -> p k t")).then_inc(s_ohin, 16)

        @block.gpsimd
        def _(pool):
            n_set = [0]

            def setup(ins):
                n_set[0] += 1
                ins.then_inc(s_setup, 1)
                wait_apart(pool, s_setup, n_set[0])

            setup(pool.memset(idt, 0.0))
            setup(pool.affine_select(out=idt, in_=idt, compare_op=ALU.not_equal, fill=1.0,
                                     base=0, pattern=[[-1, P]], channel_multiplier=1))
            setup(pool.tensor_copy(identb[:, :], idt))
            setup(pool.tensor_copy(identr[:, :], idt))
            setup(pool.iota(tmi[:, 0:T], [[1, T]], base=0, channel_multiplier=0))
            setup(pool.tensor_copy(kidx[:, :], tmi[:, 0:T]))
            setup(pool.iota(tmi[:, 0:NT], [[-512, CLUSTERS], [-1, NT // CLUSTERS]],
                            base=512 * (CLUSTERS - 1) + 8 * SLICE + NT // CLUSTERS - 1, channel_multiplier=0))
            setup(pool.tensor_copy(tie[:, :], tmi[:, 0:NT]))
            setup(pool.memset(run[:, 0, :], BIG))
            setup(pool.memset(run[:, 1, :], -BIG))
            setup(pool.memset(nhalf[:, :], -0.5))
            pool.dma_start(sl[0:NT, :], slopes.rearrange("t j g -> t (j g)")).then_inc(s_sl, 16)
            wait_apart(pool, s_seta, 1)
            pool.dma_start(ss_dram, sgn64[0:NT, :]).then_inc(s_ssd, 16)
            wait_apart(pool, s_ssd, 16)
            pool.dma_start(ssf, ss_dram.rearrange("(a t) j -> a (t j)", a=1).broadcast_to([P, D]))\
                .then_inc(s_ssb, 16)
            wait_apart(pool, s_ssb, 16)
            setup(pool.tensor_copy(ssb[:, :], ssf))

            def masks(b, first):
                if not first:
                    wait_apart(pool, s_sm, b * H * TT)
                    for i in range(HQ):
                        wait_apart(pool, s_stack[i], 64 * b * NQ)
                pool.dma_start(segi[:, :], seg_v[b], allow_slow_non_contiguous=True).then_inc(s_seg, 16)
                wait_apart(pool, s_seg, 16 * (b + 1))
                c = Chain(pool, s_mask, b * NM)
                c.do(pool.tensor_copy(segf[:, 0, :], segi[:, :]))
                c.do(pool.tensor_scalar(segf[:, 1, :], segf[:, 0, :], -float(LOOKBACK), None, ALU.add))
                for t in range(TT):
                    lo, hi = mtmp[:, 0, :], mtmp[:, 1, :]
                    c.do(pool.tensor_scalar(lo, kidx[:, :], segf[:, 1, t:t + 1], None, ALU.is_ge))
                    c.do(pool.tensor_scalar(hi, kidx[:, :], segf[:, 0, t:t + 1], None, ALU.is_le))
                    c.do(pool.tensor_tensor(lo, lo, hi, ALU.mult))
                    c.do(pool.tensor_scalar(mask[:, t, :], lo, 1.0, -NEG, ALU.subtract, ALU.mult))
                assert c.n == NM

            def rstds(b):
                for t in range(TT):
                    wait_apart(pool, s_ln, (b * TT + t) * NL + 4)
                    pool.tensor_tensor(mv[:, 3:4], mv[:, 2:3], nhalf[:, :], ALU.pow).then_inc(s_rstd, 1)

            def rope_lo(b, k):
                wait_apart(pool, s_rhi, rope_no(b, k) + 1)
                pool.tensor_tensor(rl[:, :, :], rr[:, :, :], rh[:, :, :].bitcast(F32), ALU.subtract)\
                    .then_inc(s_rlo, 1)

            def k_rope_lo(b):
                wait_apart(pool, s_rhi, b * (NQ + 1) + 2)
                pool.tensor_tensor(krl[:, :], rr[0:R, 0, :], krh[0:R, :].bitcast(F32), ALU.subtract)\
                    .then_inc(s_rlo, 1)

            def wo_lo(b, q, pair):
                for j in range(2):
                    n = ((b * NQ + q) * 2 + pair) * 2 + j
                    wait_apart(pool, s_wohi, n + 1)
                    pool.tensor_tensor(WO[1][:, j, :], xs[:, j, :], WO[0][:, j, :].bitcast(F32), ALU.subtract)\
                        .then_inc(s_wolo, 1)

            def ffn_norms(b, t, x1):
                k = b * TT + t
                base = k * NF
                wait_apart(pool, s_f, base + 4)
                pool.tensor_tensor(mv2[:, 3:4], mv2[:, 2:3], nhalf[:, :], ALU.pow).then_inc(s_rstd2, 1)
                wait_apart(pool, s_f, base + 9)
                pool.tensor_tensor(mv2[:, 7:8], mv2[:, 6:7], nhalf[:, :], ALU.pow).then_inc(s_rstd2, 1)
                wait_apart(pool, s_f, base + 10)
                pool.tensor_tensor(fy, fy, x1, ALU.add).then_inc(s_fpool, 1)
                wait_apart(pool, s_sign, k + 1)
                pool.tensor_tensor(fs, fs, ssb[:, :], ALU.mult).then_inc(s_fpool, 1)

            def ffn_select(b, t):
                base = (b * TT + t) * NF
                wait_apart(pool, s_f, base + 17)
                pool.tensor_tensor(fsel.rearrange("p (t j) -> p t j", j=SLICE),
                                   fx.rearrange("p (t j) -> p t j", j=SLICE),
                                   onehot_wide(), ALU.mult).then_inc(s_fpool, 1)

            def sort_qr(n):
                wait_apart(pool, s_wqr, 16 * (n + 1))
                for c in range(QB):
                    for j in range(2):
                        ins = pool.tensor_copy(
                            wqp[:, c, j, :].rearrange("p (h r) -> p h r", r=HR),
                            wqr[:, c, :].rearrange("p (h j r) -> p j h r", j=2, r=HR)[:, j])
                ins.then_inc(s_sorted, 1)

            rstds(0)
            sort_qr(0)
            masks(0, True)
            rope_lo(0, 0)
            k_rope_lo(0)
            sort_qr(1)

            def body(b, first, last):
                def quad(q):
                    if not first:
                        ffn_norms(b - 1, q, fsel)
                    wo_lo(b, q, 0)
                    if not first:
                        ffn_select(b - 1, q)

                quad(0)
                with pool.Fori(1, NQ) as q:
                    rope_lo(b, q)
                    wo_lo(b, q - 1, 1)
                    sort_qr(b * NQ + q + 1)
                    quad(q)
                wo_lo(b, NQ - 1, 1)
                if not last:
                    rstds(b + 1)
                    masks(b + 1, False)
                    rope_lo(b + 1, 0)
                    k_rope_lo(b + 1)
                    sort_qr((b + 1) * NQ + 1)

            batches(pool, body)
            for t in range(TT):
                ffn_norms(B - 1, t, acc[:, t, :])
                ffn_select(B - 1, t)

            wait_apart(pool, fullD, B * DN)
            wait_apart(pool, fullC, B * CN)
            wait_apart(pool, fullA, B * AN)
            wait_apart(pool, fullB, B * BN)
            c = Chain(pool, s_iota, 0)
            c.do(pool.iota(rampi[:, 0:GRID], [[1, GRID]], base=0, channel_multiplier=0))
            c.do(pool.tensor_copy(gramp, rampi[:, 0:GRID]))
            c.do(pool.iota(rampi[:, 0:NTOK], [[P * NT, NTOK]], base=0, channel_multiplier=NT))
            c.do(pool.tensor_copy(tokb, rampi[:, 0:NTOK]))
            c.do(pool.iota(rampi[0:NT, 0:1], [[1, 1]], base=0, channel_multiplier=1))
            c.do(pool.tensor_copy(tab[:, 3:4], rampi[0:NT, 0:1]))
            rows = out.rearrange("b s (t j) -> (b s t) j", j=SLICE)
            wait_apart(pool, s_z, 16 * NTOK)
            wait_apart(pool, s_gv, NG)
            for k in range(NTOK):
                pool.indirect_dma_start(rows, bass.IndirectOffsetOnAxis(ap=idxi[:, k:k + 1], axis=0),
                                        fd[:, k, :], None, compute_op=ALU.add).then_inc(s_sc, 16)
            wait_apart(pool, s_sc, 16 * NTOK)

        @block.scalar
        def _(act):
            act.wait_ge(s_setv, 1)
            act.activation(sgn64[0:NT, :], ssum[0:NT, :], ACT.Sign).then_inc(s_seta, 1)

            def stage_turned(b, j, ctx_side):
                for half in range(2):
                    k = (TT * 2 if ctx_side else 0) + 2 * j + half
                    act.wait_ge(fullT, b * TN + k + 1)
                    if k == 0 and not (isinstance(b, int) and b <= 1):
                        act.wait_ge(s_f, (b - 1) * TT * NF)
                        act.wait_ge(s_fpool, (b - 1) * TT * 3)
                        act.wait_ge(s_z, 16 * (b - 1) * TT)
                    if k == 0 and isinstance(b, int) and b == 0:
                        act.wait_ge(s_setup, 11)
                        act.wait_ge(s_setup, 12)
                        act.wait_ge(s_ssd, 16)
                        act.wait_ge(s_setv, 7)
                    act.activation(xT[:, 4 * half:4 * half + 4, j * P:(j + 1) * P],
                                   psT[k % 2][:, :].rearrange("p (c n) -> p c n", c=4), ACT.Copy)\
                       .then_inc(freeT, 1)

            def down(ps, full, free, n, dst):
                act.wait_ge(full, n + 1)
                act.activation(dst, ps[:, :], ACT.Copy).then_inc(free, 1)

            def q_hi(b, q, i):
                act.wait_ge(fullA, pos_a(b, q, 1 + i) + 1)
                act.activation(qh[:, :], psA[:, :], ACT.Copy).then_inc(s_qhi, 1)

            def k_hi(b, q, i):
                act.wait_ge(fullB, pos_b(b, q, 1 + i) + 1)
                act.activation(kh[:, :], psB[:, :], ACT.Copy).then_inc(s_khi, 1)

            def values(b, q):
                for kt in range(TT):
                    ps, full, free, n = ((psC, fullC, freeC, pos_c(b, q, kt // 2)) if kt % 2 == 0 else
                                         (psD, fullD, freeD, pos_d(b, q, kt // 2)))
                    act.wait_ge(full, n + 1)
                    act.activation(V[0][:, kt, :], ps[:, :], ACT.Copy).then_inc(s_vhi, 1)

            def k_rope_hi(b):
                act.wait_ge(s_rope, b * NR + 5)
                act.activation(krh[:, :], rr[:, 0, :], ACT.Copy).then_inc(s_rhi, 1)

            def rope_hi(b, q, prev):
                act.wait_ge(s_rope, rope_base(b, q) + 4)
                if prev:
                    for i in range(HQ):
                        act.wait_ge(s_stack[i], 64 * (b * NQ + q))
                act.activation(rh[:, :, :], rr[:, :, :], ACT.Copy).then_inc(s_rhi, 1)

            def expo(b, q, i, qt):
                act.wait_ge(s_sm, tile_no(b, q, i, qt) + 1)
                act.activation(E[:, qt % 2, :], E[:, qt % 2, :], ACT.Exp, scale=-1.0,
                               bias=mx[:, i % 2, qt:qt + 1],
                               accum_out=rs[:, i % 2, qt:qt + 1]).then_inc(s_exp, 1)

            def probs_turned(b, q, i, qt):
                for part in range(2):
                    act.wait_ge(fullT, pos_t(b, q, i, qt) + part + 1)
                    act.activation(PT[part][:, :, qt * P:(qt + 1) * P],
                                   psT[part][:, :].rearrange("p (c n) -> p c n", c=TT), ACT.Copy)\
                       .then_inc(freeT, 1)

            def attended(b, q, i):
                act.wait_ge(fullD, pos_av(b, q, i) + 1)
                act.activation(attn[0][:, i % 2, :], psD[:, :], ACT.Copy).then_inc(s_ahi, 1)

            def wo_hi(b, q, pair, j, very_first):
                n = (b * NQ + q) * 2 + pair
                act.wait_ge(s_wo[j], 16 * (n + 1))
                if not very_first:
                    act.wait_ge(fullC, pos_oc(b, q, 0, 8) if pair else pos_oc(b, q - 1, 1, 8))
                    act.wait_ge(fullD, pos_od(b, q, 0, 8) if pair else pos_od(b, q - 1, 1, 8))
                act.activation(WO[0][:, j, :], xs[:, j, :], ACT.Copy).then_inc(s_wohi, 1)

            def sign(b, t):
                act.wait_ge(s_f, (b * TT + t) * NF + 11)
                act.activation(fs, fx, ACT.Sign).then_inc(s_sign, 1)

            def prologue(b, first):
                for j in range(TT):
                    stage_turned(b, j, False)
                down(psA, fullA, freeA, b * AN, qc[:, 0, :])
                down(psB, fullB, freeB, b * BN, qc[:, 1, :])
                down(psA, fullA, freeA, b * AN + 1, qc[:, 2, :])
                stage_turned(b, 0, True)
                stage_turned(b, 1, True)
                stage_turned(b, 2, True)
                stage_turned(b, 3, True)
                rope_hi(b, 0, not first)
                down(psB, fullB, freeB, b * BN + 2, kvc[:, 0, :])
                down(psA, fullA, freeA, b * AN + 3, kvc[:, 1, :])
                k_rope_hi(b)
                q_hi(b, 0, 0)
                k_hi(b, 0, 0)

            prologue(0, True)

            def body(b, first, last):
                def head(q, i, q0, nxt=None):
                    if nxt is not None:
                        rope_hi(b, nxt, True)
                    expo(b, q, i, 0)
                    expo(b, q, i, 1)
                    if i > 0:
                        attended(b, q, i - 1)
                    elif not q0:
                        attended(b, q - 1, HQ - 1)
                    probs_turned(b, q, i, 0)
                    if i % 2 == 1:
                        wo_hi(b, q, i // 2, 0, first and q0 and i == 1)
                    expo(b, q, i, 2)
                    probs_turned(b, q, i, 1)
                    expo(b, q, i, 3)
                    if nxt is not None:
                        q_hi(b, nxt, 0)
                    elif i < HQ - 1:
                        q_hi(b, q, i + 1)
                    probs_turned(b, q, i, 2)
                    if nxt is not None:
                        k_hi(b, nxt, 0)
                    elif i < HQ - 1:
                        k_hi(b, q, i + 1)
                    probs_turned(b, q, i, 3)
                    if i % 2 == 1:
                        wo_hi(b, q, i // 2, 1, first and q0 and i == 1)
                    if i == 0 and not q0:
                        values(b, q)
                    if i == 0 and not first:
                        sign(b - 1, q)

                values(b, 0)
                for i in range(HQ - 1):
                    head(0, i, True)
                with act.Fori(1, NQ) as q:
                    head(q - 1, HQ - 1, False, q)
                    for i in range(HQ - 1):
                        head(q, i, False)
                head(NQ - 1, HQ - 1, False)
                attended(b, NQ - 1, HQ - 1)
                if not last:
                    prologue(b + 1, False)

            batches(act, body)
            for t in range(TT):
                sign(B - 1, t)
            act.wait_ge(s_z, 16 * NTOK)
            for g in range(NTOK // 4):
                act.wait_ge(s_g, 2 + g + 1)
                act.activation(ohT[:, g * 512:(g + 1) * 512], psTb[g % 2][0:NT, 0:512], ACT.Copy)\
                   .then_inc(s_ge, 1)

        @block.vector
        def _(dve):
            dve.wait_ge(s_sl, 16)
            dve.tensor_reduce(ssum[0:NT, :], sl[0:NT, :].rearrange("p (j g) -> p j g", g=GRID), AX.X, ALU.add)\
               .then_inc(s_setv, 1)
            dve.wait_ge(s_wkr, 16)
            for c in range(2):
                dve.tensor_copy(wkra[:, :, c, :], wkr).then_inc(s_setv, 1)
                dve.tensor_scalar(wkrb[:, :, c, 0:HR], wkr[:, :, HR:R], -1.0, None, ALU.mult).then_inc(s_setv, 1)
                dve.tensor_copy(wkrb[:, :, c, HR:R], wkr[:, :, 0:HR]).then_inc(s_setv, 1)

            def norm_x(b, t):
                xt = xs[:, t % 2, :]
                dve.wait_ge(s_xs[t % 2], 16 * (b * TT + t // 2 + 1))
                c = Chain(dve, s_ln, (b * TT + t) * NL)
                for h in range(2):
                    c.do(dve.bn_stats(st[:, h, :], xt[:, h * HALF:(h + 1) * HALF]), wait=h == 1)
                c.do(dve.bn_aggr(mv[:, 0:2], st[:, :, :].rearrange("p a s -> p (a s)")))
                c.do(dve.tensor_scalar(mv[:, 2:3], mv[:, 1:2], LN_EPS, None, ALU.add), wait=False)
                dve.wait_ge(s_rstd, b * TT + t + 1)
                c.do(dve.tensor_scalar(xt, xt, mv[:, 0:1], mv[:, 3:4], ALU.subtract, ALU.mult))
                assert c.n == NL

            def rope_k(b):
                dve.wait_ge(s_rope, b * NR + 4)
                dve.wait_ge(s_rhi, b * (NQ + 1) + 1)
                dve.wait_ge(s_rlo, b * (NQ + 1) + 1)
                dve.wait_ge(fullA, b * AN + 5)
                dve.tensor_tensor(rt[:, 0, :], psA[:, :], cosT[:, :], ALU.mult).then_inc(freeA, 1)
                dve.wait_ge(fullB, b * BN + 4)
                dve.tensor_tensor(rt[:, 1, :], psB[:, :], sinT[:, :], ALU.mult).then_inc(freeB, 1)
                dve.wait_ge(freeA, b * AN + 5)
                dve.wait_ge(freeB, b * BN + 4)
                dve.tensor_tensor(rr[:, 0, :], rt[:, 0, :], rt[:, 1, :], ALU.add).then_inc(s_rope, 1)

            def rope_q(b, q):
                n = rope_no(b, q)
                c = Chain(dve, s_rope, rope_base(b, q))
                if not (isinstance(n, int) and n == 0):
                    dve.wait_ge(s_rope, rope_base(b, q))
                dve.wait_ge(fullA, pos_a(b, q, 0) + 1)
                c.do(dve.tensor_tensor(rt[:, 0, :], psA[:, :], cosT[:, :], ALU.mult), wait=False)
                dve.wait_ge(fullB, pos_b(b, q, 0) + 1)
                c.do(dve.tensor_tensor(rt[:, 1, :], psB[:, :], sinT[:, :], ALU.mult))
                if not (isinstance(n, int) and n == 0):
                    dve.wait_ge(s_rhi, n)
                    dve.wait_ge(s_rlo, n)
                c.do(dve.tensor_tensor(rr[:, 0, :], rt[:, 0, :], rt[:, 1, :], ALU.subtract))
                dve.tensor_tensor(rt[:, 0, :], psA[:, :], sinT[:, :], ALU.mult).then_inc(freeA, 1)
                dve.tensor_tensor(rt[:, 1, :], psB[:, :], cosT[:, :], ALU.mult).then_inc(freeB, 1)
                dve.wait_ge(freeA, pos_a(b, q, 0) + 1)
                dve.wait_ge(freeB, pos_b(b, q, 0) + 1)
                c.do(dve.tensor_tensor(rr[:, 1, :], rt[:, 0, :], rt[:, 1, :], ALU.add), wait=False)

            def q_lo(b, q, i):
                dve.wait_ge(s_qhi, b * H + q * HQ + i + 1)
                dve.tensor_tensor(ql[:, :], psA[:, :], qh[:, :].bitcast(F32), ALU.subtract)\
                   .then_inc(freeA, 1)

            def k_lo(b, q, i):
                dve.wait_ge(s_khi, b * H + q * HQ + i + 1)
                dve.tensor_tensor(kl[:, :], psB[:, :], kh[:, :].bitcast(F32), ALU.subtract)\
                   .then_inc(freeB, 1)

            def values_lo(b, q):
                for kt in range(TT):
                    ps, free = (psC, freeC) if kt % 2 == 0 else (psD, freeD)
                    dve.wait_ge(s_vhi, (b * NQ + q) * TT + kt + 1)
                    dve.tensor_tensor(V[1][:, kt, :], ps[:, :], V[0][:, kt, :].bitcast(F32), ALU.subtract)\
                       .then_inc(free, 1)

            def mask_scores(b, q, i, qt, head0):
                n = tile_no(b, q, i, qt)
                if head0 and qt == 0:
                    dve.wait_ge(s_mask, (b + 1) * NM)
                wait_apart(dve, s_S, n + 1)
                dve.tensor_tensor_reduce(E[:, qt % 2, :], psS[qt % 2][:, :], mask[:, qt, :], -SCALE, BIG,
                                         ALU.add, ALU.min, mx[:, i % 2, qt:qt + 1]).then_inc(s_sm, 1)

            def divide(b, q, i, qt, very_first):
                n = tile_no(b, q, i, qt)
                e, r = E[:, qt % 2, :], ri[:, i % 2, qt:qt + 1]
                dve.wait_ge(s_exp, n + 1)
                dve.reciprocal(r, rs[:, i % 2, qt:qt + 1]).then_inc(s_rinv, 1)
                if not very_first:
                    if qt < 2 and isinstance(q, int) and q == 0 and i == 0:
                        dve.wait_ge(fullT, b * TN - 4 + 2 * qt + 2)
                    else:
                        dve.wait_ge(fullT, pos_t(b, q, i, qt) - 2)
                dve.wait_ge(s_rinv, n + 1)
                dve.tensor_scalar(Ph[0][:, qt % 2, :], e, r, None, ALU.mult).then_inc(s_prob, 1)
                dve.wait_ge(s_prob, n + 1)
                dve.scalar_tensor_tensor(out=Ph[1][:, qt % 2, :], in0=e, scalar=r,
                                         in1=Ph[0][:, qt % 2, :].bitcast(F32), op0=ALU.mult, op1=ALU.subtract)\
                   .then_inc(s_plo, 1)

            def attended_lo(b, q, i):
                dve.wait_ge(s_ahi, b * H + q * HQ + i + 1)
                dve.tensor_tensor(attn[1][:, i % 2, :], psD[:, :], attn[0][:, i % 2, :].bitcast(F32), ALU.subtract)\
                   .then_inc(freeD, 1)

            def add_out(b, q, pair, w, first_add=False):
                half, t = w // TT, w % TT
                if w % 2 == 0:
                    ps, full, free, n = psC, fullC, freeC, pos_oc(b, q, pair, w)
                else:
                    ps, full, free, n = psD, fullD, freeD, pos_od(b, q, pair, w)
                if first_add:
                    dve.wait_ge(s_acc, 16 * TT * (b + 1))
                dve.wait_ge(full, n + 1)
                a = acc[:, t, half * HALF:(half + 1) * HALF]
                dve.tensor_tensor(a, a, ps[:, :], ALU.add).then_inc(free, 1)

            def ffn_chunks(b, t, x1, tail):
                k = b * TT + t
                c = Chain(dve, s_f, k * NF)

                def stats_x():
                    if not tail:
                        wait_apart(dve, s_x1in, 16 * (k + 1))
                    elif t == 0:
                        dve.wait_ge(freeC, (b + 1) * CN)
                        dve.wait_ge(freeD, (b + 1) * DN)
                    for h in range(2):
                        c.do(dve.bn_stats(st2[:, h, :], x1[:, h * HALF:(h + 1) * HALF]), wait=h == 1)

                def aggregate_x():
                    c.do(dve.bn_aggr(mv2[:, 0:2], st2[:, :, :].rearrange("p a s -> p (a s)")))
                    c.do(dve.tensor_scalar(mv2[:, 2:3], mv2[:, 1:2], LN_EPS, None, ALU.add), wait=False)

                def norm():
                    dve.wait_ge(s_rstd2, 2 * k + 1)
                    if not (isinstance(k, int) and k == 0):
                        dve.wait_ge(s_z, z_before(k))
                    c.do(dve.tensor_scalar(fy, x1, mv2[:, 0:1], mv2[:, 3:4], ALU.subtract, ALU.mult))

                def stats_norm():
                    for h in range(2):
                        c.do(dve.bn_stats(st2[:, h, :], fy[:, h * HALF:(h + 1) * HALF]), wait=h == 1)

                def aggregate_norm():
                    c.do(dve.bn_aggr(mv2[:, 4:6], st2[:, :, :].rearrange("p a s -> p (a s)")))
                    c.do(dve.tensor_scalar(mv2[:, 6:7], mv2[:, 5:6], LN_EPS, None, ALU.add), wait=False)

                def scale_in():
                    c.do(dve.scalar_tensor_tensor(out=fx, in0=fy, scalar=mv2[:, 4:5], in1=gb[:, :],
                                                  op0=ALU.subtract, op1=ALU.mult))

                def shift_in():
                    dve.wait_ge(s_rstd2, 2 * k + 2)
                    c.do(dve.scalar_tensor_tensor(out=fx, in0=fx, scalar=mv2[:, 7:8], in1=bb[:, :],
                                                  op0=ALU.mult, op1=ALU.add), wait=False)
                    assert c.n == 11

                def score_tiles():
                    dve.wait_ge(s_fpool, k * 3 + 2)
                    c.do(dve.tensor_reduce(ts[:, :], fs.rearrange("p (t j) -> p t j", j=SLICE), AX.X, ALU.add))

                def choose():
                    by_cluster = {"c": CLUSTERS}
                    c.do(dve.tensor_reduce(cs[:, :], ts[:, :].rearrange("p (c t) -> p c t", **by_cluster),
                                           AX.X, ALU.add))
                    wide = cs[:, :].rearrange("p (c a) -> p c a", a=1).broadcast_to([P, CLUSTERS, NT // CLUSTERS])
                    c.do(dve.scalar_tensor_tensor(out=key[:, :].rearrange("p (c t) -> p c t", **by_cluster),
                                                  in0=wide, scalar=4096.0,
                                                  in1=tie[:, :].rearrange("p (c t) -> p c t", **by_cluster),
                                                  op0=ALU.mult, op1=ALU.add))
                    c.do(dve.scalar_tensor_tensor(out=key[:, :], in0=ts[:, :], scalar=float(NT // CLUSTERS),
                                                  in1=key[:, :], op0=ALU.mult, op1=ALU.add))
                    c.do(dve.tensor_reduce(kmax[:, :], key[:, :], AX.X, ALU.max))
                    if not (isinstance(k, int) and k == 0):
                        dve.wait_ge(s_oh, z_before(k))
                    c.do(dve.tensor_scalar(oh[:, :], key[:, :], kmax[:, 0:1], None, ALU.is_equal), wait=False)
                    assert c.n == 17

                def take_slice():
                    xk = xsl[:, k, :]
                    wait_apart(dve, s_fpool, k * 3 + 3)
                    c.do(dve.tensor_reduce(xk, fsel.rearrange("p (t j) -> p j t", j=SLICE), AX.X, ALU.add))
                    c.do(dve.tensor_reduce(mm[:, 0:1], xk, AX.X, ALU.min), wait=False)
                    c.do(dve.tensor_reduce(mm[:, 1:2], xk, AX.X, ALU.max), wait=False)
                    c.do(dve.tensor_scalar(cand[:, 2, :], oh[:, :], 1.0, -BIG, ALU.subtract, ALU.mult))
                    c.do(dve.scalar_tensor_tensor(out=cand[:, 0, :], in0=oh[:, :], scalar=mm[:, 0:1],
                                                  in1=cand[:, 2, :], op0=ALU.mult, op1=ALU.add), wait=False)
                    c.do(dve.scalar_tensor_tensor(out=cand[:, 1, :], in0=oh[:, :], scalar=mm[:, 1:2],
                                                  in1=cand[:, 2, :], op0=ALU.mult, op1=ALU.subtract))
                    c.do(dve.tensor_tensor(run[:, 0, :], run[:, 0, :], cand[:, 0, :], ALU.min), wait=False)
                    c.do(dve.tensor_tensor(run[:, 1, :], run[:, 1, :], cand[:, 1, :], ALU.max))
                    assert c.n == NF

                return [[[stats_x, aggregate_x], [norm], [stats_norm, aggregate_norm], [scale_in], [shift_in]],
                        [[], [score_tiles], [choose], [], []],
                        [[], [take_slice], [], [], []]]

            def z_before(k):
                return 16 * k

            def prologue(b):
                rope_q(b, 0)
                rope_k(b)
                q_lo(b, 0, 0)
                k_lo(b, 0, 0)

            for t in range(TT):
                norm_x(0, t)
            dve.wait_ge(s_const, 64)
            dve.wait_ge(s_setup, 11)
            prologue(0)

            def body(b, first, last):
                def head(q, i, q0, nxt=None, ffn=None):
                    head0 = q0 and i == 0
                    vf = first and head0
                    adds = (q - 1, 1) if i == 0 and not q0 else (q, 0) if i == 2 else None

                    def piece(slot):
                        for part in (ffn[i][slot] if ffn else ()):
                            part()

                    def add(*ws):
                        for w in ws if adds else ():
                            add_out(b, adds[0], adds[1], w, q0 and w == 0)

                    if nxt is not None:
                        rope_q(b, nxt)
                    if i == HQ - 1:
                        add_out(b, q, 0, 6)
                    mask_scores(b, q, i, 0, head0)
                    if i == HQ - 1:
                        add_out(b, q, 0, 7)
                    mask_scores(b, q, i, 1, head0)
                    divide(b, q, i, 0, vf)
                    divide(b, q, i, 1, vf)
                    if i > 0:
                        attended_lo(b, q, i - 1)
                    elif not q0:
                        attended_lo(b, q - 1, HQ - 1)
                    piece(0)
                    mask_scores(b, q, i, 2, head0)
                    add(0, 1)
                    divide(b, q, i, 2, False)
                    mask_scores(b, q, i, 3, head0)
                    piece(1)
                    add(2, 3)
                    if nxt is not None:
                        q_lo(b, nxt, 0)
                    elif i < HQ - 1:
                        q_lo(b, q, i + 1)
                    divide(b, q, i, 3, False)
                    piece(2)
                    add(4, 5)
                    if nxt is not None:
                        k_lo(b, nxt, 0)
                    elif i < HQ - 1:
                        k_lo(b, q, i + 1)
                    piece(3)
                    if i == 0:
                        add(6)
                    piece(4)
                    if i == 0:
                        add(7)
                    if i == 0 and not q0:
                        values_lo(b, q)

                def steps(q):
                    return None if first else ffn_chunks(b - 1, q, fsel, False)

                values_lo(b, 0)
                ffn = steps(0)
                for i in range(HQ - 1):
                    head(0, i, True, None, ffn)
                with dve.Fori(1, NQ) as q:
                    head(q - 1, HQ - 1, False, q)
                    ffn = steps(q)
                    for i in range(HQ - 1):
                        head(q, i, False, None, ffn)
                head(NQ - 1, HQ - 1, False)
                if not last:
                    norm_x(b + 1, 0)
                attended_lo(b, NQ - 1, HQ - 1)
                if not last:
                    norm_x(b + 1, 1)
                for t in range(TT):
                    add_out(b, NQ - 1, 1, 2 * t)
                    add_out(b, NQ - 1, 1, 2 * t + 1)
                    if t < 2 and not last:
                        norm_x(b + 1, t + 2)
                if not last:
                    prologue(b + 1)

            batches(dve, body)
            for t in range(TT):
                for step in ffn_chunks(B - 1, t, acc[:, t, :], True):
                    for slot in step:
                        for part in slot:
                            part()

            dve.wait_ge(s_g, 2)
            dve.wait_ge(s_tab, 48)
            c = Chain(dve, s_gv, 0)
            c.do(dve.tensor_reduce(tab[:, 0:1], psA[0:NT, 0:P], AX.X, ALU.min), wait=False)
            c.do(dve.tensor_reduce(tab[:, 1:2], psB[0:NT, 0:P], AX.X, ALU.max), wait=False)
            dve.wait_ge(s_g, 3 + NTOK // 4)
            wide = [NTOK, SLICE]

            def per_tile(v):
                return v.rearrange("p (k a) -> p k a", a=1).broadcast_to([P, NTOK, SLICE])

            c.do(dve.tensor_copy(fin, psC[:, 0:NTOK * 4].rearrange("p (k c) -> p k c", c=4)))
            c.do(dve.tensor_tensor(dena, fin[:, :, 1], fin[:, :, 0], ALU.subtract))
            c.do(dve.tensor_scalar(dena, dena, 1e-8, None, ALU.add))
            c.do(dve.tensor_tensor(fu, xsl[:, :, :], per_tile(fin[:, :, 0]), ALU.subtract))
            c.do(dve.reciprocal(dena, dena))
            c.do(dve.tensor_tensor(fu, fu, per_tile(dena), ALU.mult))
            c.do(dve.tensor_scalar(fu, fu, 0.0, 1.0 - 1e-6, ALU.max, ALU.min))
            c.do(dve.tensor_scalar(fu, fu, float(GRID), None, ALU.mult))
            c.do(dve.tensor_scalar(fg, fu, ROUND, None, ALU.add))
            c.do(dve.tensor_scalar(fg, fg, ROUND, None, ALU.subtract))
            c.do(dve.tensor_tensor(fl, fg, fu, ALU.is_gt))
            c.do(dve.tensor_tensor(fg, fg, fl, ALU.subtract))
            c.do(dve.tensor_tensor(fl, fu, fg, ALU.subtract))
            dve.wait_ge(s_iota, 6)
            c.do(dve.tensor_tensor(idxf, fin[:, :, 3], tokb, ALU.add))
            c.do(dve.tensor_copy(idxi, idxf))
            n0 = c.n
            for g in range(2):
                eq = eqb.rearrange("p (k g) -> p k g", g=GRID)
                cells = fg[:, g * 16:(g + 1) * 16, :].rearrange("p k (j a) -> p (k j) a", a=1)
                ramp = gramp.rearrange("p (a g) -> p a g", a=1).broadcast_to([P, 16 * SLICE, GRID])
                c.do(dve.tensor_tensor(eq, cells.broadcast_to([P, 16 * SLICE, GRID]), ramp, ALU.is_equal))
                for kk in range(16):
                    k = g * 16 + kk
                    ps = [psA, psB, psD, psS[0]][k % 4]
                    dve.wait_ge(s_gb, k + 1)
                    e = eqb.rearrange("p (k j g) -> p k j g", j=SLICE, g=GRID)[:, kk, :, :]
                    pr = prod[:, k % 2, :].rearrange("p (a j g) -> p a j g", a=2, g=GRID)
                    for a in range(2):
                        ins = dve.tensor_tensor(pr[:, a], ps[:, a * 256:(a + 1) * 256]
                                                .rearrange("p (j g) -> p j g", g=GRID), e, ALU.mult)
                        if a == 0:
                            ins.then_inc(s_gv, 1)
                            c.n += 1
                        else:
                            ins.then_inc(s_gf, 1)
                    dve.wait_ge(s_gf, k + 1)
                    dve.wait_ge(s_gv, c.n)
                    c.do(dve.tensor_reduce(bsel[:, k // 8, (k % 8) * 32:(k % 8 + 1) * 32],
                                           prod[:, k % 2, :].rearrange("p (m g) -> p m g", g=GRID),
                                           AX.X, ALU.add), wait=False)
                dve.wait_ge(s_gv, c.n)
            bs = bsel.rearrange("p m (k a j) -> p m k a j", a=2, j=SLICE)
            fd4 = fd.rearrange("p (m k) j -> p m k j", m=4)
            fl4 = fl.rearrange("p (m k) j -> p m k j", m=4)
            c.do(dve.tensor_tensor(fd4, bs[:, :, :, 1, :], fl4, ALU.mult))
            c.do(dve.tensor_tensor(fd4, fd4, bs[:, :, :, 0, :], ALU.add))
            c.do(dve.tensor_tensor(fd, fd, per_tile(fin[:, :, 2]), ALU.mult), wait=False)
            assert c.n == NG, c.n

        @block.tensor
        def _(pe):
            def turn_stage(b, j, ctx_side):
                jj = j + (TT if ctx_side else 0)
                if ctx_side:
                    pe.wait_ge(s_xs[j % 2], 16 * (b * TT + 2 + j // 2 + 1))
                else:
                    pe.wait_ge(s_ln, (b * TT + j + 1) * NL)
                for half in range(2):
                    k = 2 * jj + half
                    if not (isinstance(b, int) and b == 0 and k < 2):
                        pe.wait_ge(freeT, b * TN + k - 1)
                    for c in range(4):
                        blk = 4 * half + c
                        mm_ = pe.transpose(psT[k % 2][:, c * P:(c + 1) * P],
                                           xs[:, j % 2, blk * P:(blk + 1) * P], ident)
                    mm_.then_inc(fullT, 1)

            def wait_free(free, n):
                if not (isinstance(n, int) and n == 0):
                    pe.wait_ge(free, n)

            def down(ps, full, free, n, col):
                wait_free(free, n)
                for c in range(DB):
                    mm_ = pe.matmul(ps[:, :], wD[:, c, col * P:(col + 1) * P], xT[:, c, :],
                                    start=c == 0, stop=c == DB - 1)
                mm_.then_inc(full, 1)

            def rope_keys(b):
                for ps, full, free, n, w in ((psA, fullA, freeA, b * AN + 4, wkra),
                                             (psB, fullB, freeB, b * BN + 3, wkrb)):
                    wait_free(free, n)
                    for c in range(CB):
                        mm_ = pe.matmul(ps[:, :], w[:, c].rearrange("p a r -> p (a r)"), kvc[:, c, :],
                                        start=c == 0, stop=c == CB - 1)
                    mm_.then_inc(full, 1)

            def rope_queries(b, q):
                pe.wait_ge(s_sorted, b * NQ + q + 1)
                for ps, full, free, n, j in ((psA, fullA, freeA, pos_a(b, q, 0), 0),
                                             (psB, fullB, freeB, pos_b(b, q, 0), 1)):
                    wait_free(free, n)
                    for c in range(QB):
                        mm_ = pe.matmul(ps[:, :], wqp[:, c, j, :], qc[:, c, :],
                                        start=c == 0, stop=c == QB - 1)
                    mm_.then_inc(full, 1)

            def queries(b, q, i):
                pe.wait_ge(s_wuq[i % 2], 16 * (b * (H // 2) + q * (HQ // 2) + i // 2 + 1))
                wait_free(freeA, pos_a(b, q, 1 + i))
                for c in range(QB):
                    mm_ = pe.matmul(psA[:, :], wuq[:, i % 2, c, :], qc[:, c, :], start=c == 0, stop=c == QB - 1)
                mm_.then_inc(fullA, 1)

            def keys(b, q, i):
                pe.wait_ge(s_wuk[i % 2], 16 * (b * (H // 2) + q * (HQ // 2) + i // 2 + 1))
                wait_free(freeB, pos_b(b, q, 1 + i))
                for c in range(CB):
                    mm_ = pe.matmul(psB[:, :], wuk[:, i % 2, c, :], kvc[:, c, :], start=c == 0, stop=c == CB - 1)
                mm_.then_inc(fullB, 1)

            def values(b, q):
                pe.wait_ge(s_wuv, 16 * (b * NQ + q + 1))
                for kt in range(TT):
                    ps, full, free, n = ((psC, fullC, freeC, pos_c(b, q, kt // 2)) if kt % 2 == 0 else
                                         (psD, fullD, freeD, pos_d(b, q, kt // 2)))
                    wait_free(free, n)
                    for c in range(CB):
                        mm_ = pe.matmul(ps[:, :], kvc[:, c, kt * P:(kt + 1) * P], wuv[:, c, :],
                                        start=c == 0, stop=c == CB - 1)
                    mm_.then_inc(full, 1)

            def scores(b, q, i, qt, very_first):
                n = tile_no(b, q, i, qt)
                if qt == 0:
                    pe.wait_ge(freeA, pos_a(b, q, 1 + i) + 1)
                    pe.wait_ge(s_khi, b * H + q * HQ + i + 1)
                    pe.wait_ge(s_stack[i], 64 * (b * NQ + q + 1))
                    if i == 0 and isinstance(q, int):
                        pe.wait_ge(s_rhi, b * (NQ + 1) + 2)
                        pe.wait_ge(s_rlo, b * (NQ + 1) + 2)
                if not (very_first and qt < 2):
                    pe.wait_ge(s_sm, n - 1)
                cols = slice(qt * P, (qt + 1) * P)
                ps = psS[qt % 2][:, :]
                pe.matmul(ps, qh[:, cols], kh[:, :], start=True, stop=False)
                pe.matmul(ps, ql[:, cols], kh[:, :], start=False, stop=False)
                pe.matmul(ps, stack[:, i, cols], krh[:, :], start=False, stop=False)
                pe.matmul(ps, stack[0:R, i, cols], krl[:, :], start=False, stop=False)
                if qt == 0:
                    pe.wait_ge(freeB, pos_b(b, q, 1 + i) + 1)
                pe.matmul(ps, qh[:, cols], kl[:, :], start=False, stop=True).then_inc(s_S, 1)

            def turn_probs(b, q, i, qt, part):
                pe.wait_ge(s_plo if part else s_prob, tile_no(b, q, i, qt) + 1)
                pe.wait_ge(freeT, pos_t(b, q, i, qt) + part - 1)
                for c in range(TT):
                    mm_ = pe.transpose(psT[part][:, c * P:(c + 1) * P].bitcast(F32R),
                                       Ph[part][:, qt % 2, c * P:(c + 1) * P], identr[:, :])
                mm_.then_inc(fullT, 1)

            def attend(b, q, i):
                pe.wait_ge(freeT, pos_t(b, q, i, TT - 1) + 2)
                if i == 0:
                    pe.wait_ge(freeC, pos_c(b, q, 2))
                pe.wait_ge(freeD, pos_av(b, q, i))
                for kt in range(TT):
                    for v, p in ((0, 0), (0, 1), (1, 0)):
                        mm_ = pe.matmul(psD[:, :], V[v][:, kt, i * P:(i + 1) * P], PT[p][:, kt, :],
                                        start=kt == 0 and v + p == 0, stop=kt == TT - 1 and v == 1)
                mm_.then_inc(fullD, 1)

            def out_proj(b, q, pair, w):
                half, t = w // TT, w % TT
                if w % 2 == 0:
                    ps, full, free, n = psC, fullC, freeC, pos_oc(b, q, pair, w)
                else:
                    ps, full, free, n = psD, fullD, freeD, pos_od(b, q, pair, w)
                if w == 0:
                    pe.wait_ge(s_wolo, 2 * ((b * NQ + q) * 2 + pair + 1))
                    pe.wait_ge(freeD, pos_od(b, q, pair, 0))
                pe.wait_ge(free, n)
                for i in range(2):
                    for a, o in ((0, 0), (0, 1), (1, 0)):
                        mm_ = pe.matmul(ps[:, :], attn[a][:, i, t * P:(t + 1) * P],
                                        WO[o][:, i, half * HALF:(half + 1) * HALF],
                                        start=i + a + o == 0, stop=i + a == 2)
                mm_.then_inc(full, 1)

            def down_q(b):
                pe.wait_ge(s_wd, 32 * b + 16)
                pe.wait_ge(freeT, b * TN + 2 * TT)
                down(psA, fullA, freeA, b * AN, 0)
                down(psB, fullB, freeB, b * BN, 1)
                down(psA, fullA, freeA, b * AN + 1, 2)

            def down_kv(b):
                pe.wait_ge(s_wd, 32 * b + 32)
                pe.wait_ge(freeT, b * TN + 4 * TT)
                down(psB, fullB, freeB, b * BN + 2, 0)
                down(psA, fullA, freeA, b * AN + 3, 1)

            def into_heads(b):
                pe.wait_ge(freeA, b * AN + 4)
                pe.wait_ge(freeB, b * BN + 3)
                rope_keys(b)
                queries(b, 0, 0)
                keys(b, 0, 0)

            pe.wait_ge(s_setup, 4)
            for j in range(TT):
                turn_stage(0, j, False)
            down_q(0)
            turn_stage(0, 0, True)
            turn_stage(0, 1, True)
            rope_queries(0, 0)
            turn_stage(0, 2, True)
            turn_stage(0, 3, True)
            down_kv(0)
            pe.wait_ge(s_setv, 7)
            into_heads(0)

            def body(b, first, last):
                def head(q, i, q0, nxt=None):
                    vf = first and q0 and i == 0
                    outs = (q - 1, 1) if i == 0 and not q0 else (q, 0) if i == 2 else None

                    def project(*ws):
                        for w in ws if outs else ():
                            out_proj(b, outs[0], outs[1], w)

                    if nxt is not None:
                        rope_queries(b, nxt)
                    if i == HQ - 1:
                        out_proj(b, q, 0, 6)
                        out_proj(b, q, 0, 7)
                    scores(b, q, i, 0, vf)
                    scores(b, q, i, 1, vf)
                    if i > 0:
                        attend(b, q, i - 1)
                    elif not q0:
                        attend(b, q - 1, HQ - 1)
                    turn_probs(b, q, i, 0, 0)
                    scores(b, q, i, 2, vf)
                    turn_probs(b, q, i, 0, 1)
                    project(0, 1)
                    turn_probs(b, q, i, 1, 0)
                    scores(b, q, i, 3, vf)
                    turn_probs(b, q, i, 1, 1)
                    project(2, 3)
                    if nxt is not None:
                        queries(b, nxt, 0)
                    elif i < HQ - 1:
                        queries(b, q, i + 1)
                    turn_probs(b, q, i, 2, 0)
                    project(4)
                    turn_probs(b, q, i, 2, 1)
                    project(5)
                    if nxt is not None:
                        keys(b, nxt, 0)
                    elif i < HQ - 1:
                        keys(b, q, i + 1)
                    turn_probs(b, q, i, 3, 0)
                    if i == 0:
                        project(6)
                    turn_probs(b, q, i, 3, 1)
                    if i == 0:
                        project(7)
                    if i == 0 and not q0:
                        values(b, q)

                values(b, 0)
                for i in range(HQ - 1):
                    head(0, i, True)
                with pe.Fori(1, NQ) as q:
                    head(q - 1, HQ - 1, False, q)
                    for i in range(HQ - 1):
                        head(q, i, False)
                head(NQ - 1, HQ - 1, False)
                attend(b, NQ - 1, HQ - 1)
                for t in range(TT):
                    if not last:
                        turn_stage(b + 1, t, False)
                    if t < TT - 1:
                        out_proj(b, NQ - 1, 1, 2 * t)
                        out_proj(b, NQ - 1, 1, 2 * t + 1)
                if not last:
                    down_q(b + 1)
                    turn_stage(b + 1, 0, True)
                    turn_stage(b + 1, 1, True)
                out_proj(b, NQ - 1, 1, 2 * TT - 2)
                out_proj(b, NQ - 1, 1, 2 * TT - 1)
                if not last:
                    rope_queries(b + 1, 0)
                    turn_stage(b + 1, 2, True)
                    turn_stage(b + 1, 3, True)
                    down_kv(b + 1)
                    into_heads(b + 1)

            batches(pe, body)

            pe.wait_ge(s_f, NTOK * NF)
            pe.wait_ge(freeA, B * AN)
            pe.wait_ge(freeB, B * BN)
            pe.transpose(psA[0:NT, 0:P], run[:, 0, :], ident).then_inc(s_g, 1)
            pe.transpose(psB[0:NT, 0:P], run[:, 1, :], ident).then_inc(s_g, 1)
            pe.wait_ge(s_ohin, 16)
            for g in range(NTOK // 4):
                if g >= 2:
                    pe.wait_ge(s_ge, g - 1)
                for k in range(4):
                    mm_ = pe.transpose(psTb[g % 2][0:NT, k * P:(k + 1) * P], ohall[:, 4 * g + k, :], identb[:, :])
                mm_.then_inc(s_g, 1)
            pe.wait_ge(s_gv, 2)
            pe.wait_ge(s_iota, 6)
            pe.wait_ge(s_tab, 48)
            pe.wait_ge(s_ge, NTOK // 4)
            pe.wait_ge(freeC, B * CN)
            for k in range(NTOK):
                mm_ = pe.matmul(psC[:, k * 4:k * 4 + 4], ohT[:, k * P:(k + 1) * P], tab[:, :], start=True, stop=True)
            mm_.then_inc(s_g, 1)
            pe.wait_ge(freeD, B * DN)
            for k in range(NTOK):
                ps = [psA, psB, psD, psS[0]][k % 4]
                if k >= 4:
                    pe.wait_ge(s_gf, k - 3)
                pe.matmul(ps[:, :], ohT[:, k * P:(k + 1) * P], spl[:, 0, :],
                          start=True, stop=True).then_inc(s_gb, 1)


NM = 2 + 4 * 4
NR = 1 + 4 * 4
NG = 2 + 15 + 2 + 32 * 2 + 3


def wait_apart(eng, sem, n):
    eng.wait_ge(sem, n)
    if not isinstance(n, int):
        eng.sem_inc(AFTER[0], 1)


AFTER = []


class Chain:

    def __init__(self, eng, sem, base):
        self.eng, self.sem, self.base, self.n = eng, sem, base, 0

    def do(self, ins, wait=True):
        self.n += 1
        ins.then_inc(self.sem, 1)
        if wait:
            wait_apart(self.eng, self.sem, self.base + self.n)


_INS = ['x', 'ctx_2048', 'itok_BxS_0_1023', 'L0_xattn_W_kvc', 'L0_xattn_W_dq', 'L0_xattn_W_uq', 'L0_xattn_W_qr',
        'L0_xattn_W_uk', 'L0_xattn_W_kr', 'L0_xattn_W_uv', 'L0_xattn_W_o', 'L0_ffn_ln_gamma', 'L0_ffn_ln_beta',
        'L0_ffn_spline_bases', 'L0_ffn_spline_slopes', 'L0_ffn_output_scale']
_OUTS = [((8, 512, 1024), 'float32')]


def _rotary_tables(length, half):
    import numpy as _np
    steps = _np.arange(half, dtype=_np.float32) / _np.float32(half)
    inv = (_np.float32(1.0) / _np.power(_np.float32(10000.0), steps)).astype(_np.float32)
    ang = (_np.arange(length, dtype=_np.float32)[:, None] * inv).astype(_np.float64)
    reps = 128 // half
    return [_np.ascontiguousarray(_np.tile(f(ang).astype(_np.float32).T, (reps, 1))) for f in (_np.cos, _np.sin)]


def kernel(**inputs):
    import numpy as _np
    import concourse.bacc as _bacc
    from concourse import mybir as _mybir
    from concourse.bass_utils import run_bass_kernel_spmd as _run

    nc = _bacc.Bacc("TRN2", target_bir_lowering=False, num_devices=1)
    arrays, args = {}, []
    cos_t, sin_t = _rotary_tables(512, 32)
    data = [(name, _np.ascontiguousarray(inputs[name])) for name in _INS] + [('cos_t', cos_t), ('sin_t', sin_t)]
    for name, a in data:
        arrays[f"in_{name}_dram"] = a
        args.append(nc.dram_tensor(f"in_{name}_dram", a.shape, _mybir.dt.from_np(a.dtype), kind="ExternalInput").ap())
    for i, (shape, dtype) in enumerate(_OUTS):
        dt = _mybir.dt.from_np(_np.dtype(dtype))
        args.append(nc.dram_tensor(f"out_{i}_dram", shape, dt, kind="ExternalOutput").ap())
    xattn_ffn_kernel(nc, *args)
    r = _run(nc, [arrays], core_ids=[0])
    got = tuple(r.results[0][f"out_{i}_dram"] for i in range(len(_OUTS)))
    return got[0]
```
